# Optimizing a Trainium2 kernel written in Bass

```python
import numpy as np
import jax
import jax.numpy as jnp

def _softmax(x, axis=-1):
    return jax.nn.softmax(x, axis=axis)

def _gelu(x):
    return jax.nn.gelu(x, approximate=True)

def _silu(x):
    return jax.nn.silu(x)

def _sigmoid(x):
    return jax.nn.sigmoid(x)

def _layernorm(x, axis=-1, eps=1e-05):
    m = jnp.mean(x, axis=axis, keepdims=True)
    v = jnp.var(x, axis=axis, keepdims=True)
    return (x - m) / jnp.sqrt(v + eps)

def _scatter_add(tgt, idx, src, axis=0):
    return tgt.at[idx].add(src)

def _segment_sum(src, seg, n):
    return jax.ops.segment_sum(src, seg, n)
kernel_name = 'mk_hybrid_d2_jaxref_r8_ca6d5e'

def setup_inputs(seed: int=0):
    np.random.seed(seed)
    _w = jnp.asarray

    def _L0_attn_a_setup():
        import jax, jax.numpy as jnp
        import numpy as np
        B, N, D, H = (2, 256, 128, 8)
        DH = D // H
        LAMBDA_INIT = 0.8
        EPS = 1e-05
        key = jax.random.key(seed)
        ks = jax.random.split(key, 10)
        s = 1.0 / np.sqrt(D)
        return {'X': jax.random.normal(ks[0], (B, N, D), jnp.float32), 'W_q': jax.random.normal(ks[1], (D, 2 * D), jnp.float32) * s, 'W_k': jax.random.normal(ks[2], (D, 2 * D), jnp.float32) * s, 'W_v': jax.random.normal(ks[3], (D, 2 * D), jnp.float32) * s, 'W_o': jax.random.normal(ks[4], (2 * D, D), jnp.float32) * s, 'lambda_q1': jax.random.normal(ks[5], (H, DH), jnp.float32) * 0.1, 'lambda_k1': jax.random.normal(ks[6], (H, DH), jnp.float32) * 0.1, 'lambda_q2': jax.random.normal(ks[7], (H, DH), jnp.float32) * 0.1, 'lambda_k2': jax.random.normal(ks[8], (H, DH), jnp.float32) * 0.1, 'rms_scale': jnp.ones((2 * DH,), jnp.float32)}
    _L0_attn_a_in = _L0_attn_a_setup()

    def _L0_attn_b_setup():
        import math
        import jax, jax.numpy as jnp
        import numpy as np
        N_HEADS = 16
        CHUNK = 64

        def _chunked_causal_attention(q, k, v, chunk=CHUNK):
            B, H, S, D = q.shape
            scale = 1.0 / math.sqrt(D)
            nc = S // chunk
            qc = jnp.moveaxis(q.reshape(B, H, nc, chunk, D), 2, 0)
            kpos = jnp.arange(S)

            def body(_, inp):
                qi, ci = inp
                scores = jnp.einsum('bhcd,bhsd->bhcs', qi, k) * scale
                qpos = ci * chunk + jnp.arange(chunk)
                mask = kpos[None, :] <= qpos[:, None]
                scores = jnp.where(mask, scores, jnp.finfo(scores.dtype).min)
                p = jax.nn.softmax(scores, axis=-1)
                return (None, jnp.einsum('bhcs,bhsd->bhcd', p, v))
            _, outs = jax.lax.scan(body, None, (qc, jnp.arange(nc)))
            return jnp.moveaxis(outs, 0, 2).reshape(B, H, S, D)
        key = jax.random.key(seed)
        kx, kq, kk, kv, ko = jax.random.split(key, 5)
        d = 128
        x = jax.random.normal(kx, (1, 512, d), dtype=jnp.float32)
        Wq = jax.random.normal(kq, (d, d), dtype=jnp.float32) * 0.02
        Wk = jax.random.normal(kk, (d, d), dtype=jnp.float32) * 0.02
        Wv = jax.random.normal(kv, (d, d), dtype=jnp.float32) * 0.02
        Wo = jax.random.normal(ko, (d, d), dtype=jnp.float32) * 0.02
        return {'x': x, 'Wq': Wq, 'Wk': Wk, 'Wv': Wv, 'Wo': Wo}
    _L0_attn_b_in = _L0_attn_b_setup()

    def _L0_ffn_setup():
        import jax, jax.numpy as jnp
        import numpy as np
        TOP_K = 2

        def _mlp(x, w1, b1, w2, b2):
            h = jax.nn.gelu(jnp.einsum('bsd,di->bsi', x, w1) + b1)
            return jnp.einsum('bsi,id->bsd', h, w2) + b2
        key = jax.random.key(seed)
        ks = jax.random.split(key, 8)
        B, S, D, I, E = (2, 256, 128, 512, 8)
        s_in = 1.0 / np.sqrt(D)
        s_mid = 1.0 / np.sqrt(I)
        return {'x': jax.random.normal(ks[0], (B, S, D), jnp.float32), 'gate_w': jax.random.normal(ks[1], (D, E), jnp.float32) * s_in, 'gate_b': jnp.zeros((E,), jnp.float32), 'sh_w1': jax.random.normal(ks[2], (D, I), jnp.float32) * s_in, 'sh_b1': jnp.zeros((I,), jnp.float32), 'sh_w2': jax.random.normal(ks[3], (I, D), jnp.float32) * s_mid, 'sh_b2': jnp.zeros((D,), jnp.float32), 'ew1': jax.random.normal(ks[4], (E, D, I), jnp.float32) * s_in, 'eb1': jnp.zeros((E, I), jnp.float32), 'ew2': jax.random.normal(ks[5], (E, I, D), jnp.float32) * s_mid, 'eb2': jnp.zeros((E, D), jnp.float32)}
    _L0_ffn_in = _L0_ffn_setup()

    def _L1_attn_a_setup():
        import jax, jax.numpy as jnp
        import numpy as np
        import math
        DIM_EMB = 128
        KSQRT = math.sqrt(DIM_EMB)
        key = jax.random.key(seed)
        ks = jax.random.split(key, 7)
        b, t, e, d = (4, 512, DIM_EMB, 128)
        s = 1.0 / math.sqrt(e)
        return {'x': jax.random.normal(ks[0], (b, t, e), dtype=jnp.float32), 'Wq': jax.random.normal(ks[1], (d, e), dtype=jnp.float32) * s, 'bq': jax.random.normal(ks[2], (d,), dtype=jnp.float32) * s, 'Wk': jax.random.normal(ks[3], (d, e), dtype=jnp.float32) * s, 'bk': jax.random.normal(ks[4], (d,), dtype=jnp.float32) * s, 'Wv': jax.random.normal(ks[5], (d, e), dtype=jnp.float32) * s, 'bv': jax.random.normal(ks[6], (d,), dtype=jnp.float32) * s}
    _L1_attn_a_in = _L1_attn_a_setup()

    def _L1_attn_b_setup():
        import jax, jax.numpy as jnp
        import numpy as np
        DIM = 128
        HID = int(DIM * 1.5)
        GHID = int(DIM * 2)
        K = 4
        ALPHA_LOG_SCALE = -8.0

        def _rmsnorm(x, gamma):
            n = jnp.linalg.norm(x, axis=-1, keepdims=True)
            return gamma * jnp.sqrt(jnp.asarray(x.shape[-1], x.dtype)) * (x / n)

        def _causal_depthwise_conv(x, w, b):
            xc = jnp.transpose(x, (0, 2, 1))
            xc = jnp.pad(xc, ((0, 0), (0, 0), (K - 1, 0)))
            y = jax.lax.conv_general_dilated(xc, w, window_strides=(1,), padding='VALID', dimension_numbers=('NCH', 'OIH', 'NCH'), feature_group_count=w.shape[0])
            y = y + b[None, :, None]
            return jnp.transpose(y, (0, 2, 1))

        def _linear_scan(alpha, x):

            def combine(c1, c2):
                a1, b1 = c1
                a2, b2 = c2
                return (a1 * a2, a2 * b1 + b2)
            _, h = jax.lax.associative_scan(combine, (alpha, x), axis=1)
            return h
        key = jax.random.key(seed)
        ks = jax.random.split(key, 8)
        N, T = (4, 256)
        x = jax.random.normal(ks[0], (N, T, DIM), jnp.float32)
        W_in = jax.random.normal(ks[1], (2 * HID, DIM), jnp.float32) * DIM ** (-0.5)
        conv_w = jax.random.normal(ks[2], (HID, 1, K), jnp.float32) * 0.25
        conv_b = jnp.zeros((HID,), jnp.float32)
        W_gates = jax.random.normal(ks[3], (2 * HID, HID), jnp.float32) * HID ** (-0.5)
        b_gates = jnp.zeros((2 * HID,), jnp.float32)
        forget_base = jnp.linspace(-4.323, -9.0, HID, dtype=jnp.float32)
        W_out = jax.random.normal(ks[4], (DIM, HID), jnp.float32) * HID ** (-0.5)
        W_grow = jax.random.normal(ks[5], (2 * GHID, DIM), jnp.float32) * DIM ** (-0.5)
        W_shrink = jax.random.normal(ks[6], (DIM, GHID), jnp.float32) * GHID ** (-0.5)
        gamma1 = jnp.ones((DIM,), jnp.float32)
        gamma2 = jnp.ones((DIM,), jnp.float32)
        return {'x': x, 'gamma1': gamma1, 'W_in': W_in, 'conv_w': conv_w, 'conv_b': conv_b, 'W_gates': W_gates, 'b_gates': b_gates, 'forget_base': forget_base, 'W_out': W_out, 'gamma2': gamma2, 'W_grow': W_grow, 'W_shrink': W_shrink}
    _L1_attn_b_in = _L1_attn_b_setup()

    def _L1_ffn_setup():
        import jax, jax.numpy as jnp
        import numpy as np
        D_MODEL = 128
        N_HEADS = 16
        D_HEAD = D_MODEL // N_HEADS
        N_EXPERTS = 8
        TOP_K = 2
        D_FF = 256
        EPS = 1e-06

        def rmsnorm(x, w):
            return x * jax.lax.rsqrt(jnp.mean(x * x, axis=-1, keepdims=True) + EPS) * w

        def swiglu(x, w_gate, w_up, w_down):
            return jax.nn.silu(x @ w_gate) * (x @ w_up) @ w_down
        key = jax.random.key(seed)
        ks = jax.random.split(key, 16)
        s = 0.02
        B, S = (2, 256)
        return {'X': jax.random.normal(ks[0], (B, S, D_MODEL), dtype=jnp.float32), 'norm1_w': jnp.ones((D_MODEL,), jnp.float32), 'norm2_w': jnp.ones((D_MODEL,), jnp.float32), 'wq': jax.random.normal(ks[1], (D_MODEL, D_MODEL), jnp.float32) * s, 'wk': jax.random.normal(ks[2], (D_MODEL, D_MODEL), jnp.float32) * s, 'wv': jax.random.normal(ks[3], (D_MODEL, D_MODEL), jnp.float32) * s, 'wo': jax.random.normal(ks[4], (D_MODEL, D_MODEL), jnp.float32) * s, 'router_w': jax.random.normal(ks[5], (D_MODEL, N_EXPERTS), jnp.float32) * s, 'sh_gate': jax.random.normal(ks[6], (D_MODEL, D_FF), jnp.float32) * s, 'sh_up': jax.random.normal(ks[7], (D_MODEL, D_FF), jnp.float32) * s, 'sh_down': jax.random.normal(ks[8], (D_FF, D_MODEL), jnp.float32) * s, 'e_gate': jax.random.normal(ks[9], (N_EXPERTS, D_MODEL, D_FF), jnp.float32) * s, 'e_up': jax.random.normal(ks[10], (N_EXPERTS, D_MODEL, D_FF), jnp.float32) * s, 'e_down': jax.random.normal(ks[11], (N_EXPERTS, D_FF, D_MODEL), jnp.float32) * s}
    _L1_ffn_in = _L1_ffn_setup()
    _d = {'L0_attn_a_X': _L0_attn_a_in['X'], 'L0_attn_a_W_q': _L0_attn_a_in['W_q'], 'L0_attn_a_W_k': _L0_attn_a_in['W_k'], 'L0_attn_a_W_v': _L0_attn_a_in['W_v'], 'L0_attn_a_W_o': _L0_attn_a_in['W_o'], 'L0_attn_a_lambda_q1': _L0_attn_a_in['lambda_q1'], 'L0_attn_a_lambda_k1': _L0_attn_a_in['lambda_k1'], 'L0_attn_a_lambda_q2': _L0_attn_a_in['lambda_q2'], 'L0_attn_a_lambda_k2': _L0_attn_a_in['lambda_k2'], 'L0_attn_a_rms_scale': _L0_attn_a_in['rms_scale'], 'L0_attn_b_Wq': _L0_attn_b_in['Wq'], 'L0_attn_b_Wk': _L0_attn_b_in['Wk'], 'L0_attn_b_Wv': _L0_attn_b_in['Wv'], 'L0_attn_b_Wo': _L0_attn_b_in['Wo'], 'L0_ffn_gate_w': _L0_ffn_in['gate_w'], 'L0_ffn_gate_b': _L0_ffn_in['gate_b'], 'L0_ffn_sh_w1': _L0_ffn_in['sh_w1'], 'L0_ffn_sh_b1': _L0_ffn_in['sh_b1'], 'L0_ffn_sh_w2': _L0_ffn_in['sh_w2'], 'L0_ffn_sh_b2': _L0_ffn_in['sh_b2'], 'L0_ffn_ew1': _L0_ffn_in['ew1'], 'L0_ffn_eb1': _L0_ffn_in['eb1'], 'L0_ffn_ew2': _L0_ffn_in['ew2'], 'L0_ffn_eb2': _L0_ffn_in['eb2'], 'L1_attn_a_Wq': _L1_attn_a_in['Wq'], 'L1_attn_a_bq': _L1_attn_a_in['bq'], 'L1_attn_a_Wk': _L1_attn_a_in['Wk'], 'L1_attn_a_bk': _L1_attn_a_in['bk'], 'L1_attn_a_Wv': _L1_attn_a_in['Wv'], 'L1_attn_a_bv': _L1_attn_a_in['bv'], 'L1_attn_b_gamma1': _L1_attn_b_in['gamma1'], 'L1_attn_b_W_in': _L1_attn_b_in['W_in'], 'L1_attn_b_conv_w': _L1_attn_b_in['conv_w'], 'L1_attn_b_conv_b': _L1_attn_b_in['conv_b'], 'L1_attn_b_W_gates': _L1_attn_b_in['W_gates'], 'L1_attn_b_b_gates': _L1_attn_b_in['b_gates'], 'L1_attn_b_forget_base': _L1_attn_b_in['forget_base'], 'L1_attn_b_W_out': _L1_attn_b_in['W_out'], 'L1_attn_b_gamma2': _L1_attn_b_in['gamma2'], 'L1_attn_b_W_grow': _L1_attn_b_in['W_grow'], 'L1_attn_b_W_shrink': _L1_attn_b_in['W_shrink'], 'L1_ffn_norm1_w': _L1_ffn_in['norm1_w'], 'L1_ffn_norm2_w': _L1_ffn_in['norm2_w'], 'L1_ffn_wq': _L1_ffn_in['wq'], 'L1_ffn_wk': _L1_ffn_in['wk'], 'L1_ffn_wv': _L1_ffn_in['wv'], 'L1_ffn_wo': _L1_ffn_in['wo'], 'L1_ffn_router_w': _L1_ffn_in['router_w'], 'L1_ffn_sh_gate': _L1_ffn_in['sh_gate'], 'L1_ffn_sh_up': _L1_ffn_in['sh_up'], 'L1_ffn_sh_down': _L1_ffn_in['sh_down'], 'L1_ffn_e_gate': _L1_ffn_in['e_gate'], 'L1_ffn_e_up': _L1_ffn_in['e_up'], 'L1_ffn_e_down': _L1_ffn_in['e_down']}
    _x0 = _d['L0_attn_a_X']
    _d['L0_attn_a_X'] = jax.random.normal(jax.random.fold_in(jax.random.key(seed), 1), (16, 256, 128), dtype=_x0.dtype)
    del _x0
    return _d

def reference(L0_attn_a_X, L0_attn_a_W_q, L0_attn_a_W_k, L0_attn_a_W_v, L0_attn_a_W_o, L0_attn_a_lambda_q1, L0_attn_a_lambda_k1, L0_attn_a_lambda_q2, L0_attn_a_lambda_k2, L0_attn_a_rms_scale, L0_attn_b_Wq, L0_attn_b_Wk, L0_attn_b_Wv, L0_attn_b_Wo, L0_ffn_gate_w, L0_ffn_gate_b, L0_ffn_sh_w1, L0_ffn_sh_b1, L0_ffn_sh_w2, L0_ffn_sh_b2, L0_ffn_ew1, L0_ffn_eb1, L0_ffn_ew2, L0_ffn_eb2, L1_attn_a_Wq, L1_attn_a_bq, L1_attn_a_Wk, L1_attn_a_bk, L1_attn_a_Wv, L1_attn_a_bv, L1_attn_b_gamma1, L1_attn_b_W_in, L1_attn_b_conv_w, L1_attn_b_conv_b, L1_attn_b_W_gates, L1_attn_b_b_gates, L1_attn_b_forget_base, L1_attn_b_W_out, L1_attn_b_gamma2, L1_attn_b_W_grow, L1_attn_b_W_shrink, L1_ffn_norm1_w, L1_ffn_norm2_w, L1_ffn_wq, L1_ffn_wk, L1_ffn_wv, L1_ffn_wo, L1_ffn_router_w, L1_ffn_sh_gate, L1_ffn_sh_up, L1_ffn_sh_down, L1_ffn_e_gate, L1_ffn_e_up, L1_ffn_e_down):

    def _L0_attn_a_ref(X, W_q, W_k, W_v, W_o, lambda_q1, lambda_k1, lambda_q2, lambda_k2, rms_scale):
        import jax, jax.numpy as jnp
        import numpy as np
        B, N, D, H = (2, 256, 128, 8)
        DH = D // H
        LAMBDA_INIT = 0.8
        EPS = 1e-05
        b, n, d = X.shape
        Q = (X @ W_q).reshape(b, n, H, 2 * DH).transpose(0, 2, 1, 3)
        K = (X @ W_k).reshape(b, n, H, 2 * DH).transpose(0, 2, 1, 3)
        V = (X @ W_v).reshape(b, n, H, 2 * DH).transpose(0, 2, 1, 3)
        Q1, Q2 = (Q[..., :DH], Q[..., DH:])
        K1, K2 = (K[..., :DH], K[..., DH:])
        lam = jnp.exp(jnp.sum(lambda_q1 * lambda_k1, axis=-1)) - jnp.exp(jnp.sum(lambda_q2 * lambda_k2, axis=-1)) + LAMBDA_INIT
        lam = lam[None, :, None, None]
        scaling = 1.0 / np.sqrt(DH)
        causal = jnp.tril(jnp.ones((n, n), jnp.bool_))
        neg_inf = jnp.finfo(X.dtype).min
        A1 = jnp.einsum('bhqd,bhkd->bhqk', Q1, K1) * scaling
        A2 = jnp.einsum('bhqd,bhkd->bhqk', Q2, K2) * scaling
        A1 = jnp.where(causal, A1, neg_inf)
        A2 = jnp.where(causal, A2, neg_inf)
        attn = jax.nn.softmax(A1, axis=-1) - lam * jax.nn.softmax(A2, axis=-1)
        O = jnp.einsum('bhqk,bhkd->bhqd', attn, V)
        rms = jnp.sqrt(jnp.mean(O * O, axis=-1, keepdims=True) + EPS)
        O = O / rms * rms_scale
        O = O * (1.0 - LAMBDA_INIT)
        O = O.transpose(0, 2, 1, 3).reshape(b, n, H * 2 * DH)
        return O @ W_o

    def _L0_attn_b_ref(x, Wq, Wk, Wv, Wo):
        import math
        import jax, jax.numpy as jnp
        import numpy as np
        N_HEADS = 16
        CHUNK = 64

        def _chunked_causal_attention(q, k, v, chunk=CHUNK):
            B, H, S, D = q.shape
            scale = 1.0 / math.sqrt(D)
            nc = S // chunk
            qc = jnp.moveaxis(q.reshape(B, H, nc, chunk, D), 2, 0)
            kpos = jnp.arange(S)

            def body(_, inp):
                qi, ci = inp
                scores = jnp.einsum('bhcd,bhsd->bhcs', qi, k) * scale
                qpos = ci * chunk + jnp.arange(chunk)
                mask = kpos[None, :] <= qpos[:, None]
                scores = jnp.where(mask, scores, jnp.finfo(scores.dtype).min)
                p = jax.nn.softmax(scores, axis=-1)
                return (None, jnp.einsum('bhcs,bhsd->bhcd', p, v))
            _, outs = jax.lax.scan(body, None, (qc, jnp.arange(nc)))
            return jnp.moveaxis(outs, 0, 2).reshape(B, H, S, D)
        B, S, D = x.shape
        H = N_HEADS
        hd = D // H
        q = (x @ Wq.T).reshape(B, S, H, hd).transpose(0, 2, 1, 3)
        k = (x @ Wk.T).reshape(B, S, H, hd).transpose(0, 2, 1, 3)
        v = (x @ Wv.T).reshape(B, S, H, hd).transpose(0, 2, 1, 3)
        out = _chunked_causal_attention(q, k, v)
        out = out.transpose(0, 2, 1, 3).reshape(B, S, D)
        return out @ Wo.T

    def _L0_ffn_ref(x, gate_w, gate_b, sh_w1, sh_b1, sh_w2, sh_b2, ew1, eb1, ew2, eb2):
        import jax, jax.numpy as jnp
        import numpy as np
        TOP_K = 2

        def _mlp(x, w1, b1, w2, b2):
            h = jax.nn.gelu(jnp.einsum('bsd,di->bsi', x, w1) + b1)
            return jnp.einsum('bsi,id->bsd', h, w2) + b2
        E = ew1.shape[0]
        router_probs = jax.nn.softmax(jnp.einsum('bsd,de->bse', x, gate_w) + gate_b, axis=-1)
        expert_values, expert_indices = jax.lax.top_k(router_probs, k=TOP_K)
        expert_values = expert_values / (jnp.sum(expert_values, axis=-1, keepdims=True) + 1e-09)
        h = jax.nn.gelu(jnp.einsum('bsd,edi->bsei', x, ew1) + eb1)
        all_outputs = jnp.einsum('bsei,eid->bsed', h, ew2) + eb2
        one_hot = jax.nn.one_hot(expert_indices, E, dtype=x.dtype)
        weights_E = (one_hot * expert_values[..., None]).sum(axis=2)
        moe_out = jnp.einsum('bse,bsed->bsd', weights_E, all_outputs)
        return x + _mlp(x, sh_w1, sh_b1, sh_w2, sh_b2) + moe_out

    def _L1_attn_a_ref(x, Wq, bq, Wk, bk, Wv, bv):
        import jax, jax.numpy as jnp
        import numpy as np
        import math
        DIM_EMB = 128
        KSQRT = math.sqrt(DIM_EMB)
        q = jnp.einsum('bte,de->btd', x, Wq) + bq
        k = jnp.einsum('bte,de->btd', x, Wk) + bk
        v = jnp.einsum('bte,de->btd', x, Wv) + bv
        dot = jnp.einsum('bqd,bkd->bqk', q, k) / KSQRT
        p = jax.nn.softmax(dot, axis=-1)
        z = jnp.einsum('bqk,bkd->bqd', p, v)
        return z

    def _L1_attn_b_ref(x, gamma1, W_in, conv_w, conv_b, W_gates, b_gates, forget_base, W_out, gamma2, W_grow, W_shrink):
        import jax, jax.numpy as jnp
        import numpy as np
        DIM = 128
        HID = int(DIM * 1.5)
        GHID = int(DIM * 2)
        K = 4
        ALPHA_LOG_SCALE = -8.0

        def _rmsnorm(x, gamma):
            n = jnp.linalg.norm(x, axis=-1, keepdims=True)
            return gamma * jnp.sqrt(jnp.asarray(x.shape[-1], x.dtype)) * (x / n)

        def _causal_depthwise_conv(x, w, b):
            xc = jnp.transpose(x, (0, 2, 1))
            xc = jnp.pad(xc, ((0, 0), (0, 0), (K - 1, 0)))
            y = jax.lax.conv_general_dilated(xc, w, window_strides=(1,), padding='VALID', dimension_numbers=('NCH', 'OIH', 'NCH'), feature_group_count=w.shape[0])
            y = y + b[None, :, None]
            return jnp.transpose(y, (0, 2, 1))

        def _linear_scan(alpha, x):

            def combine(c1, c2):
                a1, b1 = c1
                a2, b2 = c2
                return (a1 * a2, a2 * b1 + b2)
            _, h = jax.lax.associative_scan(combine, (alpha, x), axis=1)
            return h
        xn = _rmsnorm(x, gamma1)
        u = jnp.einsum('btd,hd->bth', xn, W_in)
        gate, v = jnp.split(u, 2, axis=-1)
        v = _causal_depthwise_conv(v, conv_w, conv_b)
        g = jnp.einsum('bth,gh->btg', v, W_gates) + b_gates
        forget, inp = jnp.split(g, 2, axis=-1)
        log_alpha = ALPHA_LOG_SCALE * jax.nn.softplus(forget_base) * jax.nn.sigmoid(forget)
        alpha = jnp.exp(log_alpha)
        beta = jnp.sqrt(1.0 - alpha ** 2 + 1e-06)
        xg = beta * jax.nn.sigmoid(inp) * v
        h = _linear_scan(alpha, xg)
        hawk_out = jnp.einsum('bth,dh->btd', jax.nn.gelu(gate, approximate=False) * h, W_out)
        x = x + hawk_out
        xn2 = _rmsnorm(x, gamma2)
        grow = jnp.einsum('btd,gd->btg', xn2, W_grow)
        gate2, v2 = jnp.split(grow, 2, axis=-1)
        mlp = jnp.einsum('btg,dg->btd', jax.nn.gelu(gate2, approximate=False) * v2, W_shrink)
        return x + mlp

    def _L1_ffn_ref(X, norm1_w, norm2_w, wq, wk, wv, wo, router_w, sh_gate, sh_up, sh_down, e_gate, e_up, e_down):
        import jax, jax.numpy as jnp
        import numpy as np
        D_MODEL = 128
        N_HEADS = 16
        D_HEAD = D_MODEL // N_HEADS
        N_EXPERTS = 8
        TOP_K = 2
        D_FF = 256
        EPS = 1e-06

        def rmsnorm(x, w):
            return x * jax.lax.rsqrt(jnp.mean(x * x, axis=-1, keepdims=True) + EPS) * w

        def swiglu(x, w_gate, w_up, w_down):
            return jax.nn.silu(x @ w_gate) * (x @ w_up) @ w_down
        B, S, d = X.shape
        scale = 1.0 / jnp.sqrt(jnp.asarray(D_HEAD, X.dtype))
        h = rmsnorm(X, norm1_w)
        q = (h @ wq).reshape(B, S, N_HEADS, D_HEAD)
        k = (h @ wk).reshape(B, S, N_HEADS, D_HEAD)
        v = (h @ wv).reshape(B, S, N_HEADS, D_HEAD)
        scores = jnp.einsum('bshd,bthd->bhst', q, k) * scale
        attn = jax.nn.softmax(scores, axis=-1)
        ctx = jnp.einsum('bhst,bthd->bshd', attn, v).reshape(B, S, d)
        X = X + ctx @ wo
        h2 = rmsnorm(X, norm2_w).reshape(B * S, d)
        logits = h2 @ router_w
        probs = jax.nn.softmax(logits, axis=-1)
        topw, topi = jax.lax.top_k(probs, TOP_K)
        topw = jax.nn.softmax(topw, axis=-1)
        combine = jnp.sum(jax.nn.one_hot(topi, N_EXPERTS, dtype=h2.dtype) * topw[..., None], axis=1)
        shared = swiglu(h2, sh_gate, sh_up, sh_down)
        gate = jnp.einsum('td,edf->etf', h2, e_gate)
        up = jnp.einsum('td,edf->etf', h2, e_up)
        eout = jnp.einsum('etf,efd->etd', jax.nn.silu(gate) * up, e_down)
        spec = jnp.einsum('etd,te->td', eout, combine)
        moe_out = (shared + spec).reshape(B, S, d)
        return X + moe_out
    x = L0_attn_a_X
    x = x + _L0_attn_a_ref(_layernorm(x, axis=-1), L0_attn_a_W_q, L0_attn_a_W_k, L0_attn_a_W_v, L0_attn_a_W_o, L0_attn_a_lambda_q1, L0_attn_a_lambda_k1, L0_attn_a_lambda_q2, L0_attn_a_lambda_k2, L0_attn_a_rms_scale)
    x = x + _L0_ffn_ref(_layernorm(x, axis=-1), L0_ffn_gate_w, L0_ffn_gate_b, L0_ffn_sh_w1, L0_ffn_sh_b1, L0_ffn_sh_w2, L0_ffn_sh_b2, L0_ffn_ew1, L0_ffn_eb1, L0_ffn_ew2, L0_ffn_eb2)
    x = x + _L0_attn_b_ref(_layernorm(x, axis=-1), L0_attn_b_Wq, L0_attn_b_Wk, L0_attn_b_Wv, L0_attn_b_Wo)
    x = x + _L0_ffn_ref(_layernorm(x, axis=-1), L0_ffn_gate_w, L0_ffn_gate_b, L0_ffn_sh_w1, L0_ffn_sh_b1, L0_ffn_sh_w2, L0_ffn_sh_b2, L0_ffn_ew1, L0_ffn_eb1, L0_ffn_ew2, L0_ffn_eb2)
    x = x + _L1_attn_a_ref(_layernorm(x, axis=-1), L1_attn_a_Wq, L1_attn_a_bq, L1_attn_a_Wk, L1_attn_a_bk, L1_attn_a_Wv, L1_attn_a_bv)
    x = x + _L1_ffn_ref(_layernorm(x, axis=-1), L1_ffn_norm1_w, L1_ffn_norm2_w, L1_ffn_wq, L1_ffn_wk, L1_ffn_wv, L1_ffn_wo, L1_ffn_router_w, L1_ffn_sh_gate, L1_ffn_sh_up, L1_ffn_sh_down, L1_ffn_e_gate, L1_ffn_e_up, L1_ffn_e_down)
    x = x + _L1_attn_b_ref(_layernorm(x, axis=-1), L1_attn_b_gamma1, L1_attn_b_W_in, L1_attn_b_conv_w, L1_attn_b_conv_b, L1_attn_b_W_gates, L1_attn_b_b_gates, L1_attn_b_forget_base, L1_attn_b_W_out, L1_attn_b_gamma2, L1_attn_b_W_grow, L1_attn_b_W_shrink)
    x = x + _L1_ffn_ref(_layernorm(x, axis=-1), L1_ffn_norm1_w, L1_ffn_norm2_w, L1_ffn_wq, L1_ffn_wk, L1_ffn_wv, L1_ffn_wo, L1_ffn_router_w, L1_ffn_sh_gate, L1_ffn_sh_up, L1_ffn_sh_down, L1_ffn_e_gate, L1_ffn_e_up, L1_ffn_e_down)
    return x

_drawn_inputs = setup_inputs


def setup_inputs(seed=0):
    import zlib

    import numpy as np

    out = dict(_drawn_inputs(seed))
    spreads = {'L0_attn_a_rms_scale': (1.0, 0.2),
     'L0_ffn_gate_b': (0.0, 0.1),
     'L0_ffn_sh_b1': (0.0, 0.1),
     'L0_ffn_sh_b2': (0.0, 0.1),
     'L0_ffn_eb1': (0.0, 0.1),
     'L0_ffn_eb2': (0.0, 0.1),
     'L1_attn_b_gamma1': (1.0, 0.6),
     'L1_attn_b_conv_b': (0.0, 0.1),
     'L1_attn_b_b_gates': (0.0, 0.8),
     'L1_attn_b_gamma2': (1.0, 0.2),
     'L1_ffn_norm1_w': (1.0, 0.6),
     'L1_ffn_norm2_w': (1.0, 0.6)}
    factors = {'L0_attn_a_lambda_q1': 3.411,
     'L0_attn_a_lambda_k2': 3.049,
     'L0_attn_b_Wq': 8.0,
     'L0_attn_b_Wk': 8.0,
     'L0_attn_b_Wv': 6.777,
     'L0_attn_b_Wo': 7.258,
     'L1_attn_a_bq': 8.0,
     'L1_attn_a_bk': 8.0,
     'L1_attn_b_W_gates': 3.685,
     'L1_ffn_wq': 8.0,
     'L1_ffn_wk': 8.0,
     'L1_ffn_wv': 8.0,
     'L1_ffn_wo': 8.0,
     'L1_ffn_router_w': 8.0,
     'L1_ffn_sh_gate': 8.0,
     'L1_ffn_sh_up': 8.0,
     'L1_ffn_sh_down': 8.0,
     'L1_ffn_e_gate': 8.0,
     'L1_ffn_e_up': 8.0,
     'L1_ffn_e_down': 8.0}
    for name, (base, spread) in spreads.items():
        noise = np.random.default_rng([zlib.crc32(name.encode()), seed]).standard_normal(out[name].shape)
        drawn = base * np.exp(spread * noise) if base else spread * noise
        out[name] = jnp.asarray(drawn.astype(out[name].dtype))
    for name, factor in factors.items():
        out[name] = (out[name] * factor).astype(out[name].dtype)
    return out
```

```python
from contextlib import ExitStack

import concourse.bass as bass
from concourse import mybir

F32 = mybir.dt.float32
F32R = mybir.dt.float32r
BF16 = mybir.dt.bfloat16
ALU = mybir.AluOpType
ACT = mybir.ActivationFunctionType
AX = mybir.AxisListType.X

P = 128
D = 128
SEQ = 256
NSEQ = 16
TPS = SEQ // P
BLK = 512
TPB = BLK // P
NBLK = NSEQ * SEQ // BLK
PAD = TPB
NT = NSEQ * TPS + 2 * PAD
E = 8
E_CONST = 2.718281828459045
BIG = 1e30


class Chain:

    def __init__(self, eng, sem, base):
        self.eng, self.sem, self.base, self.n = eng, sem, base, 0

    def __call__(self, ins):
        self.n += 1
        ins.then_inc(self.sem, 1)
        self.eng.wait_ge(self.sem, self.base + self.n)


class Stage:

    def __init__(self, nc):
        self.nc, self.ctx, self.sems = nc, ExitStack(), []

    def sb(self, name, shape, dt=F32):
        return self.ctx.enter_context(self.nc.sbuf_tensor(name, shape, dt))

    def bank(self, name, banks=1):
        return self.ctx.enter_context(self.nc.psum_tensor(name, [P, 512 * banks], F32))

    def sem(self, name):
        s = self.nc.alloc_semaphore(name)
        self.sems.append(s)
        return s

    def close(self):
        self.nc.clear_and_free_semaphores(self.sems)
        self.nc.all_engine_barrier()
        self.ctx.close()


def split_weights(nc, tag, parts, width):
    st = Stage(nc)
    RING = 3
    raw = st.sb(f"{tag}_raw", [P, RING, width])
    loaded = [st.sem(f"{tag}_loaded{k}") for k in range(RING)]
    high_done = st.sem(f"{tag}_high")
    low_done = st.sem(f"{tag}_low")
    with nc.Block() as block:
        @block.sync
        def _(sp):
            for n, (loads, _, _) in enumerate(parts):
                if n >= RING:
                    sp.wait_ge(low_done, n - RING + 1)
                for (c0, c1), src in loads:
                    sp.dma_start(raw[:, n % RING, c0:c1] if len(src.shape) == 2 else
                                 raw[:, n % RING, c0:c1].rearrange("p (a b) -> p a b", a=src.shape[1]),
                                 src).then_inc(loaded[n % RING], 16)

        @block.scalar
        def _(act):
            for n, (loads, high, _) in enumerate(parts):
                act.wait_ge(loaded[n % RING], 16 * len(loads) * (n // RING + 1))
                act.activation(high, raw[:, n % RING, :], ACT.Copy).then_inc(high_done, 1)

        @block.vector
        def _(dve):
            for n, (loads, high, low) in enumerate(parts):
                dve.wait_ge(high_done, n + 1)
                dve.tensor_tensor(low, raw[:, n % RING, :], high.bitcast(F32), ALU.subtract).then_inc(low_done, 1)
    st.close()


def expert_stage(nc, tag, kind, G, w):
    X, ident, WH, WL = G["X"], G["ident"], G["WH"], G["WL"]
    gelu = kind == "gelu"
    SRC = X if gelu else G["Y"]
    EW = 1024 if gelu else 768
    CH = 4 if gelu else 2
    U = (E + 1) * CH
    R = 4 if gelu else 3
    HB = 4 if gelu else 2
    LAG = 2
    XB = X[:, :, :].rearrange("p (b t) d -> p b t d", t=TPB)
    SB_ = SRC[:, :, :].rearrange("p (b t) d -> p b t d", t=TPB)

    st = Stage(nc)
    sb, sem = (lambda n, s, d=F32: st.sb(f"{tag}_{n}", s, d)), (lambda n: st.sem(f"{tag}_{n}"))
    spare, spare2 = sb("spare", [P, 1]), sb("spare2", [P, 1])
    epst = sb("epst", [P, 4])
    stats = sb("stats", [P, TPB, 6])
    mv = sb("mv", [P, TPB, 2])
    rs = sb("rs", [P, TPB])
    rs2 = sb("rs2", [P, TPB])
    xn = sb("xn", [P, TPB, D])
    xT = sb("xT", [P, BLK])
    xh = [sb(f"xh{k}", [P, BLK], F32R) for k in range(2)]
    xl = [sb(f"xl{k}", [P, BLK], F32R) for k in range(2)]
    lg, l2, o1, o2, cc, ex, sel, comb = [sb(n, [P, TPB, E]) for n in ("lg", "l2", "o1", "o2", "cc", "ex", "sel", "comb")]
    r1, r2, r3 = [sb(n, [P, TPB]) for n in ("r1", "r2", "r3")]
    rank = sb("rank", [P, TPB, E])
    econst = sb("econst", [P, TPB, E])
    half = sb("half", [P, TPB])
    gwr = sb("gwr", [P, E])
    gwh = sb("gwh", [P, E], F32R)
    gwl = sb("gwl", [P, E], F32R)
    cTh = [sb(f"cTh{k}", [E, BLK], F32R) for k in range(2)]
    cTl = [sb(f"cTl{k}", [E, BLK], F32R) for k in range(2)]
    selr = sb("selr", [E, E, D])
    selE = sb("selE", [E, E, D], F32R)
    wbc = sb("wbc", [P, 2, BLK])
    acc = sb("acc", [P, 2, BLK])
    tmp = sb("tmp", [P, BLK])
    credit = sb("credit", [P, 16])
    g32 = sb("g32", [P, R, BLK])
    gh = [sb(f"gh{k}", [P, BLK], F32R) for k in range(R)]
    gl = [sb(f"gl{k}", [P, BLK], F32R) for k in range(R)]
    if gelu:
        b1 = sb("b1", [P, (E + 1) * CH])
        b2 = sb("b2", [P, 1])
        gb = sb("gb", [P, E])
        eb2r = sb("eb2r", [E, D])
        eb2h = sb("eb2h", [E, D], F32R)
        eb2l = sb("eb2l", [E, D], F32R)
    else:
        s32 = sb("s32", [P, 2, BLK])
        nw = sb("nw", [P, 1])
    hb = [st.bank(f"{tag}_hb{k}", 1 if gelu else 2) for k in range(HB)]
    outb = [st.bank(f"{tag}_out{k}") for k in range(2)]
    misc = st.bank(f"{tag}_misc")
    wbb = st.bank(f"{tag}_wbb")

    started = sem("started")
    consts_in, const_ready, split_ready = sem("consts_in"), sem("const_ready"), sem("split_ready")
    mv_ready, rstd_ready, xn_ready, xadd_done = sem("mv_ready"), sem("rstd_ready"), sem("xn_ready"), sem("xadd_done")
    xT_psum, xT32_ready, xhigh_ready, xT_ready = sem("xT_psum"), sem("xT32_ready"), sem("xhigh_ready"), sem("xT_ready")
    logits_psum, lx_ready, ex_ready, comb_ready = sem("logits_psum"), sem("lx_ready"), sem("ex_ready"), sem("comb_ready")
    combT_psum, chigh_ready, combT_ready = sem("combT_psum"), sem("chigh_ready"), sem("combT_ready")
    prep_chain, pool_chain = sem("prep_chain"), sem("pool_chain")
    h_psum, silu_done, hid_done, hi_done, lo_done, g_free = [sem(n) for n in ("h_psum", "silu_done", "hid_done", "hi_done", "lo_done", "g_free")]
    wb_psum, wb_copied, out_free, acc_step = [sem(n) for n in ("wb_psum", "wb_copied", "out_free", "acc_step")]
    fin_psum, fin_done = sem("fin_psum"), sem("fin_done")
    NPREP = 19 if gelu else 20
    NPOOL = 1 if gelu else 3
    NCONST = 4 if gelu else 2

    with nc.Block() as block:
        @block.sync
        def _(sp):
            sp.dma_start(gwr[:, :], w["gate_w"]).then_inc(consts_in, 16)
            if gelu:
                sp.dma_start(b1[:, 0:CH], w["sh_b1"].rearrange("(c p) -> p c", p=P), allow_slow_non_contiguous=True).then_inc(consts_in, 16)
                sp.dma_start(b1[:, CH:].rearrange("p (e c) -> p e c", e=E), w["eb1"].rearrange("e (c p) -> p e c", p=P), allow_slow_non_contiguous=True).then_inc(consts_in, 16)
                sp.dma_start(b2[:, :], w["sh_b2"].rearrange("(p a) -> p a", a=1)).then_inc(consts_in, 16)
                sp.dma_start(gb[:, :], w["gate_b"].rearrange("(a e) -> a e", a=1).to_broadcast([P, E])).then_inc(consts_in, 16)
                sp.dma_start(eb2r[:, :], w["eb2"]).then_inc(consts_in, 16)
            else:
                sp.dma_start(nw[:, :], w["norm_w"].rearrange("(p a) -> p a", a=1)).then_inc(consts_in, 16)

        NCIN = 16 * (6 if gelu else 2)

        @block.gpsimd
        def _(pool):
            pool.memset(econst[:, :, :], E_CONST)
            pool.memset(epst[:, :], w["eps"])
            pool.memset(half[:, :], -0.5)
            for e in range(E):
                pool.memset(rank[:, :, e:e + 1], float(E - e))
            pool.memset(selr[:, :, :], 0.0).then_inc(const_ready, 1)
            pool.wait_ge(const_ready, 1)
            pool.affine_select(out=selr[:, :, :], in_=selr[:, :, :], compare_op=ALU.not_equal, fill=1.0, base=0,
                               pattern=[[-1, E], [0, D]], channel_multiplier=1).then_inc(const_ready, 1)

            def prep(b):
                pool.wait_ge(mv_ready, b + 1)
                ch = Chain(pool, pool_chain, b * NPOOL)
                if gelu:
                    ch(pool.tensor_tensor(rs2[:, :], mv[:, :, 1], epst[:, 0:mv.shape[1]], ALU.add))
                else:
                    ch(pool.tensor_tensor(rs[:, :], mv[:, :, 0], mv[:, :, 0], ALU.mult))
                    ch(pool.tensor_tensor(rs2[:, :], rs[:, :], mv[:, :, 1], ALU.add))
                    ch(pool.tensor_tensor(rs[:, :], rs2[:, :], epst[:, :], ALU.add))
                pool.tensor_tensor(rs[:, :], (rs2 if gelu else rs)[:, :], half[:, :], ALU.pow).then_inc(rstd_ready, 1)
                assert ch.n == NPOOL
                if gelu:
                    pool.wait_ge(xn_ready, b + 1)
                    pool.tensor_tensor(XB[:, b + 1, :, :], XB[:, b + 1, :, :], xn[:, :, :], ALU.add).then_inc(xadd_done, 1)
                k = 1 if gelu else 2
                for j in range(k):
                    pool.wait_ge(lx_ready, b * k + j + 1)
                    pool.tensor_tensor(ex[:, :, :], econst[:, :, :], l2[:, :, :], ALU.pow).then_inc(ex_ready, 1)

            pool.memset(spare2[:, :], 0.0).then_inc(xadd_done, 1)
            prep(0)
            with pool.Fori(0, NBLK) as b:
                prep(b + 1)

        @block.scalar
        def _(act):
            act.wait_ge(consts_in, NCIN)
            act.wait_ge(started, 1)

            def turn(b):
                act.wait_ge(xT_psum, b + 1)
                if gelu:
                    act.activation(xT[:, :], misc[:, :], ACT.Identity).then_inc(xT32_ready, 1)
                else:
                    act.activation(xT[:, :], misc[:, :], ACT.Identity, scale=nw[:, :]).then_inc(xT32_ready, 1)

            def high(b, n):
                act.wait_ge(hid_done, b * U + n + 1 + HB)
                act.wait_ge(g_free, b * U + n + 1)
                act.activation(gh[n % R][:, :], g32[:, n % R, :], ACT.Identity).then_inc(hi_done, 1)

            def spread(b, e):
                act.wait_ge(wb_psum, b * E + e)
                act.wait_ge(out_free, b * (E + 1) + e - 1 + 2)
                act.activation(wbc[:, e % 2, :], wbb[:, :], ACT.Identity).then_inc(wb_copied, 1)

            turn(0)
            with act.Fori(0, NBLK // 2) as i:
                for p in range(2):
                    b = i * 2 + p
                    for n in range(U):
                        e, c = divmod(n, CH)
                        act.wait_ge(h_psum, b * U + n + 1)
                        if gelu:
                            act.wait_ge(g_free, b * U + n + 1)
                            act.activation(g32[:, n % R, :], hb[n % HB][:, :], ACT.Gelu_apprx_tanh, bias=b1[:, n:n + 1])
                            act.activation(gh[n % R][:, :], hb[n % HB][:, :], ACT.Gelu_apprx_tanh,
                                           bias=b1[:, n:n + 1]).then_inc(hid_done, 1)
                        else:
                            act.activation(s32[:, n % 2, :], hb[n % HB][:, 0:512], ACT.Silu).then_inc(silu_done, 1)
                            if n >= 1:
                                high(b, n - 1)
                            if c == 1 and e + 1 <= E:
                                spread(b, e + 1)
                        if n == (13 if gelu else 6):
                            turn(b + 1)
                    if not gelu:
                        high(b, U - 1)

        @block.vector
        def _(dve):
            for j, s in enumerate([hid_done] * HB + [g_free] * R + [out_free] * 2 + [wb_copied, acc_step]):
                dve.memset(credit[:, j:j + 1], 0.0).then_inc(s, 1)
            dve.memset(acc[:, :, :], 0.0).then_inc(started, 1)
            dve.wait_ge(consts_in, NCIN)
            dve.wait_ge(const_ready, 2)
            dve.tensor_copy(gwh[:, :], gwr[:, :])
            dve.tensor_copy(selE[:, :, :], selr[:, :, :]).then_inc(split_ready, 1)
            if gelu:
                dve.tensor_copy(eb2h[:, :], eb2r[:, :]).then_inc(split_ready, 1)
            dve.wait_ge(split_ready, 2 if gelu else 1)
            dve.tensor_tensor(gwl[:, :], gwr[:, :], gwh[:, :].bitcast(F32), ALU.subtract).then_inc(split_ready, 1)
            if gelu:
                dve.tensor_tensor(eb2l[:, :], eb2r[:, :], eb2h[:, :].bitcast(F32), ALU.subtract).then_inc(split_ready, 1)

            def stat(b):
                ch = Chain(dve, prep_chain, b * NPREP)
                for t in range(TPB):
                    last = dve.bn_stats(stats[:, t, :], SB_[:, b + 1, t, :])
                ch(last)
                dve.memset(spare[:, :], 0.0)
                for t in range(TPB):
                    last = dve.bn_aggr(mv[:, t, :], stats[:, t, :])
                last.then_inc(mv_ready, 1)

            def norm(b):
                dve.wait_ge(rstd_ready, b + 1)
                for t in range(TPB):
                    if gelu:
                        last = dve.tensor_scalar(xn[:, t, :], SB_[:, b + 1, t, :], mv[:, t, 0:1], rs[:, t:t + 1], ALU.subtract, ALU.mult)
                    else:
                        last = dve.tensor_scalar(xn[:, t, :], SB_[:, b + 1, t, :], rs[:, t:t + 1], None, ALU.mult)
                last.then_inc(xn_ready, 1)

            def split_x(b, q):
                dve.wait_ge(xT32_ready, b + 1)
                dve.tensor_copy(xh[q][:, :], xT[:, :]).then_inc(xhigh_ready, 1)
                dve.wait_ge(xhigh_ready, b + 1)
                dve.tensor_tensor(xl[q][:, :], xT[:, :], xh[q][:, :].bitcast(F32), ALU.subtract).then_inc(xT_ready, 1)

            def bc(a):
                return a.unsqueeze(2).to_broadcast([P, TPB, E])

            def route1(b):
                ch = Chain(dve, prep_chain, b * NPREP + 1)
                dve.wait_ge(logits_psum, b + 1)
                lp = misc[:, 0:TPB * E].rearrange("p (t e) -> p t e", e=E)
                if gelu:
                    ch(dve.tensor_tensor(lg[:, :, :], lp, gb[:, :].unsqueeze(1).to_broadcast([P, TPB, E]), ALU.add))
                else:
                    ch(dve.tensor_copy(lg[:, :, :], lp))
                ch(dve.reduce_max(r1[:, :], lg[:, :, :], AX))
                dve.tensor_tensor(l2[:, :, :], lg[:, :, :], bc(r1[:, :]), ALU.subtract).then_inc(lx_ready, 1)
                ch(dve.tensor_tensor(cc[:, :, :], lg[:, :, :], bc(r1[:, :]), ALU.is_equal))
                ch(dve.tensor_tensor(o1[:, :, :], cc[:, :, :], rank[:, :, :], ALU.mult))
                ch(dve.reduce_max(r2[:, :], o1[:, :, :], AX))
                ch(dve.tensor_tensor(cc[:, :, :], o1[:, :, :], bc(r2[:, :]), ALU.is_equal))
                ch(dve.scalar_tensor_tensor(o2[:, :, :], cc[:, :, :], -3e38, lg[:, :, :], ALU.mult, ALU.add))
                ch(dve.reduce_max(r1[:, :], o2[:, :, :], AX))
                ch(dve.tensor_tensor(o1[:, :, :], o2[:, :, :], bc(r1[:, :]), ALU.is_equal))
                ch(dve.tensor_tensor(o2[:, :, :], o1[:, :, :], rank[:, :, :], ALU.mult))
                ch(dve.reduce_max(r2[:, :], o2[:, :, :], AX))
                ch(dve.tensor_tensor(o1[:, :, :], o2[:, :, :], bc(r2[:, :]), ALU.is_equal))
                ch(dve.tensor_tensor(sel[:, :, :], o1[:, :, :], cc[:, :, :], ALU.add))
                assert ch.n == 13

            def route2(b):
                ch = Chain(dve, prep_chain, b * NPREP + 14)
                k = 1 if gelu else 2
                dve.wait_ge(ex_ready, b * k + 1)
                ch(dve.reduce_sum(r1[:, :], ex[:, :, :], AX))
                if gelu:
                    ch(dve.tensor_tensor(cc[:, :, :], ex[:, :, :], sel[:, :, :], ALU.mult))
                    ch(dve.reduce_sum(r2[:, :], cc[:, :, :], AX))
                    ch(dve.scalar_tensor_tensor(r3[:, :], r1[:, :], 1e-9, r2[:, :], ALU.mult, ALU.add))
                    ch(dve.reciprocal(r1[:, :], r3[:, :]))
                else:
                    ch(dve.reciprocal(r2[:, :], r1[:, :]))
                    ch(dve.tensor_tensor(cc[:, :, :], ex[:, :, :], bc(r2[:, :]), ALU.mult))
                    dve.tensor_tensor(l2[:, :, :], cc[:, :, :], bc(r2[:, :]), ALU.subtract).then_inc(lx_ready, 1)
                    dve.wait_ge(ex_ready, b * k + 2)
                    ch(dve.tensor_tensor(cc[:, :, :], ex[:, :, :], sel[:, :, :], ALU.mult))
                    ch(dve.reduce_sum(r2[:, :], cc[:, :, :], AX))
                    ch(dve.reciprocal(r1[:, :], r2[:, :]))
                dve.tensor_tensor(comb[:, :, :], cc[:, :, :], bc(r1[:, :]), ALU.mult).then_inc(comb_ready, 1)
                assert ch.n == NPREP - 14

            def split_comb(b, q):
                dve.wait_ge(combT_psum, b + 1)
                dve.tensor_copy(cTh[q][:, :], misc[0:E, :]).then_inc(chigh_ready, 1)
                dve.wait_ge(chigh_ready, b + 1)
                dve.tensor_tensor(cTl[q][:, :], misc[0:E, :], cTh[q][:, :].bitcast(F32), ALU.subtract).then_inc(combT_ready, 1)

            def spread(b, e):
                dve.wait_ge(wb_psum, b * E + e)
                dve.wait_ge(out_free, b * (E + 1) + e - 1 + 2)
                dve.tensor_copy(wbc[:, e % 2, :], wbb[:, :]).then_inc(wb_copied, 1)

            def combine(b, e, q):
                ob = b * (E + 1) + e
                dve.wait_ge(g_free, b * U + (e + 1) * CH + R)
                if e == 0:
                    if gelu:
                        ins = dve.tensor_scalar(acc[:, q, :], outb[(q + e) % 2][:, :], b2[:, :], None, ALU.add)
                    else:
                        ins = dve.tensor_copy(acc[:, q, :], outb[(q + e) % 2][:, :])
                    ins.then_inc(out_free, 1)
                else:
                    dve.wait_ge(acc_step, b * E + e)
                    dve.wait_ge(wb_copied, b * E + e + 1)
                    dve.tensor_tensor(tmp[:, :], outb[(q + e) % 2][:, :], wbc[:, e % 2, :], ALU.mult).then_inc(out_free, 1)
                    dve.wait_ge(out_free, ob + 1 + 2)
                    dve.tensor_tensor(acc[:, q, :], acc[:, q, :], tmp[:, :], ALU.add).then_inc(acc_step, 1)

            def low(b, n):
                dve.wait_ge(hi_done, b * U + n + 1)
                dve.tensor_tensor(gl[n % R][:, :], g32[:, n % R, :], gh[n % R][:, :].bitcast(F32), ALU.subtract).then_inc(lo_done, 1)

            def finish(k):
                dve.wait_ge(fin_psum, k + 1)
                if gelu:
                    dve.wait_ge(xadd_done, k + 1)
                dve.tensor_tensor(XB[:, k, :, :], XB[:, k, :, :], misc[:, :].rearrange("p (t d) -> p t d", d=D), ALU.add).then_inc(fin_done, 1)

            stat(0)
            norm(0)
            split_x(0, 0)
            route1(0)
            route2(0)
            split_comb(0, 0)
            with dve.Fori(0, NBLK // 2) as i:
                for p in range(2):
                    b = i * 2 + p
                    for n in range(U):
                        e, c = divmod(n, CH)
                        if gelu:
                            dve.wait_ge(hid_done, b * U + n + 1 + HB)
                            dve.tensor_tensor(gl[n % R][:, :], g32[:, n % R, :], gh[n % R][:, :].bitcast(F32), ALU.subtract).then_inc(lo_done, 1)
                            if c == 2 and e + 1 <= E:
                                spread(b, e + 1)
                            if c == 1 and e >= 1:
                                combine(b, e - 1, p)
                            at = {5: 0, 8: 1, 11: 2, 15: 3, 19: 4, 23: 5, 27: 6}.get(n)
                        else:
                            dve.wait_ge(silu_done, b * U + n + 1)
                            dve.tensor_tensor(g32[:, n % R, :], s32[:, n % 2, :], hb[n % HB][:, 512:1024], ALU.mult).then_inc(hid_done, 1)
                            if n >= 1:
                                low(b, n - 1)
                            if c == 1 and e >= 1:
                                combine(b, e - 1, p)
                            at = {2: 0, 3: 1, 5: 2, 7: 3, 9: 4, 10: 5, 13: 6}.get(n)
                        if at == 0:
                            finish(b)
                        elif at == 1:
                            stat(b + 1)
                        elif at == 2:
                            norm(b + 1)
                        elif at == 3:
                            split_x(b + 1, 1 - p)
                        elif at == 4:
                            route1(b + 1)
                        elif at == 5:
                            route2(b + 1)
                        elif at == 6:
                            split_comb(b + 1, 1 - p)
                    if not gelu:
                        low(b, U - 1)
                    combine(b, E, p)
            finish(NBLK)

        @block.tensor
        def _(pe):
            pe.wait_ge(split_ready, 4 if gelu else 2)
            pe.wait_ge(started, 1)

            def product(out, pairs, first=True, last=True):
                for k, (sh, sl, mh, ml) in enumerate(pairs):
                    pe.matmul(out, sh, mh, start=first and k == 0, stop=False)
                    pe.matmul(out, sh, ml, start=False, stop=False)
                    ins = pe.matmul(out, sl, mh, start=False, stop=last and k == len(pairs) - 1)
                return ins

            def turn(b):
                pe.wait_ge(xn_ready, b + 1)
                for t in range(TPB):
                    last = pe.transpose(misc[:, t * P:(t + 1) * P], xn[:, t, :], ident[:, :])
                last.then_inc(xT_psum, 1)

            def route(b, q):
                pe.wait_ge(xT_ready, b + 1)
                for t in range(TPB):
                    c = slice(t * P, (t + 1) * P)
                    last = product(misc[:, t * E:(t + 1) * E], [(xh[q][:, c], xl[q][:, c], gwh[:, :], gwl[:, :])])
                last.then_inc(logits_psum, 1)

            def turn_comb(b):
                pe.wait_ge(comb_ready, b + 1)
                for t in range(TPB):
                    last = pe.transpose(misc[0:E, t * P:(t + 1) * P], comb[:, t, :], ident[:, :])
                last.then_inc(combT_psum, 1)

            def first(b, n, q):
                pe.wait_ge(hid_done, b * U + n + 1)
                e, c = divmod(n, CH)
                o = e * EW + c * P
                last = product(hb[n % HB][:, 0:512], [(WH[:, o:o + P], WL[:, o:o + P], xh[q][:, :], xl[q][:, :])])
                if not gelu:
                    o += CH * P
                    last = product(hb[n % HB][:, 512:1024], [(WH[:, o:o + P], WL[:, o:o + P], xh[q][:, :], xl[q][:, :])])
                last.then_inc(h_psum, 1)

            def second(b, n, q):
                e, c = divmod(n, CH)
                ob = b * (E + 1) + e
                o = outb[(q + e) % 2][:, :]
                if c == 0:
                    pe.wait_ge(out_free, ob + 1)
                pe.wait_ge(lo_done, b * U + n + 1)
                k = e * EW + (EW - CH * P) + c * P
                bias = gelu and e == 0 and c == 0
                if bias:
                    product(o, [(eb2h[:, :], eb2l[:, :], cTh[q][:, :], cTl[q][:, :])], True, False)
                last = product(o, [(WH[:, k:k + P], WL[:, k:k + P], gh[n % R][:, :], gl[n % R][:, :])],
                               c == 0 and not bias, c == CH - 1)
                last.then_inc(g_free, 1)

            def spread(b, e, q):
                pe.wait_ge(wb_copied, b * E + e)
                pe.matmul(wbb[:, :], selE[:, e - 1, :], cTh[q][:, :], start=True, stop=False)
                pe.matmul(wbb[:, :], selE[:, e - 1, :], cTl[q][:, :], start=False, stop=True).then_inc(wb_psum, 1)

            def finish(k, q):
                pe.wait_ge(acc_step, k * E + 1)
                for t in range(TPB):
                    last = pe.transpose(misc[:, t * P:(t + 1) * P], acc[:, q, t * P:(t + 1) * P], ident[:, :])
                last.then_inc(fin_psum, 1)

            turn(0)
            route(0, 0)
            turn_comb(0)
            pe.wait_ge(combT_ready, 1)
            for n in range(LAG):
                first(0, n, 0)
            with pe.Fori(0, NBLK // 2) as i:
                for p in range(2):
                    b = i * 2 + p
                    for n in range(U):
                        e, c = divmod(n, CH)
                        if n + LAG < U:
                            first(b, n + LAG, p)
                        else:
                            first(b + 1, n + LAG - U, 1 - p)
                        second(b, n, p)
                        if c == (1 if gelu else 0) and e + 1 <= E:
                            spread(b, e + 1, p)
                        at = ({4: 0, 12: 1, 17: 2, 25: 3} if gelu else {1: 0, 5: 1, 8: 2, 12: 3}).get(n)
                        if at == 0:
                            finish(b, 1 - p)
                        elif at == 1:
                            pe.wait_ge(fin_done, b + 1)
                            turn(b + 1)
                        elif at == 2:
                            route(b + 1, 1 - p)
                        elif at == 3:
                            turn_comb(b + 1)
                    pe.wait_ge(combT_ready, b + 2)
            finish(NBLK, 1)
    st.close()


def make_globals(nc, ctx):
    G = {}
    G["X"] = ctx.enter_context(nc.sbuf_tensor("X", [P, NT, D], F32))
    G["Y"] = ctx.enter_context(nc.sbuf_tensor("Y", [P, NT, D], F32))
    G["ident"] = ctx.enter_context(nc.sbuf_tensor("ident", [P, P], F32))
    return G


def weight_memory(nc, ctx, G, tag, width):
    G["WH"] = ctx.enter_context(nc.sbuf_tensor(f"{tag}_WH", [P, (E + 1) * width], F32R))
    G["WL"] = ctx.enter_context(nc.sbuf_tensor(f"{tag}_WL", [P, (E + 1) * width], F32R))


def init_globals(nc, G, x, y=None):
    st = Stage(nc)
    loaded, cleared = st.sem("init_loaded"), st.sem("init_cleared")
    X, Y, ident = G["X"], G["Y"], G["ident"]
    with nc.Block() as block:
        @block.sync
        def _(sp):
            sp.dma_start(X[:, PAD:NT - PAD, :], x.rearrange("(t p) d -> p t d", p=P)).then_inc(loaded, 16)
            if y is not None:
                sp.dma_start(Y[:, PAD:NT - PAD, :], y.rearrange("(t p) d -> p t d", p=P)).then_inc(loaded, 16)
            sp.wait_ge(loaded, 16 if y is None else 32)

        @block.vector
        def _(dve):
            for T in (X, Y):
                dve.memset(T[:, 0:PAD, :], 0.0)
                dve.memset(T[:, NT - PAD:NT, :], 0.0)

        @block.gpsimd
        def _(pool):
            pool.memset(ident[:, :], 0.0).then_inc(cleared, 1)
            pool.wait_ge(cleared, 1)
            pool.affine_select(out=ident[:, :], in_=ident[:, :], compare_op=ALU.not_equal, fill=1.0, base=0,
                               pattern=[[-1, P]], channel_multiplier=1).then_inc(cleared, 1)
    st.close()


def store(nc, G, out):
    st = Stage(nc)
    stored = st.sem("stored")
    with nc.Block() as block:
        @block.sync
        def _(sp):
            sp.dma_start(out.rearrange("(t p) d -> p t d", p=P), G["X"][:, PAD:NT - PAD, :]).then_inc(stored, 16)
            sp.wait_ge(stored, 16)
    st.close()


def load_gelu_experts(nc, tag, G, a):
    parts = []
    for e in range(E + 1):
        w1 = a["L0_ffn_sh_w1"] if e == 0 else a["L0_ffn_ew1"][e - 1]
        w2 = a["L0_ffn_sh_w2"] if e == 0 else a["L0_ffn_ew2"][e - 1]
        cols = slice(e * 1024, (e + 1) * 1024)
        parts.append(([((0, 512), w1), ((512, 1024), w2.rearrange("(c p) d -> p c d", p=P))],
                      G["WH"][:, cols], G["WL"][:, cols]))
    split_weights(nc, tag, parts, 1024)


def load_swiglu_experts(nc, tag, G, a):
    parts = []
    for e in range(E + 1):
        wg, wu, wd = [a[f"L1_ffn_sh_{n}"] if e == 0 else a[f"L1_ffn_e_{n}"][e - 1] for n in ("gate", "up", "down")]
        cols = slice(e * 768, (e + 1) * 768)
        parts.append(([((0, 256), wg), ((256, 512), wu), ((512, 768), wd.rearrange("(c p) d -> p c d", p=P))],
                      G["WH"][:, cols], G["WL"][:, cols]))
    split_weights(nc, tag, parts, 768)


def gelu_args(a):
    return {k: a[f"L0_ffn_{k}"] for k in ("gate_w", "gate_b", "sh_b1", "eb1", "sh_b2", "eb2")} | {"eps": 1e-5}


def swiglu_args(a):
    return {"gate_w": a["L1_ffn_router_w"], "norm_w": a["L1_ffn_norm2_w"], "eps": 1e-6}


def attention_stage(nc, tag, kind, G, w):
    X, Y, ident = G["X"], G["Y"], G["ident"]
    diff, full, masked = kind == "diff", kind == "full", kind != "full"
    NMAP, QUAD, NQ = 16, 4, 4
    DH, DV = (16, 32) if diff else (8, 8)
    GR = 64 if diff else 32
    NTL = NMAP * GR // P
    HPT = P // GR
    QT = QUAD // HPT
    KR = 3 * DH + 2
    NV = NMAP // 2 if diff else NMAP
    VW = NV * DV
    NC = VW // P
    OV = DV + 1
    RO = 1 if diff else 2
    SCALE = float(DH) ** -0.5
    XS = X[:, :, :].rearrange("p (s t) d -> p s t d", t=TPS)
    YS = Y[:, :, :].rearrange("p (s t) d -> p s t d", t=TPS)
    S0 = PAD // TPS

    st = Stage(nc)
    sb, sem = (lambda n, s, d=F32: st.sb(f"{tag}_{n}", s, d)), (lambda n: st.sem(f"{tag}_{n}"))
    spare = sb("spare", [P, 1])
    epst = sb("epst", [P, 4])
    stats, mv = sb("stats", [P, TPS, 6]), sb("mv", [P, TPS, 2])
    rs, rs2, rs3 = sb("rs", [P, TPS]), sb("rs2", [P, TPS]), sb("rs3", [P, TPS])
    half, epsr = sb("half", [P, 32]), sb("epsr", [P, TPS])
    nil, inv_dv, eps_dv = sb("nil", [P, TPS * QUAD]), sb("inv_dv", [P, 16]), sb("eps_dv", [P, 16])
    xn = sb("xn", [P, TPS, D])
    xhat = sb("xhat", [P, 2, TPS, D]) if full else None
    xT, xh, xl = sb("xT", [P, SEQ]), sb("xh", [P, SEQ], F32R), sb("xl", [P, SEQ], F32R)
    hi2 = sb("hi2", [P, 512], F32R)
    Q1 = [sb(f"Q1_{k}", [P, NTL * SEQ], F32R) for k in range(2)]
    KS = [sb(f"KS_{k}", [P, NTL * SEQ], F32R) for k in range(2)]
    Q2 = [sb(f"Q2_{k}", [P, QT * SEQ], F32R) for k in range(2)]
    V = [sb(f"V_{k}", [P, TPS, NV, OV]) for k in range(2)]
    Pm = [sb(f"Pm{k}", [P, 512]) for k in range(4)]
    mx = sb("mx", [P, TPS, QUAD])
    mh = sb("mh", [P, TPS, QUAD], F32R)
    padm = sb("padm", [P, QT, TPS, HPT, GR])
    O = sb("O", [P, TPS, NMAP, OV])
    rec = sb("rec", [P, TPS, NMAP])
    ctx = sb("ctx", [P, TPS, VW])
    cT = sb("cT", [P, NC * SEQ])
    cTh, cTl = sb("cTh", [P, NC * SEQ], F32R), sb("cTl", [P, NC * SEQ], F32R)
    credit = sb("credit", [P, 16])
    if diff:
        T2 = sb("T2", [P, TPS, NMAP, DV])
        Dd = sb("Dd", [P, TPS, NV, DV])
        ss, sm, sm2, rr = [sb(n, [P, TPS * NV]) for n in ("ss", "sm", "sm2", "rr")]
        lamr = sb("lamr", [P, 4, NV * DH])
        lamp = sb("lamp", [P, 2, NV * DH])
        lams, lame, econst = sb("lams", [P, 2 * NV]), sb("lame", [P, 2 * NV]), sb("econst", [P, 2 * NV])
        wmap = sb("wmap", [P, NV, 2])
    raw = sb("raw", [P, 2 * NMAP * DH + VW + NC * D])
    wqk = [[sb(f"w{n}{k}", [P, NTL * P], F32R) for k in "hl"] for n in "qk"]
    wv = [sb(f"wv{k}", [P, VW], F32R) for k in "hl"]
    wo = [sb(f"wo{k}", [P, NC * D], F32R) for k in "hl"]
    rows = sb("rows", [P, 3, HPT])
    rvec = sb("rvec", [P, 3])
    colc = sb("colc", [P, 3])
    insc = sb("insc", [P, 1])
    outsc = sb("outsc", [P, 1])
    if masked:
        mf = sb("mf", [P, 2, 512])
        identb, maskS, maskT = sb("identb", [P, P], BF16), sb("maskS", [P, 512], BF16), sb("maskT", [P, 512], BF16)
    sbank = [st.bank(f"{tag}_s{k}") for k in range(2)]
    tbank = [st.bank(f"{tag}_t{k}") for k in range(4)]
    misc = st.bank(f"{tag}_misc")
    pvb = st.bank(f"{tag}_pv")

    w_in, c_pool, w_step, started = sem("w_in"), sem("c_pool"), sem("w_step"), sem("started")
    mv_ready, rstd_ready, xhat_ready, xn_ready, xhigh, xT_ready = [sem(n) for n in ("mv_ready", "rstd_ready", "xhat_ready", "xn_ready", "xhigh", "xT_ready")]
    misc_full, misc_read = sem("misc_full"), sem("misc_read")
    qk_high = sem("qk_high")
    s_psum, s_free, m_ready, pool_chain = sem("s_psum"), sem("s_free"), sem("m_ready"), sem("pool_chain")
    t_psum, t_free, p_free, o_free = sem("t_psum"), sem("t_free"), sem("p_free"), sem("o_free")
    norm_chain, ss_ready, rr_ready, ctx_ready = sem("norm_chain"), sem("ss_ready"), sem("rr_ready"), sem("ctx_ready")
    chigh, cT_ready, y_done = sem("chigh"), sem("cT_ready"), sem("y_done")
    m_high, ss_mean, stat_step = sem("m_high"), sem("ss_mean"), sem("stat_step")

    QK = [f"QK{k}" for k in range(NTL)]
    free = [(1, 2), (1, 3)] + [(g, j) for g in (2, 3) for j in range(4)]
    at = {(0, 2): "ctxT", (0, 3): "y", (1, 0): "T"} | dict(zip(free, QK + ["V"]))
    before = ["T"] + QK + ["V", "mT"]
    order = []
    for g in range(NQ):
        order += [at[g, j] for j in range(QUAD) if (g, j) in at] + [f"mT{g}"]
    NM, N0 = len(order), len(before)
    lead = {n: k for k, n in enumerate(before)}

    def use(b, name):
        return b * NM + N0 + order.index(name)

    NROOT = 5 if full else 1
    NNORM = 5 if diff else 1

    with nc.Block() as block:
        @block.sync
        def _(sp):
            n = NMAP * DH
            sp.dma_start(raw[:, 0:n], w["wq"]).then_inc(w_in, 16)
            sp.dma_start(raw[:, n:2 * n], w["wk"]).then_inc(w_in, 16)
            sp.dma_start(raw[:, 2 * n:2 * n + VW], w["wv"]).then_inc(w_in, 16)
            sp.dma_start(raw[:, 2 * n + VW:].rearrange("p (c d) -> p c d", d=D), w["wo"].rearrange("(c p) d -> p c d", p=P)).then_inc(w_in, 16)
            if diff:
                for k, name in enumerate(("lambda_q1", "lambda_q2", "lambda_k1", "lambda_k2")):
                    sp.dma_start(lamr[:, k, :], w[name].rearrange("h d -> (h d)").unsqueeze(0).to_broadcast([P, NV * DH])).then_inc(w_in, 16)
                for k in range(P // DV):
                    sp.dma_start(outsc[k * DV:(k + 1) * DV, :], w["rms_scale"].rearrange("(p a) -> p a", a=1)).then_inc(w_in, 16)
            if full:
                sp.dma_start(insc[:, :], w["norm_w"].rearrange("(p a) -> p a", a=1)).then_inc(w_in, 16)

        NWIN = 16 * (4 + (4 + P // DV if diff else 0) + (1 if full else 0))

        @block.gpsimd
        def _(pool):
            pool.memset(epst[:, :], 1e-5)
            pool.memset(half[:, :], -0.5)
            pool.memset(padm[:, :, :, :, :], 0.0)
            pool.memset(epsr[:, :], 1e-6)
            pool.memset(nil[:, :], 0.0)
            pool.memset(inv_dv[:, :], 1.0 / DV)
            pool.memset(eps_dv[:, :], 1e-5)
            pool.memset(rows[:, :, :], -1.0)
            if diff:
                pool.memset(econst[:, :], E_CONST)
            if masked:
                pool.memset(mf[:, :, :], 0.0)
            pool.memset(credit[:, 15:16], 0.0).then_inc(c_pool, 1)
            pool.wait_ge(c_pool, 1)
            for k, (a, z) in enumerate(((DH, 2 * DH), (2 * DH, 3 * DH), (3 * DH, 3 * DH + 2))):
                pool.affine_select(out=rows[:, k, :], in_=rows[:, k, :], compare_op=ALU.is_ge, fill=0.0, base=-a,
                                   pattern=[[-GR, HPT]], channel_multiplier=1).then_inc(c_pool, 1)
            pool.wait_ge(c_pool, 4)
            for k, (a, z) in enumerate(((DH, 2 * DH), (2 * DH, 3 * DH), (3 * DH, 3 * DH + 2))):
                pool.affine_select(out=rows[:, k, :], in_=rows[:, k, :], compare_op=ALU.is_ge, fill=0.0, base=z - 1,
                                   pattern=[[GR, HPT]], channel_multiplier=-1)
            if masked:
                pool.affine_select(out=mf[:, 0, :].rearrange("p (a b) -> p a b", a=2), in_=mf[:, 0, :].rearrange("p (a b) -> p a b", a=2),
                                   compare_op=ALU.is_ge, fill=-BIG, base=0, pattern=[[P, 2], [-1, SEQ]], channel_multiplier=1)
                pool.affine_select(out=mf[:, 1, :].rearrange("p (a b) -> p a b", a=2), in_=mf[:, 1, :].rearrange("p (a b) -> p a b", a=2),
                                   compare_op=ALU.is_ge, fill=-BIG, base=0, pattern=[[-P, 2], [1, SEQ]], channel_multiplier=-1)
            pool.memset(credit[:, 14:15], 0.0).then_inc(c_pool, 1)
            if diff:
                pool.wait_ge(w_step, 4)
                pool.tensor_tensor(lame[:, :], econst[:, :], lams[:, :], ALU.pow).then_inc(c_pool, 1)
            pool.wait_ge(started, 1)

            def root(b):
                pool.wait_ge(mv_ready, b + 1)
                ch = Chain(pool, pool_chain, b * NROOT)
                ch(pool.tensor_tensor(rs2[:, :], mv[:, :, 1], epst[:, 0:mv.shape[1]], ALU.add))
                last = pool.tensor_tensor(rs[:, :], rs2[:, :], half[:, 0:TPS], ALU.pow)
                if full:
                    ch(last)
                    ch(pool.tensor_tensor(rs2[:, :], rs[:, :], rs[:, :], ALU.mult))
                    ch(pool.tensor_tensor(rs3[:, :], rs2[:, :], mv[:, :, 1], ALU.mult))
                    ch(pool.tensor_tensor(rs2[:, :], rs3[:, :], epsr[:, :], ALU.add))
                    last = pool.tensor_tensor(rs3[:, :], rs2[:, :], half[:, 0:TPS], ALU.pow)
                last.then_inc(rstd_ready, 1)

            def maxima(q):
                pool.wait_ge(s_free, 2 + (q + 1) * QUAD)
                pool.tensor_tensor(mh[:, :, :], mx[:, :, :], nil[:, :].rearrange("p (t j) -> p t j", t=TPS), ALU.add).then_inc(m_high, 1)
                pool.wait_ge(m_high, q + 1)
                src = mh[:, :, :].bitcast(F32).rearrange("p q (t r) -> p t q r", r=HPT)
                raw_m = mx[:, :, :].rearrange("p q (t r) -> p t q r", r=HPT)
                pool.tensor_tensor(padm[:, :, :, :, 3 * DH], src, nil[:, :].rearrange("p (t q r) -> p t q r", t=QT, q=TPS), ALU.add)
                pool.tensor_tensor(padm[:, :, :, :, 3 * DH + 1], raw_m, src, ALU.subtract).then_inc(m_ready, 1)

            def head_root(k):
                pool.wait_ge(ss_ready, k + 1)
                pool.tensor_tensor(sm[:, :], ss[:, :], inv_dv[:, :], ALU.mult).then_inc(ss_mean, 1)
                pool.wait_ge(ss_mean, k * 2 + 1)
                pool.tensor_tensor(sm2[:, :], sm[:, :], eps_dv[:, :], ALU.add).then_inc(ss_mean, 1)
                pool.wait_ge(ss_mean, k * 2 + 2)
                pool.tensor_tensor(rr[:, :], sm2[:, :], half[:, 0:TPS * NV], ALU.pow).then_inc(rr_ready, 1)

            root(0)
            maxima(0)
            with pool.Fori(0, NSEQ) as b:
                if diff:
                    head_root(b)
                root(b + 1)
                maxima(b * NQ + 1)
                if full:
                    pool.wait_ge(y_done, b + 1)
                    pool.tensor_tensor(XS[:, b + S0 - 1, :, :], XS[:, b + S0 - 1, :, :], YS[:, b + S0 - 1, :, :], ALU.add)
                for g in range(1, NQ):
                    maxima(b * NQ + g + 1)
            if diff:
                head_root(NSEQ)
            if full:
                pool.wait_ge(y_done, NSEQ + 1)
                pool.tensor_tensor(XS[:, NSEQ + S0 - 1, :, :], XS[:, NSEQ + S0 - 1, :, :], YS[:, NSEQ + S0 - 1, :, :], ALU.add)

        @block.scalar
        def _(act):
            act.wait_ge(started, 1)

            def turned(m):
                act.wait_ge(misc_full, m + 1)
                act.activation(xT[:, :], misc[:, 0:SEQ], ACT.Identity, scale=insc[:, :] if full else 1.0).then_inc(misc_read, 1)

            def high(m, k, nqk):
                act.wait_ge(misc_full, m + 1)
                if k % 2:
                    act.activation(hi2[:, :], misc[:, :], ACT.Identity, bias=colc[:, 2:3]).then_inc(qk_high, 1)
                else:
                    act.activation(hi2[:, :], misc[:, :], ACT.Identity).then_inc(qk_high, 1)

            def values(m, q):
                act.wait_ge(misc_full, m + 1)
                act.activation(V[q][:, :, :, 0:DV], misc[:, 0:TPS * VW].rearrange("p (t h d) -> p t h d", t=TPS, d=DV),
                               ACT.Identity).then_inc(misc_read, 1)

            def exp(hg, r):
                act.wait_ge(t_psum, hg + 1)
                act.wait_ge(p_free, hg + 1)
                act.activation(Pm[r][:, :], tbank[r][:, :], ACT.Exp, scale=SCALE).then_inc(t_free, 1)

            def context(gq, g, r, k):
                act.wait_ge(p_free, 4 + (gq + 1) * QUAD)
                if g == 0:
                    act.wait_ge(ctx_ready, k + 1)
                act.activation(O[:, :, g * QUAD:(g + 1) * QUAD, :],
                               pvb[:, r * 256:r * 256 + TPS * QUAD * OV].rearrange("p (t h d) -> p t h d", t=TPS, d=OV),
                               ACT.Identity).then_inc(o_free, 1)

            def ctx_turned(m):
                act.wait_ge(misc_full, m + 1)
                act.activation(cT[:, :], misc[:, 0:NC * SEQ], ACT.Identity, scale=outsc[:, :] if diff else 1.0).then_inc(misc_read, 1)

            turned(lead["T"])
            for k in range(NTL):
                high(lead[f"QK{k}"], k, k)
            values(lead["V"], 0)
            with act.Fori(0, NSEQ // 2) as i:
                for p in range(2):
                    b = i * 2 + p
                    for g in range(NQ):
                        gq = b * NQ + g
                        for j in range(QUAD):
                            exp(gq * QUAD + j, j)
                            name = at.get((g, j), "")
                            if name == "T":
                                turned(use(b, name))
                            elif name == "ctxT":
                                ctx_turned(use(b, name))
                            elif name == "V":
                                values(use(b, name), 1 - p)
                            elif name.startswith("QK"):
                                high(use(b, name), int(name[2:]), None)
                        context(gq, g, g % RO, b)
            ctx_turned(NSEQ * NM + N0)

        @block.vector
        def _(dve):
            for j, s in enumerate([s_free] * 2 + [t_free] * 4 + [p_free] * 4 + [o_free] * RO):
                dve.memset(credit[:, j:j + 1], 0.0).then_inc(s, 1)
            for k in range(2):
                dve.memset(V[k][:, :, :, DV:OV], 1.0)
            dve.memset(O[:, :, :, :], 1.0)
            if full:
                dve.memset(xhat[:, :, :, :], 0.0)
            for n in range(2):
                for k in range(2):
                    dve.memset(wqk[n][k][:, :].bitcast(F32), 0.0)
            dve.wait_ge(w_in, NWIN)
            dve.wait_ge(c_pool, 5)
            if masked:
                dve.tensor_copy(identb[:, :], ident[:, :])
                dve.tensor_copy(maskS[:, :], mf[:, 0, :])
                dve.tensor_copy(maskT[:, :], mf[:, 1, :])
            dve.tensor_copy(wv[0][:, :], raw[:, 2 * NMAP * DH:2 * NMAP * DH + VW])
            dve.tensor_copy(wo[0][:, :], raw[:, 2 * NMAP * DH + VW:])
            dve.reduce_sum(rvec[:, :], rows[:, :, :], AX).then_inc(w_step, 1)
            dve.wait_ge(w_step, 1)
            for n in range(2):
                src = raw[:, n * NMAP * DH:(n + 1) * NMAP * DH].rearrange("p (h d) -> p h d", d=DH)
                for rep in range(3):
                    last = dve.tensor_copy(wqk[n][0][:, :].rearrange("p (h g) -> p h g", g=GR)[:, :, rep * DH:(rep + 1) * DH], src)
            last.then_inc(w_step, 1)
            dve.wait_ge(w_step, 2)
            for n in range(2):
                src = raw[:, n * NMAP * DH:(n + 1) * NMAP * DH].rearrange("p (h d) -> p h d", d=DH)
                for rep in range(3):
                    sl = (slice(None), slice(None), slice(rep * DH, (rep + 1) * DH))
                    dve.tensor_tensor(wqk[n][1][:, :].rearrange("p (h g) -> p h g", g=GR)[sl], src,
                                      wqk[n][0][:, :].bitcast(F32).rearrange("p (h g) -> p h g", g=GR)[sl], ALU.subtract)
            dve.tensor_tensor(wv[1][:, :], raw[:, 2 * NMAP * DH:2 * NMAP * DH + VW], wv[0][:, :].bitcast(F32), ALU.subtract)
            dve.tensor_tensor(wo[1][:, :], raw[:, 2 * NMAP * DH + VW:], wo[0][:, :].bitcast(F32), ALU.subtract)
            dve.tensor_copy(colc[:, 0:1], rvec[:, 0:1])
            dve.tensor_tensor(colc[:, 1:2], rvec[:, 1:2], rvec[:, 2:3], ALU.subtract)
            dve.tensor_copy(colc[:, 2:3], rvec[:, 2:3])
            if diff:
                dve.tensor_tensor(lamp[:, :, :], lamr[:, 0:2, :], lamr[:, 2:4, :], ALU.mult).then_inc(w_step, 1)
                dve.wait_ge(w_step, 3)
                dve.reduce_sum(lams[:, :], lamp[:, :, :].rearrange("p a (h d) -> p (a h) d", d=DH), AX).then_inc(w_step, 1)
                dve.memset(wmap[:, :, 0:1], 1.0)
                dve.wait_ge(c_pool, 6)
                dve.tensor_tensor(lamp[:, 0, 0:NV], lame[:, NV:2 * NV], lame[:, 0:NV], ALU.subtract).then_inc(w_step, 1)
                dve.wait_ge(w_step, 5)
                dve.tensor_scalar(wmap[:, :, 1], lamp[:, 0, 0:NV], 0.8, None, ALU.subtract)
                dve.tensor_scalar(outsc[:, :], outsc[:, :], 1.0 - 0.8, None, ALU.mult)
            dve.memset(credit[:, 13:14], 0.0).then_inc(started, 1)
            dve.wait_ge(started, 1)

            def stat(b):
                for t in range(TPS):
                    last = dve.bn_stats(stats[:, t, :], XS[:, b + S0, t, :])
                last.then_inc(stat_step, 1)
                dve.wait_ge(stat_step, b + 1)
                dve.memset(spare[:, :], 0.0)
                for t in range(TPS):
                    last = dve.bn_aggr(mv[:, t, :], stats[:, t, :])
                last.then_inc(mv_ready, 1)

            def norm(b, q):
                dve.wait_ge(rstd_ready, b + 1)
                for t in range(TPS):
                    last = dve.tensor_scalar(xhat[:, q, t, :] if full else xn[:, t, :], XS[:, b + S0, t, :], mv[:, t, 0:1], rs[:, t:t + 1], ALU.subtract, ALU.mult)
                if full:
                    last.then_inc(xhat_ready, 1)
                    dve.wait_ge(xhat_ready, b + 1)
                    for t in range(TPS):
                        last = dve.tensor_scalar(xn[:, t, :], xhat[:, q, t, :], rs3[:, t:t + 1], None, ALU.mult)
                last.then_inc(xn_ready, 1)

            def split_x(b, m):
                dve.wait_ge(misc_read, m + 1)
                dve.tensor_copy(xh[:, :], xT[:, :]).then_inc(xhigh, 1)
                dve.wait_ge(xhigh, b + 1)
                dve.tensor_tensor(xl[:, :], xT[:, :], xh[:, :].bitcast(F32), ALU.subtract).then_inc(xT_ready, 1)

            def stack(b, m, k, q):
                dve.wait_ge(qk_high, b * NTL + k + 1)
                n, c = k % 2, slice((k // 2) * 512, (k // 2 + 1) * 512)
                dve.scalar_tensor_tensor((KS if n else Q1)[q][:, c], hi2[:, :].bitcast(F32), colc[:, n:n + 1], misc[:, :], ALU.mult, ALU.add).then_inc(misc_read, 1)

            def top(hg, j):
                dve.wait_ge(s_psum, hg + 1)
                dve.reduce_max(mx[:, :, j], sbank[j % 2][:, :].rearrange("p (t k) -> p t k", t=TPS), AX).then_inc(s_free, 1)

            def with_max(m, g, q):
                dve.wait_ge(misc_full, m + 1)
                c = slice(g * QT * SEQ, (g + 1) * QT * SEQ)
                dve.tensor_tensor(Q2[g % 2][:, :], Q1[q][:, c].bitcast(F32), misc[:, 0:QT * SEQ], ALU.add).then_inc(misc_read, 1)

            def normalise(k):
                ch = Chain(dve, norm_chain, k * NNORM)
                dve.wait_ge(o_free, RO + k * NQ)
                ch(dve.reciprocal(rec[:, :, :], O[:, :, :, DV]))
                if not diff:
                    dve.tensor_tensor(ctx[:, :, :].rearrange("p t (h d) -> p t h d", d=DV), O[:, :, :, 0:DV],
                                      rec[:, :, :].unsqueeze(3).to_broadcast([P, TPS, NMAP, DV]), ALU.mult).then_inc(ctx_ready, 1)
                    return
                ch(dve.tensor_tensor(rec[:, :, :], rec[:, :, :], wmap[:, :, :].rearrange("p h s -> p (h s)").unsqueeze(1).to_broadcast([P, TPS, NMAP]), ALU.mult))
                ch(dve.tensor_tensor(T2[:, :, :, :], O[:, :, :, 0:DV], rec[:, :, :].unsqueeze(3).to_broadcast([P, TPS, NMAP, DV]), ALU.mult))
                tv = T2[:, :, :, :].rearrange("p t (h s) d -> p (t h) s d", s=2)
                dv_ = Dd[:, :, :, :].rearrange("p t h d -> p (t h) d")
                ch(dve.tensor_tensor(dv_, tv[:, :, 0, :], tv[:, :, 1, :], ALU.add))
                ch(dve.tensor_tensor(T2[:, 0, :, :], dv_, dv_, ALU.mult))
                dve.reduce_sum(ss[:, :], T2[:, 0, :, :], AX).then_inc(ss_ready, 1)

            def normalise2(k):
                if diff:
                    dve.wait_ge(rr_ready, k + 1)
                    dve.tensor_tensor(ctx[:, :, :].rearrange("p t (h d) -> p (t h) d", d=DV), Dd[:, :, :, :].rearrange("p t h d -> p (t h) d"),
                                      rr[:, :].unsqueeze(2).to_broadcast([P, TPS * NV, DV]), ALU.mult).then_inc(ctx_ready, 1)

            def split_ctx(k, m):
                dve.wait_ge(misc_read, m + 1)
                dve.tensor_copy(cTh[:, :], cT[:, :]).then_inc(chigh, 1)
                dve.wait_ge(chigh, k + 1)
                dve.tensor_tensor(cTl[:, :], cT[:, :], cTh[:, :].bitcast(F32), ALU.subtract).then_inc(cT_ready, 1)

            def add_y(k, m, q):
                dve.wait_ge(misc_full, m + 1)
                y = misc[:, 0:SEQ].rearrange("p (t d) -> p t d", d=D)
                if full:
                    dve.tensor_tensor(YS[:, k + S0 - 1, :, :], y, xhat[:, q, :, :], ALU.add).then_inc(misc_read, 1)
                    dve.wait_ge(misc_read, m + 1)
                    dve.memset(credit[:, 12:13], 0.0).then_inc(y_done, 1)
                else:
                    dve.tensor_tensor(XS[:, k + S0 - 1, :, :], XS[:, k + S0 - 1, :, :], y, ALU.add).then_inc(misc_read, 1)

            stat(0)
            norm(0, 0)
            split_x(0, lead["T"])
            for k in range(NTL):
                stack(0, lead[f"QK{k}"], k, 0)
            for j in range(QUAD):
                top(j, j)
            with_max(lead["mT"], 0, 0)
            with dve.Fori(0, NSEQ // 2) as i:
                for p in range(2):
                    b = i * 2 + p
                    for g in range(NQ):
                        gq = b * NQ + g
                        for j in range(QUAD):
                            top((gq + 1) * QUAD + j, j)
                            name = at.get((g, j), "")
                            if (g, j) == (0, 0):
                                normalise(b)
                            elif (g, j) == (0, 1):
                                normalise2(b)
                                stat(b + 1)
                            elif name == "ctxT":
                                split_ctx(b, use(b, name))
                            elif name == "y":
                                add_y(b, use(b, name), 1 - p)
                                norm(b + 1, 1 - p)
                            elif (g, j) == (1, 1):
                                split_x(b + 1, use(b, "T"))
                            elif name.startswith("QK"):
                                stack(b + 1, use(b, name), int(name[2:]), 1 - p)
                        with_max(use(b, f"mT{g}"), (g + 1) % NQ, p if g < NQ - 1 else 1 - p)
            normalise(NSEQ)
            normalise2(NSEQ)
            split_ctx(NSEQ, NSEQ * NM + N0)
            add_y(NSEQ, NSEQ * NM + N0 + 1, 1)

        @block.tensor
        def _(pe):
            pe.wait_ge(started, 1)

            def product(out, pairs):
                for k, (sh, sl, mh_, ml) in enumerate(pairs):
                    pe.matmul(out, sh, mh_, start=k == 0, stop=False)
                    pe.matmul(out, sh, ml, start=False, stop=False)
                    ins = pe.matmul(out, sl, mh_, start=False, stop=k == len(pairs) - 1)
                return ins

            def free_bank(m):
                pe.wait_ge(misc_read, m)

            def turn(b, m):
                free_bank(m)
                pe.wait_ge(xn_ready, b + 1)
                for t in range(TPS):
                    last = pe.transpose(misc[:, t * P:(t + 1) * P], xn[:, t, :], ident[:, :])
                last.then_inc(misc_full, 1)

            def project(b, m, k):
                free_bank(m)
                pe.wait_ge(xT_ready, b + 1)
                n = k % 2
                for r in range(2):
                    c = slice((k // 2 * 2 + r) * P, (k // 2 * 2 + r + 1) * P)
                    last = product(misc[:, r * SEQ:(r + 1) * SEQ], [(wqk[n][0][:, c], wqk[n][1][:, c], xh[:, :], xl[:, :])])
                last.then_inc(misc_full, 1)

            def values(b, m):
                free_bank(m)
                for t in range(TPS):
                    c = slice(t * P, (t + 1) * P)
                    last = product(misc[:, t * VW:(t + 1) * VW], [(xh[:, c], xl[:, c], wv[0][:, :], wv[1][:, :])])
                last.then_inc(misc_full, 1)

            def rows_of(j):
                r0 = (j % HPT) * GR
                return slice(r0, r0 + KR)

            def score(hg, g, j, q):
                pe.wait_ge(s_free, hg + 1)
                o, r = sbank[j % 2], rows_of(j)
                c0 = (g * QT + j // HPT) * SEQ
                if masked:
                    pe.matmul(o[:, :], identb[:, :], maskS[:, :], start=True, stop=True)
                for t in range(TPS):
                    nk = P if masked and t == 0 else SEQ
                    last = pe.matmul(o[:, t * SEQ:t * SEQ + nk], Q1[q][r, c0 + t * P:c0 + (t + 1) * P], KS[q][r, c0:c0 + nk],
                                     start=not masked, stop=True, skip_group_check=masked)
                last.then_inc(s_psum, 1)

            def score_t(hg, g, j, q):
                pe.wait_ge(t_free, hg + 1)
                o, r = tbank[j], rows_of(j)
                c0 = (g * QT + j // HPT) * SEQ
                c2 = (j // HPT) * SEQ
                if masked:
                    pe.matmul(o[:, :], identb[:, :], maskT[:, :], start=True, stop=True)
                for t in range(TPS):
                    q0 = P if masked and t == 1 else 0
                    last = pe.matmul(o[:, t * SEQ + q0:(t + 1) * SEQ], KS[q][r, c0 + t * P:c0 + (t + 1) * P], Q2[g % 2][r, c2 + q0:c2 + SEQ],
                                     start=not masked, stop=True, skip_group_check=masked)
                last.then_inc(t_psum, 1)

            def weigh(hg, gq, g, j, q):
                pe.wait_ge(t_free, hg + 1 + 4)
                if j == 0:
                    pe.wait_ge(o_free, gq + 1)
                h = (g * QUAD + j) // (2 if diff else 1)
                for t in range(TPS):
                    o0 = (g % RO) * 256 + (t * QUAD + j) * OV
                    nk = 1 if masked and t == 0 else TPS
                    for s in range(nk):
                        last = pe.matmul(pvb[:, o0:o0 + OV], Pm[j][:, s * SEQ + t * P:s * SEQ + (t + 1) * P], V[q][:, s, h, :],
                                         start=s == 0, stop=s == nk - 1)
                last.then_inc(p_free, 1)

            def turn_max(q, m):
                free_bank(m)
                pe.wait_ge(m_ready, q + 1)
                for u in range(QT):
                    for t in range(TPS):
                        c = (u * TPS + t) * P
                        last = pe.transpose(misc[:, c:c + P], padm[:, u, t, :, :].rearrange("p r g -> p (r g)"), ident[:, :])
                last.then_inc(misc_full, 1)

            def turn_ctx(k, m):
                free_bank(m)
                pe.wait_ge(ctx_ready, k + 1)
                for c in range(NC):
                    for t in range(TPS):
                        last = pe.transpose(misc[:, (c * TPS + t) * P:(c * TPS + t + 1) * P], ctx[:, t, c * P:(c + 1) * P], ident[:, :])
                last.then_inc(misc_full, 1)

            def project_out(k, m):
                free_bank(m)
                pe.wait_ge(cT_ready, k + 1)
                for t in range(TPS):
                    last = product(misc[:, t * D:(t + 1) * D],
                                   [(cTh[:, c * SEQ + t * P:c * SEQ + (t + 1) * P], cTl[:, c * SEQ + t * P:c * SEQ + (t + 1) * P],
                                     wo[0][:, c * D:(c + 1) * D], wo[1][:, c * D:(c + 1) * D]) for c in range(NC)])
                last.then_inc(misc_full, 1)

            turn(0, lead["T"])
            for k in range(NTL):
                project(0, lead[f"QK{k}"], k)
            values(0, lead["V"])
            pe.wait_ge(misc_read, lead["V"])
            for j in range(QUAD):
                score(j, 0, j, 0)
            turn_max(0, lead["mT"])
            with pe.Fori(0, NSEQ // 2) as i:
                for p in range(2):
                    b = i * 2 + p
                    for g in range(NQ):
                        gq = b * NQ + g
                        pe.wait_ge(misc_read, use(b, f"mT{g - 1}") + 1 if g else b * NM + N0)
                        for j in range(QUAD):
                            score((gq + 1) * QUAD + j, (g + 1) % NQ, j, p if g < NQ - 1 else 1 - p)
                            score_t(gq * QUAD + j, g, j, p)
                            name = at.get((g, j), "")
                            if name == "ctxT":
                                turn_ctx(b, use(b, name))
                            elif name == "y":
                                project_out(b, use(b, name))
                            elif name == "T":
                                turn(b + 1, use(b, name))
                            elif name == "V":
                                values(b + 1, use(b, name))
                            elif name.startswith("QK"):
                                project(b + 1, use(b, name), int(name[2:]))
                        for j in range(QUAD):
                            if j == 2:
                                turn_max(gq + 1, use(b, f"mT{g}"))
                            weigh(gq * QUAD + j, gq, g, j, p)
            turn_ctx(NSEQ, NSEQ * NM + N0)
            project_out(NSEQ, NSEQ * NM + N0 + 1)
    st.close()


def attn_args(kind, a):
    if kind == "diff":
        return {k: a["L0_attn_a_" + n] for k, n in (("wq", "W_q"), ("wk", "W_k"), ("wv", "W_v"), ("wo", "W_o"), ("rms_scale", "rms_scale"),
                                                    ("lambda_q1", "lambda_q1"), ("lambda_k1", "lambda_k1"), ("lambda_q2", "lambda_q2"), ("lambda_k2", "lambda_k2"))}
    if kind == "causal":
        return {k: a["L0_attn_b_" + n] for k, n in (("wq", "Wq"), ("wk", "Wk"), ("wv", "Wv"), ("wo", "Wo"))}
    return {k: a["L1_ffn_" + n] for k, n in (("wq", "wq"), ("wk", "wk"), ("wv", "wv"), ("wo", "wo"), ("norm_w", "norm1_w"))}


def single_head_stage(nc, tag, G, w):
    X, ident = G["X"], G["ident"]
    XS = X[:, :, :].rearrange("p (s t) d -> p s t d", t=TPS)
    S0 = PAD // TPS
    SCALE = float(D) ** -0.5
    st = Stage(nc)
    sb, sem = (lambda n, s, d=F32: st.sb(f"{tag}_{n}", s, d)), (lambda n: st.sem(f"{tag}_{n}"))
    spare = sb("spare", [P, 1])
    epst = sb("epst", [P, 4])
    stats, mv, rs, rs2 = sb("stats", [P, TPS, 6]), sb("mv", [P, TPS, 2]), sb("rs", [P, TPS]), sb("rs2", [P, TPS])
    half = sb("half", [P, TPS])
    xn, xT = sb("xn", [P, TPS, D]), sb("xT", [P, SEQ])
    wq, wk, wv = sb("wq", [D, D]), sb("wk", [D, D]), sb("wv", [D, D])
    bq, bk, bv = sb("bq", [D, 1]), sb("bk", [D, 1]), sb("bv", [P, D])
    QT, KT, V = [sb(f"QT{k}", [P, SEQ]) for k in range(2)], [sb(f"KT{k}", [P, SEQ]) for k in range(2)], [sb(f"V{k}", [P, TPS, D]) for k in range(2)]
    m, nm, rsum, rinv = sb("m", [P, TPS]), sb("nm", [P, TPS]), sb("rsum", [P, TPS]), sb("rinv", [P, TPS])
    Pm, PT = sb("Pm", [P, TPS, SEQ]), sb("PT", [P, TPS, SEQ])
    xb, qkb, vb, scb, ptb, ob = [st.bank(f"{tag}_{n}") for n in ("xb", "qkb", "vb", "scb", "ptb", "ob")]
    w_in, half_set, stat_step, mv_ready, var_ready, rstd_ready, xn_ready = [sem(n) for n in ("w_in", "half_set", "stat_step", "mv_ready", "var_ready", "rstd_ready", "xn_ready")]
    xT_psum, xT_ready, qk_psum, qk_ready, v_psum, v_ready = [sem(n) for n in ("xT_psum", "xT_ready", "qk_psum", "qk_ready", "v_psum", "v_ready")]
    s_psum, m_ready, nm_ready, p_ready, pT_psum, pT_ready, rinv_ready, o_psum, x_done = [sem(n) for n in ("s_psum", "m_ready", "nm_ready", "p_ready", "pT_psum", "pT_ready", "rinv_ready", "o_psum", "x_done")]

    with nc.Block() as block:
        @block.sync
        def _(sp):
            for dst, src in ((wq, w["Wq"]), (wk, w["Wk"]), (wv, w["Wv"])):
                sp.dma_start(dst[:, :], src).then_inc(w_in, 16)
            sp.dma_start(bq[:, :], w["bq"].rearrange("(p a) -> p a", a=1)).then_inc(w_in, 16)
            sp.dma_start(bk[:, :], w["bk"].rearrange("(p a) -> p a", a=1)).then_inc(w_in, 16)
            sp.dma_start(bv[:, :], w["bv"].unsqueeze(0).to_broadcast([P, D])).then_inc(w_in, 16)

        @block.gpsimd
        def _(pool):
            pool.memset(epst[:, :], 1e-5)
            pool.memset(half[:, :], -0.5).then_inc(half_set, 1)
            pool.wait_ge(half_set, 1)

            def root(b):
                pool.wait_ge(mv_ready, b + 1)
                pool.tensor_tensor(rs2[:, :], mv[:, :, 1], epst[:, 0:mv.shape[1]], ALU.add).then_inc(var_ready, 1)
                pool.wait_ge(var_ready, b + 1)
                pool.tensor_tensor(rs[:, :], rs2[:, :], half[:, :], ALU.pow).then_inc(rstd_ready, 1)

            root(0)
            root(1)
            with pool.Fori(0, NSEQ) as b:
                root(b + 2)

        @block.scalar
        def _(act):
            act.wait_ge(w_in, 96)

            def turned(b):
                act.wait_ge(xT_psum, b + 1)
                act.activation(xT[:, :], xb[:, 0:SEQ], ACT.Identity).then_inc(xT_ready, 1)

            def queries_keys(b, q):
                act.wait_ge(qk_psum, b + 1)
                act.activation(QT[q][:, :], qkb[:, 0:SEQ], ACT.Identity, bias=bq[:, :])
                act.activation(KT[q][:, :], qkb[:, SEQ:2 * SEQ], ACT.Identity, bias=bk[:, :]).then_inc(qk_ready, 1)

            turned(0)
            queries_keys(0, 0)
            with act.Fori(0, NSEQ // 2) as i:
                for p in range(2):
                    b = i * 2 + p
                    turned(b + 1)
                    act.wait_ge(nm_ready, b + 1)
                    for t in range(TPS):
                        last = act.activation(Pm[:, t, :], scb[:, t * SEQ:(t + 1) * SEQ], ACT.Exp, bias=nm[:, t:t + 1],
                                              scale=SCALE, accum_out=rsum[:, t:t + 1])
                    last.then_inc(p_ready, 1)
                    queries_keys(b + 1, 1 - p)
                    act.wait_ge(pT_psum, b + 1)
                    act.activation(PT[:, :, :].rearrange("p k q -> p (k q)"), ptb[:, :], ACT.Identity).then_inc(pT_ready, 1)

        @block.vector
        def _(dve):
            dve.memset(spare[:, :], 0.0).then_inc(x_done, 1)
            dve.wait_ge(w_in, 96)

            def norm(b):
                for t in range(TPS):
                    last = dve.bn_stats(stats[:, t, :], XS[:, b + S0, t, :])
                last.then_inc(stat_step, 1)
                dve.wait_ge(stat_step, b + 1)
                dve.memset(spare[:, :], 0.0)
                for t in range(TPS):
                    last = dve.bn_aggr(mv[:, t, :], stats[:, t, :])
                last.then_inc(mv_ready, 1)

            def norm2(b):
                dve.wait_ge(rstd_ready, b + 1)
                for t in range(TPS):
                    last = dve.tensor_scalar(xn[:, t, :], XS[:, b + S0, t, :], mv[:, t, 0:1], rs[:, t:t + 1], ALU.subtract, ALU.mult)
                last.then_inc(xn_ready, 1)

            def values(b, q):
                dve.wait_ge(v_psum, b + 1)
                dve.tensor_tensor(V[q][:, :, :], vb[:, 0:SEQ].rearrange("p (t d) -> p t d", d=D),
                                  bv[:, :].unsqueeze(1).to_broadcast([P, TPS, D]), ALU.add).then_inc(v_ready, 1)

            norm(0)
            norm2(0)
            values(0, 0)
            norm(1)
            norm2(1)
            with dve.Fori(0, NSEQ // 2) as i:
                for p in range(2):
                    b = i * 2 + p
                    dve.wait_ge(s_psum, b + 1)
                    dve.reduce_max(m[:, :], scb[:, :].rearrange("p (t k) -> p t k", t=TPS), AX).then_inc(m_ready, 1)
                    dve.wait_ge(m_ready, b + 1)
                    dve.tensor_scalar(nm[:, :], m[:, :], -SCALE, None, ALU.mult).then_inc(nm_ready, 1)
                    values(b + 1, 1 - p)
                    norm(b + 2)
                    dve.wait_ge(p_ready, b + 1)
                    dve.reciprocal(rinv[:, :], rsum[:, :]).then_inc(rinv_ready, 1)
                    norm2(b + 2)
                    dve.wait_ge(rinv_ready, b + 1)
                    dve.wait_ge(o_psum, b + 1)
                    for t in range(TPS):
                        last = dve.scalar_tensor_tensor(XS[:, b + S0, t, :], ob[:, t * D:(t + 1) * D], rinv[:, t:t + 1], XS[:, b + S0, t, :], ALU.mult, ALU.add)
                    last.then_inc(x_done, 1)

        @block.tensor
        def _(pe):
            pe.wait_ge(w_in, 96)

            def turn(b):
                pe.wait_ge(xn_ready, b + 1)
                for t in range(TPS):
                    last = pe.transpose(xb[:, t * P:(t + 1) * P], xn[:, t, :], ident[:, :])
                last.then_inc(xT_psum, 1)

            def project(b):
                pe.wait_ge(xT_ready, b + 1)
                pe.matmul(qkb[:, 0:SEQ], wq[:, :], xT[:, :], start=True, stop=True)
                pe.matmul(qkb[:, SEQ:], wk[:, :], xT[:, :], start=True, stop=True).then_inc(qk_psum, 1)
                for t in range(TPS):
                    last = pe.matmul(vb[:, t * D:(t + 1) * D], xT[:, t * P:(t + 1) * P], wv[:, :], start=True, stop=True)
                last.then_inc(v_psum, 1)

            turn(0)
            project(0)
            with pe.Fori(0, NSEQ // 2) as i:
                for p in range(2):
                    b = i * 2 + p
                    pe.wait_ge(qk_ready, b + 1)
                    for t in range(TPS):
                        last = pe.matmul(scb[:, t * SEQ:(t + 1) * SEQ], QT[p][:, t * P:(t + 1) * P], KT[p][:, :], start=True, stop=True)
                    last.then_inc(s_psum, 1)
                    turn(b + 1)
                    pe.wait_ge(v_ready, b + 1)
                    project(b + 1)
                    pe.wait_ge(p_ready, b + 1)
                    for s in range(TPS):
                        for t in range(TPS):
                            last = pe.transpose(ptb[:, s * SEQ + t * P:s * SEQ + (t + 1) * P], Pm[:, t, s * P:(s + 1) * P], ident[:, :])
                    last.then_inc(pT_psum, 1)
                    pe.wait_ge(pT_ready, b + 1)
                    pe.wait_ge(x_done, b + 1)
                    for t in range(TPS):
                        for s in range(TPS):
                            last = pe.matmul(ob[:, t * D:(t + 1) * D], PT[:, s, t * P:(t + 1) * P], V[p][:, s, :], start=s == 0, stop=s == TPS - 1)
                    last.then_inc(o_psum, 1)
    st.close()


HID = 192
HC = HID // 2
CONV = 4


def recurrence_in_stage(nc, tag, G, w):
    X, Y, ident, GT, VT = G["X"], G["Y"], G["ident"], G["GT"], G["VT"]
    XB = X[:, :, :].rearrange("p (b t) d -> p b t d", t=TPB)
    YB = Y[:, :, :].rearrange("p (b t) d -> p b t d", t=TPB)
    GB = GT[:, :, :].rearrange("p c (b t) -> p b c t", t=BLK)
    VB = VT[:, :, :, :].rearrange("p c (b s) t -> p b c s t", s=2)
    st = Stage(nc)
    sb, sem = (lambda n, s, d=F32: st.sb(f"{tag}_{n}", s, d)), (lambda n: st.sem(f"{tag}_{n}"))
    spare, credit = sb("spare", [P, 1]), sb("credit", [P, 2])
    epst = sb("epst", [P, 4])
    stats, mv, half = sb("stats", [P, TPB, 6]), sb("mv", [P, TPB, 2]), sb("half", [P, TPB])
    rs, r2, r3, rq = [sb(n, [P, TPB]) for n in ("rs", "r2", "r3", "rq")]
    xn, xT = sb("xn", [P, TPB, D]), sb("xT", [P, BLK])
    win, g1 = sb("win", [D, 4 * HC]), sb("g1", [P, 1])
    xb = st.bank(f"{tag}_xb")
    ub = [st.bank(f"{tag}_u{k}") for k in range(4)]
    w_in, half_set, stat_step, mv_ready, pool_chain, rstd_ready, y_ready, xn_ready = [sem(n) for n in ("w_in", "half_set", "stat_step", "mv_ready", "pool_chain", "rstd_ready", "y_ready", "xn_ready")]
    xT_psum, xT_ready, gate_psum, gate_done, v_psum, v_done, zero_set = [sem(n) for n in ("xT_psum", "xT_ready", "gate_psum", "gate_done", "v_psum", "v_done", "zero_set")]

    with nc.Block() as block:
        @block.sync
        def _(sp):
            sp.dma_start(win[:, :], w["W_in"]).then_inc(w_in, 16)
            sp.dma_start(g1[:, :], w["gamma1"].rearrange("(p a) -> p a", a=1)).then_inc(w_in, 16)

        @block.gpsimd
        def _(pool):
            pool.memset(VT[:, :, :, 0:CONV - 1], 0.0)
            pool.memset(epst[:, :], 1e-5)
            pool.memset(half[:, :], -0.5).then_inc(half_set, 1)
            pool.wait_ge(half_set, 1)

            def root(b):
                pool.wait_ge(mv_ready, b + 1)
                ch = Chain(pool, pool_chain, b * 4)
                ch(pool.tensor_tensor(r2[:, :], mv[:, :, 1], epst[:, 0:mv.shape[1]], ALU.add))
                ch(pool.tensor_tensor(rs[:, :], r2[:, :], half[:, :], ALU.pow))
                ch(pool.tensor_tensor(r3[:, :], rs[:, :], rs[:, :], ALU.mult))
                ch(pool.tensor_tensor(r2[:, :], r3[:, :], mv[:, :, 1], ALU.mult))
                pool.tensor_tensor(rq[:, :], r2[:, :], half[:, :], ALU.pow).then_inc(rstd_ready, 1)

            root(0)
            with pool.Fori(1, NBLK) as b:
                root(b)

        @block.scalar
        def _(act):
            act.wait_ge(w_in, 32)

            def turned(b):
                act.wait_ge(xT_psum, b + 1)
                act.activation(xT[:, :], xb[:, :], ACT.Identity, scale=g1[:, :]).then_inc(xT_ready, 1)

            with act.Fori(0, NBLK) as b:
                turned(b)
                act.wait_ge(gate_psum, b + 1)
                for c in range(2):
                    last = act.activation(GB[:, b, c, :], ub[c][0:HC, :], ACT.Gelu)
                last.then_inc(gate_done, 1)

        @block.vector
        def _(dve):
            def stat(b):
                for t in range(TPB):
                    last = dve.bn_stats(stats[:, t, :], XB[:, b + 1, t, :])
                last.then_inc(stat_step, 1)
                dve.wait_ge(stat_step, b + 1)
                dve.memset(spare[:, :], 0.0)
                for t in range(TPB):
                    last = dve.bn_aggr(mv[:, t, :], stats[:, t, :])
                last.then_inc(mv_ready, 1)

            def norm(b):
                dve.wait_ge(rstd_ready, b + 1)
                for t in range(TPB):
                    last = dve.tensor_scalar(YB[:, b + 1, t, :], XB[:, b + 1, t, :], mv[:, t, 0:1], rs[:, t:t + 1], ALU.subtract, ALU.mult)
                last.then_inc(y_ready, 1)
                dve.wait_ge(y_ready, b + 1)
                for t in range(TPB):
                    last = dve.tensor_scalar(xn[:, t, :], YB[:, b + 1, t, :], rq[:, t:t + 1], None, ALU.mult)
                last.then_inc(xn_ready, 1)

            def take(b):
                dve.wait_ge(v_psum, b + 1)
                for c in range(2):
                    last = dve.tensor_copy(VB[:, b, c, :, CONV - 1:], ub[2 + c][0:HC, :].rearrange("p (s t) -> p s t", s=2))
                last.then_inc(v_done, 1)

            for k, s in enumerate((gate_done, v_done)):
                dve.memset(credit[:, k:k + 1], 0.0).then_inc(s, 1)
            stat(0)
            norm(0)
            with dve.Fori(1, NBLK) as b:
                stat(b)
                dve.wait_ge(xT_psum, b)
                norm(b)
                take(b - 1)
            take(NBLK - 1)

        @block.tensor
        def _(pe):
            pe.wait_ge(w_in, 32)

            with pe.Fori(0, NBLK) as b:
                pe.wait_ge(xn_ready, b + 1)
                for t in range(TPB):
                    last = pe.transpose(xb[:, t * P:(t + 1) * P], xn[:, t, :], ident[:, :])
                last.then_inc(xT_psum, 1)
                pe.wait_ge(xT_ready, b + 1)
                pe.wait_ge(gate_done, b + 1)
                pe.wait_ge(v_done, b + 1)
                for k in range(4):
                    last = pe.matmul(ub[k][0:HC, :], win[:, k * HC:(k + 1) * HC], xT[:, :], start=True, stop=True)
                    if k % 2:
                        last.then_inc((gate_psum, v_psum)[k // 2], 1)
    st.close()


def recurrence_stage(nc, tag, G, w):
    Y, GT, VT = G["Y"], G["GT"], G["VT"]
    YB = Y[:, :, :].rearrange("p (b t) d -> p b t d", t=TPB)
    GB = GT[:, :, :].rearrange("p c (b t) -> p b c t", t=BLK)
    VB = VT[:, :, :, :].rearrange("p c (b s) t -> p b c s t", s=2)
    st = Stage(nc)
    sb, sem = (lambda n, s, d=F32: st.sb(f"{tag}_{n}", s, d)), (lambda n: st.sem(f"{tag}_{n}"))
    wg, wout = sb("wg", [HC, 2, 4 * HC]), sb("wout", [HC, 2, D])
    cw, cb, bg, fb = sb("cw", [HC, 2, CONV]), sb("cb", [HC, 2]), sb("bg", [HC, 4]), sb("fb", [HC, 2])
    nbg, sp_, ca, eps = sb("nbg", [HC, 4]), sb("sp", [HC, 4]), sb("ca", [HC, 2]), sb("eps", [HC, 2])
    vc = [sb(f"vc{k}", [HC, 2, BLK]) for k in range(2)]
    credit = sb("credit", [HC, 6])
    eps2 = sb("eps2", [HC, 1])
    ex, al, be, t1, xg, hh = [sb(n, [HC, 4 if n == "ex" else 2, BLK]) for n in ("ex", "al", "be", "t1", "xg", "hh")]
    gb = [st.bank(f"{tag}_g{k}") for k in range(4)]
    yb = st.bank(f"{tag}_y")
    w_in, prep, vc_step, vc_ready, g_psum, ex_ready, sg_step, sg_ready = [sem(n) for n in ("w_in", "prep", "vc_step", "vc_ready", "g_psum", "ex_ready", "sg_step", "sg_ready")]
    al_ready, one_ready, be_step, be_ready, xi_ready, xg_ready, h_ready, gh_ready, y_psum, y_done = [sem(n) for n in ("al_ready", "one_ready", "be_step", "be_ready", "xi_ready", "xg_ready", "h_ready", "gh_ready", "y_psum", "y_done")]

    with nc.Block() as block:
        @block.sync
        def _(sp):
            sp.dma_start(wg[:, :, :], w["W_gates"].rearrange("(c p) g -> p c g", p=HC)).then_inc(w_in, 16)
            sp.dma_start(wout[:, :, :], w["W_out"].rearrange("(c p) d -> p c d", p=HC)).then_inc(w_in, 16)
            sp.dma_start(cw[:, :, :], w["conv_w"].rearrange("(c p) a k -> p c (a k)", p=HC)).then_inc(w_in, 16)
            for dst, src in ((cb, "conv_b"), (bg, "b_gates"), (fb, "forget_base")):
                sp.dma_start(dst[:, :], w[src].rearrange("(c p) -> p c", p=HC), allow_slow_non_contiguous=True).then_inc(w_in, 16)

        @block.gpsimd
        def _(pool):
            with pool.Fori(0, NBLK) as b:
                pool.wait_ge(sg_ready, b + 1)
                pool.tensor_tensor(xg[:, :, :], ex[:, 2:4, :], vc[0][:, :, :], ALU.mult).then_inc(xi_ready, 1)

        @block.scalar
        def _(act):
            act.wait_ge(prep, 1)
            act.activation(sp_[:, 0:2], fb[:, :], ACT.Abs).then_inc(prep, 1)
            act.wait_ge(prep, 2)
            act.activation(sp_[:, 2:4], sp_[:, 0:2], ACT.Exp, scale=-1.0).then_inc(prep, 1)
            act.wait_ge(prep, 3)
            act.activation(sp_[:, 0:2], sp_[:, 2:4], ACT.Ln, bias=eps[:, 1:2]).then_inc(prep, 1)
            with act.Fori(0, NBLK) as b:
                act.wait_ge(g_psum, b + 1)
                act.wait_ge(xi_ready, b + 1)
                act.wait_ge(al_ready, b * 2 + 1)
                for k in range(4):
                    last = act.activation(ex[:, k, :], gb[k][0:HC, :], ACT.Exp, scale=-1.0, bias=nbg[:, k:k + 1])
                last.then_inc(ex_ready, 1)
                act.wait_ge(sg_ready, b + 1)
                act.wait_ge(h_ready, b + 1)
                for c in range(2):
                    last = act.activation(al[:, c, :], ex[:, c, :], ACT.Exp, scale=ca[:, c:c + 1])
                last.then_inc(al_ready, 1)
                act.wait_ge(al_ready, b * 2 + 2)
                act.activation(t1[:, :, :], al[:, :, :], ACT.Square).then_inc(al_ready, 1)
                act.wait_ge(one_ready, b + 1)
                act.activation(be[:, :, :], t1[:, :, :], ACT.Ln, bias=eps[:, 0:1]).then_inc(be_step, 1)
                act.wait_ge(be_step, b + 1)
                act.activation(t1[:, :, :], be[:, :, :], ACT.Exp, scale=0.5).then_inc(be_ready, 1)

        @block.vector
        def _(dve):
            for k, s in enumerate((xi_ready, h_ready, ex_ready, y_psum, y_done, al_ready)):
                dve.memset(credit[:, k:k + 1], 0.0).then_inc(s, 1)
            dve.memset(eps[:, 0:1], 1e-6)
            dve.memset(eps[:, 1:2], 1.0)
            dve.wait_ge(w_in, 96)
            dve.tensor_scalar(nbg[:, :], bg[:, :], -1.0, None, ALU.mult).then_inc(prep, 1)
            dve.wait_ge(prep, 4)
            dve.tensor_scalar(ca[:, :], fb[:, :], 0.0, None, ALU.max).then_inc(vc_step, 1)
            dve.wait_ge(vc_step, 1)
            dve.tensor_tensor(ca[:, :], ca[:, :], sp_[:, 0:2], ALU.add).then_inc(vc_step, 1)
            dve.wait_ge(vc_step, 2)
            dve.tensor_scalar(ca[:, :], ca[:, :], -8.0, None, ALU.mult).then_inc(vc_step, 1)
            dve.wait_ge(vc_step, 3)

            def conv(b):
                ch = Chain(dve, vc_step, b * 4 + 3)
                out = vc[1][:, :, :].rearrange("p c (s t) -> p c s t", s=2)
                for c in range(2):
                    last = dve.tensor_scalar(out[:, c, :, :], VB[:, b, c, :, 0:SEQ], cw[:, c, 0:1], cb[:, c:c + 1], ALU.mult, ALU.add)
                ch(last)
                for k in range(1, CONV):
                    dst = (vc[0] if k == CONV - 1 else vc[1])[:, :, :].rearrange("p c (s t) -> p c s t", s=2)
                    for c in range(2):
                        last = dve.scalar_tensor_tensor(dst[:, c, :, :], VB[:, b, c, :, k:k + SEQ], cw[:, c, k:k + 1], out[:, c, :, :], ALU.mult, ALU.add)
                    ch(last)
                dve.tensor_copy(eps2[:, 0:1], eps[:, 0:1]).then_inc(vc_ready, 1)

            with dve.Fori(0, NBLK) as b:
                dve.wait_ge(xi_ready, b + 1)
                conv(b)
                dve.wait_ge(ex_ready, b + 2)
                dve.tensor_scalar(ex[:, :, :], ex[:, :, :], 1.0, None, ALU.add).then_inc(sg_step, 1)
                dve.wait_ge(sg_step, b + 1)
                dve.reciprocal(ex[:, :, :], ex[:, :, :]).then_inc(sg_ready, 1)
                dve.wait_ge(al_ready, b * 2 + 3)
                dve.tensor_scalar(t1[:, :, :], t1[:, :, :], -1.0, 1.0, ALU.mult, ALU.add).then_inc(one_ready, 1)
                dve.wait_ge(be_ready, b + 1)
                dve.wait_ge(xi_ready, b + 2)
                dve.tensor_tensor(xg[:, :, :], xg[:, :, :], t1[:, :, :], ALU.mult).then_inc(xg_ready, 1)
                dve.wait_ge(xg_ready, b + 1)
                dve.wait_ge(y_psum, b + 1)
                for c in range(2):
                    for s in range(2):
                        cols = slice(s * SEQ, (s + 1) * SEQ)
                        last = dve.tensor_tensor_scan(hh[:, c, cols], al[:, c, cols], xg[:, c, cols], 0.0, ALU.mult, ALU.add)
                last.then_inc(h_ready, 1)
                dve.wait_ge(h_ready, b + 2)
                dve.tensor_tensor(hh[:, :, :], hh[:, :, :], GB[:, b, :, :], ALU.mult).then_inc(gh_ready, 1)
                dve.wait_ge(y_psum, b + 2)
                dve.tensor_tensor(YB[:, b + 1, :, :], YB[:, b + 1, :, :], yb[:, :].rearrange("p (t d) -> p t d", d=D), ALU.add).then_inc(y_done, 1)

        @block.tensor
        def _(pe):
            pe.wait_ge(w_in, 96)
            with pe.Fori(0, NBLK) as b:
                pe.wait_ge(vc_ready, b + 1)
                pe.wait_ge(ex_ready, b + 1)
                for k in range(4):
                    for c in range(2):
                        last = pe.matmul(gb[k][0:HC, :], wg[:, c, k * HC:(k + 1) * HC], vc[0][:, c, :], start=c == 0, stop=c == 1)
                last.then_inc(g_psum, 1)
                pe.wait_ge(gh_ready, b + 1)
                pe.wait_ge(y_done, b + 1)
                for t in range(TPB):
                    for c in range(2):
                        last = pe.matmul(yb[:, t * D:(t + 1) * D], hh[:, c, t * P:(t + 1) * P], wout[:, c, :], start=c == 0, stop=c == 1)
                last.then_inc(y_psum, 1)
    st.close()


def gated_mlp_stage(nc, tag, G, w):
    X, Y, ident = G["X"], G["Y"], G["ident"]
    XB = X[:, :, :].rearrange("p (b t) d -> p b t d", t=TPB)
    YB = Y[:, :, :].rearrange("p (b t) d -> p b t d", t=TPB)
    st = Stage(nc)
    sb, sem = (lambda n, s, d=F32: st.sb(f"{tag}_{n}", s, d)), (lambda n: st.sem(f"{tag}_{n}"))
    spare, credit = sb("spare", [P, 1]), sb("credit", [P, 2])
    stats, mv, half = sb("stats", [P, TPB, 6]), sb("mv", [P, TPB, 2]), sb("half", [P, TPB])
    rs, r2, r3 = [sb(n, [P, TPB]) for n in ("rs", "r2", "r3")]
    xn, xT = sb("xn", [P, TPB, D]), sb("xT", [P, BLK])
    wgr, wsh, g2 = sb("wgr", [D, 4 * P]), sb("wsh", [P, 2, D]), sb("g2", [P, 1])
    gt, mm = sb("gt", [P, 2, BLK]), sb("mm", [P, 2, BLK])
    xb, ob = st.bank(f"{tag}_xb"), st.bank(f"{tag}_ob")
    ub = [st.bank(f"{tag}_u{k}") for k in range(4)]
    w_in, half_set, stat_step, mv_ready, pool_chain, rstd_ready, xn_ready, x_added = [sem(n) for n in ("w_in", "half_set", "stat_step", "mv_ready", "pool_chain", "rstd_ready", "xn_ready", "x_added")]
    xT_psum, xT_ready, u_psum, gate_ready, m_ready, o_psum, x_done = [sem(n) for n in ("xT_psum", "xT_ready", "u_psum", "gate_ready", "m_ready", "o_psum", "x_done")]

    with nc.Block() as block:
        @block.sync
        def _(sp):
            sp.dma_start(wgr[:, :], w["W_grow"]).then_inc(w_in, 16)
            sp.dma_start(wsh[:, :, :], w["W_shrink"].rearrange("(c p) d -> p c d", p=P)).then_inc(w_in, 16)
            sp.dma_start(g2[:, :], w["gamma2"].rearrange("(p a) -> p a", a=1)).then_inc(w_in, 16)

        @block.gpsimd
        def _(pool):
            pool.memset(half[:, :], -0.5).then_inc(half_set, 1)
            pool.wait_ge(half_set, 1)

            def root(b):
                pool.wait_ge(mv_ready, b + 1)
                ch = Chain(pool, pool_chain, b * 2)
                ch(pool.tensor_tensor(r2[:, :], mv[:, :, 0], mv[:, :, 0], ALU.mult))
                ch(pool.tensor_tensor(r3[:, :], r2[:, :], mv[:, :, 1], ALU.add))
                pool.tensor_tensor(rs[:, :], r3[:, :], half[:, :], ALU.pow).then_inc(rstd_ready, 1)
                pool.tensor_tensor(XB[:, b + 1, :, :], XB[:, b + 1, :, :], YB[:, b + 1, :, :], ALU.add).then_inc(x_added, 1)

            root(0)
            with pool.Fori(1, NBLK) as b:
                root(b)

        @block.scalar
        def _(act):
            act.wait_ge(w_in, 48)
            with act.Fori(0, NBLK) as b:
                act.wait_ge(xT_psum, b + 1)
                act.activation(xT[:, :], xb[:, :], ACT.Identity, scale=g2[:, :]).then_inc(xT_ready, 1)
                act.wait_ge(u_psum, b + 1)
                for c in range(2):
                    last = act.activation(gt[:, c, :], ub[c][:, :], ACT.Gelu)
                last.then_inc(gate_ready, 1)

        @block.vector
        def _(dve):
            def stat(b):
                for t in range(TPB):
                    last = dve.bn_stats(stats[:, t, :], YB[:, b + 1, t, :])
                last.then_inc(stat_step, 1)
                dve.wait_ge(stat_step, b + 1)
                dve.memset(spare[:, :], 0.0)
                for t in range(TPB):
                    last = dve.bn_aggr(mv[:, t, :], stats[:, t, :])
                last.then_inc(mv_ready, 1)

            def norm(b):
                dve.wait_ge(rstd_ready, b + 1)
                for t in range(TPB):
                    last = dve.tensor_scalar(xn[:, t, :], YB[:, b + 1, t, :], rs[:, t:t + 1], None, ALU.mult)
                last.then_inc(xn_ready, 1)

            def gate(b):
                dve.wait_ge(gate_ready, b + 1)
                for c in range(2):
                    last = dve.tensor_tensor(mm[:, c, :], gt[:, c, :], ub[2 + c][:, :], ALU.mult)
                last.then_inc(m_ready, 1)

            def add(b):
                dve.wait_ge(o_psum, b + 1)
                dve.wait_ge(x_added, b + 1)
                dve.tensor_tensor(XB[:, b + 1, :, :], XB[:, b + 1, :, :], ob[:, :].rearrange("p (t d) -> p t d", d=D), ALU.add).then_inc(x_done, 1)

            for k, s in enumerate((m_ready, x_done)):
                dve.memset(credit[:, k:k + 1], 0.0).then_inc(s, 1)
            stat(0)
            norm(0)
            with dve.Fori(1, NBLK) as b:
                stat(b)
                dve.wait_ge(xT_psum, b)
                norm(b)
                gate(b - 1)
                add(b - 1)
            gate(NBLK - 1)
            add(NBLK - 1)

        @block.tensor
        def _(pe):
            pe.wait_ge(w_in, 48)
            with pe.Fori(0, NBLK) as b:
                pe.wait_ge(xn_ready, b + 1)
                for t in range(TPB):
                    last = pe.transpose(xb[:, t * P:(t + 1) * P], xn[:, t, :], ident[:, :])
                last.then_inc(xT_psum, 1)
                pe.wait_ge(xT_ready, b + 1)
                pe.wait_ge(m_ready, b + 1)
                for k in range(4):
                    last = pe.matmul(ub[k][:, :], wgr[:, k * P:(k + 1) * P], xT[:, :], start=True, stop=True)
                last.then_inc(u_psum, 1)
                pe.wait_ge(m_ready, b + 2)
                pe.wait_ge(x_done, b + 1)
                for t in range(TPB):
                    for c in range(2):
                        last = pe.matmul(ob[:, t * D:(t + 1) * D], mm[:, c, t * P:(t + 1) * P], wsh[:, c, :], start=c == 0, stop=c == 1)
                last.then_inc(o_psum, 1)
    st.close()


def recurrence_layer(nc, G, a):
    w = {k: a["L1_attn_b_" + k] for k in ("gamma1", "W_in", "conv_w", "conv_b", "W_gates", "b_gates", "forget_base", "W_out", "gamma2", "W_grow", "W_shrink")}
    with nc.sbuf_tensor("GT", [HC, 2, NSEQ * SEQ], F32) as GT, nc.sbuf_tensor("VT", [HC, 2, NSEQ, CONV - 1 + SEQ], F32) as VT:
        H = G | {"GT": GT, "VT": VT}
        recurrence_in_stage(nc, "RI", H, w)
        recurrence_stage(nc, "RR", H, w)
    gated_mlp_stage(nc, "RM", G, w)


def network(nc, a, out):
    with ExitStack() as ctx:
        G = make_globals(nc, ctx)
        init_globals(nc, G, a["L0_attn_a_X"].rearrange("b s d -> (b s) d"))
        attention_stage(nc, "A1", "diff", G, attn_args("diff", a))
        with ExitStack() as weights:
            weight_memory(nc, weights, G, "L0", 1024)
            load_gelu_experts(nc, "W0", G, a)
            expert_stage(nc, "F1", "gelu", G, gelu_args(a))
            attention_stage(nc, "A2", "causal", G, attn_args("causal", a))
            expert_stage(nc, "F2", "gelu", G, gelu_args(a))
        single_head_stage(nc, "A3", G, {k: a["L1_attn_a_" + k] for k in ("Wq", "bq", "Wk", "bk", "Wv", "bv")})
        weight_memory(nc, ctx, G, "L1", 768)
        load_swiglu_experts(nc, "W1", G, a)
        attention_stage(nc, "A4", "full", G, attn_args("full", a))
        expert_stage(nc, "F3", "swiglu", G, swiglu_args(a))
        recurrence_layer(nc, G, a)
        attention_stage(nc, "A5", "full", G, attn_args("full", a))
        expert_stage(nc, "F4", "swiglu", G, swiglu_args(a))
        store(nc, G, out.rearrange("b s d -> (b s) d"))


_TURNED = ("L0_attn_b_Wq", "L0_attn_b_Wk", "L0_attn_b_Wv", "L0_attn_b_Wo", "L1_attn_a_Wq", "L1_attn_a_Wk", "L1_attn_a_Wv",
           "L1_attn_b_W_in", "L1_attn_b_W_gates", "L1_attn_b_W_out", "L1_attn_b_W_grow", "L1_attn_b_W_shrink")


def kernel(**inputs):
    import numpy as _np
    import concourse.bacc as _bacc
    from concourse import mybir as _mybir
    from concourse.bass_utils import run_bass_kernel_spmd as _run

    nc = _bacc.Bacc("TRN2", target_bir_lowering=False, num_devices=1)
    arrays, args = {}, {}
    for name, a in inputs.items():
        a = _np.asarray(a)
        a = _np.ascontiguousarray(a.T if name in _TURNED else a)
        arrays[f"in_{name}"] = a
        args[name] = nc.dram_tensor(f"in_{name}", a.shape, _mybir.dt.from_np(a.dtype), kind="ExternalInput").ap()
    out = nc.dram_tensor("out", (NSEQ, SEQ, D), F32, kind="ExternalOutput").ap()
    network(nc, args, out)
    r = _run(nc, [arrays], core_ids=[0])
    return r.results[0]["out"]
```

```python
from contextlib import ExitStack

import concourse.bass as bass
from concourse import mybir

F32 = mybir.dt.float32
F32R = mybir.dt.float32r
BF16 = mybir.dt.bfloat16
ALU = mybir.AluOpType
ACT = mybir.ActivationFunctionType
AX = mybir.AxisListType.X

P = 128
D = 128
SEQ = 256
NSEQ = 16
TPS = SEQ // P
BLK = 512
TPB = BLK // P
NBLK = NSEQ * SEQ // BLK
PAD = TPB
NT = NSEQ * TPS + 2 * PAD
E = 8
E_CONST = 2.718281828459045
BIG = 1e30


class Chain:

    def __init__(self, eng, sem, base):
        self.eng, self.sem, self.base, self.n = eng, sem, base, 0

    def __call__(self, ins):
        self.n += 1
        ins.then_inc(self.sem, 1)
        self.eng.wait_ge(self.sem, self.base + self.n)


class Stage:

    def __init__(self, nc):
        self.nc, self.ctx, self.sems = nc, ExitStack(), []

    def sb(self, name, shape, dt=F32):
        return self.ctx.enter_context(self.nc.sbuf_tensor(name, shape, dt))

    def bank(self, name, banks=1):
        return self.ctx.enter_context(self.nc.psum_tensor(name, [P, 512 * banks], F32))

    def sem(self, name):
        s = self.nc.alloc_semaphore(name)
        self.sems.append(s)
        return s

    def close(self):
        self.nc.clear_and_free_semaphores(self.sems)
        self.nc.all_engine_barrier()
        self.ctx.close()


def split_weights(nc, tag, parts, width):
    st = Stage(nc)
    RING = 3
    raw = st.sb(f"{tag}_raw", [P, RING, width])
    loaded = [st.sem(f"{tag}_loaded{k}") for k in range(RING)]
    high_done = st.sem(f"{tag}_high")
    low_done = st.sem(f"{tag}_low")
    with nc.Block() as block:
        @block.sync
        def _(sp):
            for n, (loads, _, _) in enumerate(parts):
                if n >= RING:
                    sp.wait_ge(low_done, n - RING + 1)
                for (c0, c1), src in loads:
                    sp.dma_start(raw[:, n % RING, c0:c1] if len(src.shape) == 2 else
                                 raw[:, n % RING, c0:c1].rearrange("p (a b) -> p a b", a=src.shape[1]),
                                 src).then_inc(loaded[n % RING], 16)

        @block.scalar
        def _(act):
            for n, (loads, high, _) in enumerate(parts):
                act.wait_ge(loaded[n % RING], 16 * len(loads) * (n // RING + 1))
                act.activation(high, raw[:, n % RING, :], ACT.Copy).then_inc(high_done, 1)

        @block.vector
        def _(dve):
            for n, (loads, high, low) in enumerate(parts):
                dve.wait_ge(high_done, n + 1)
                dve.tensor_tensor(low, raw[:, n % RING, :], high.bitcast(F32), ALU.subtract).then_inc(low_done, 1)
    st.close()


def expert_stage(nc, tag, kind, G, w):
    X, ident, WH, WL = G["X"], G["ident"], G["WH"], G["WL"]
    gelu = kind == "gelu"
    SRC = X if gelu else G["Y"]
    EW = 1024 if gelu else 768
    CH = 4 if gelu else 2
    U = (E + 1) * CH
    R = 4 if gelu else 3
    HB = 4 if gelu else 2
    LAG = 2
    XB = X[:, :, :].rearrange("p (b t) d -> p b t d", t=TPB)
    SB_ = SRC[:, :, :].rearrange("p (b t) d -> p b t d", t=TPB)

    st = Stage(nc)
    sb, sem = (lambda n, s, d=F32: st.sb(f"{tag}_{n}", s, d)), (lambda n: st.sem(f"{tag}_{n}"))
    spare, spare2 = sb("spare", [P, 1]), sb("spare2", [P, 1])
    epst = sb("epst", [P, 4])
    stats = sb("stats", [P, TPB, 6])
    mv = sb("mv", [P, TPB, 2])
    rs = sb("rs", [P, TPB])
    rs2 = sb("rs2", [P, TPB])
    xn = sb("xn", [P, TPB, D])
    xT = sb("xT", [P, BLK])
    xh = [sb(f"xh{k}", [P, BLK], F32R) for k in range(2)]
    xl = [sb(f"xl{k}", [P, BLK], F32R) for k in range(2)]
    lg, l2, o1, o2, cc, ex, sel, comb = [sb(n, [P, TPB, E]) for n in ("lg", "l2", "o1", "o2", "cc", "ex", "sel", "comb")]
    r1, r2, r3 = [sb(n, [P, TPB]) for n in ("r1", "r2", "r3")]
    rank = sb("rank", [P, TPB, E])
    econst = sb("econst", [P, TPB, E])
    half = sb("half", [P, TPB])
    gwr = sb("gwr", [P, E])
    gwh = sb("gwh", [P, E], F32R)
    gwl = sb("gwl", [P, E], F32R)
    cTh = [sb(f"cTh{k}", [E, BLK], F32R) for k in range(2)]
    cTl = [sb(f"cTl{k}", [E, BLK], F32R) for k in range(2)]
    selr = sb("selr", [E, E, D])
    selE = sb("selE", [E, E, D], F32R)
    wbc = sb("wbc", [P, 2, BLK])
    acc = sb("acc", [P, 2, BLK])
    tmp = sb("tmp", [P, 2, BLK])
    credit = sb("credit", [P, 16])
    g32 = sb("g32", [P, R, BLK])
    gh = [sb(f"gh{k}", [P, BLK], F32R) for k in range(R)]
    gl = [sb(f"gl{k}", [P, BLK], F32R) for k in range(R)]
    if gelu:
        b1 = sb("b1", [P, (E + 1) * CH])
        b2 = sb("b2", [P, 1])
        gb = sb("gb", [P, E])
        eb2r = sb("eb2r", [E, D])
        eb2h = sb("eb2h", [E, D], F32R)
        eb2l = sb("eb2l", [E, D], F32R)
    else:
        s32 = sb("s32", [P, 2, BLK])
        nw = sb("nw", [P, 1])
    hb = [st.bank(f"{tag}_hb{k}", 1 if gelu else 2) for k in range(HB)]
    outb = [st.bank(f"{tag}_out{k}") for k in range(2)]
    misc = st.bank(f"{tag}_misc")
    wbb = st.bank(f"{tag}_wbb")

    started = sem("started")
    consts_in, const_ready, split_ready = sem("consts_in"), sem("const_ready"), sem("split_ready")
    mv_ready, rstd_ready, xn_ready, xadd_done = sem("mv_ready"), sem("rstd_ready"), sem("xn_ready"), sem("xadd_done")
    xT_psum, xT32_ready, xhigh_ready, xT_ready = sem("xT_psum"), sem("xT32_ready"), sem("xhigh_ready"), sem("xT_ready")
    logits_psum, lx_ready, ex_ready, comb_ready = sem("logits_psum"), sem("lx_ready"), sem("ex_ready"), sem("comb_ready")
    combT_psum, chigh_ready, combT_ready = sem("combT_psum"), sem("chigh_ready"), sem("combT_ready")
    prep_chain, pool_chain = sem("prep_chain"), sem("pool_chain")
    h_psum, silu_done, hid_done, hi_done, lo_done, g_free = [sem(n) for n in ("h_psum", "silu_done", "hid_done", "hi_done", "lo_done", "g_free")]
    wb_psum, wb_copied, out_free, acc_step = [sem(n) for n in ("wb_psum", "wb_copied", "out_free", "acc_step")]
    gate_psum, tmp_ready = sem("gate_psum"), sem("tmp_ready")
    fin_psum, fin_done = sem("fin_psum"), sem("fin_done")
    NPREP = 19 if gelu else 20
    NPOOL = 1 if gelu else 3
    NCONST = 4 if gelu else 2

    with nc.Block() as block:
        @block.sync
        def _(sp):
            sp.dma_start(gwr[:, :], w["gate_w"]).then_inc(consts_in, 16)
            if gelu:
                sp.dma_start(b1[:, 0:CH], w["sh_b1"].rearrange("(c p) -> p c", p=P), allow_slow_non_contiguous=True).then_inc(consts_in, 16)
                sp.dma_start(b1[:, CH:].rearrange("p (e c) -> p e c", e=E), w["eb1"].rearrange("e (c p) -> p e c", p=P), allow_slow_non_contiguous=True).then_inc(consts_in, 16)
                sp.dma_start(b2[:, :], w["sh_b2"].rearrange("(p a) -> p a", a=1)).then_inc(consts_in, 16)
                sp.dma_start(gb[:, :], w["gate_b"].rearrange("(a e) -> a e", a=1).to_broadcast([P, E])).then_inc(consts_in, 16)
                sp.dma_start(eb2r[:, :], w["eb2"]).then_inc(consts_in, 16)
            else:
                sp.dma_start(nw[:, :], w["norm_w"].rearrange("(p a) -> p a", a=1)).then_inc(consts_in, 16)

        NCIN = 16 * (6 if gelu else 2)

        @block.gpsimd
        def _(pool):
            pool.memset(econst[:, :, :], E_CONST)
            pool.memset(epst[:, :], w["eps"])
            pool.memset(half[:, :], -0.5)
            for e in range(E):
                pool.memset(rank[:, :, e:e + 1], float(E - e))
            pool.memset(selr[:, :, :], 0.0).then_inc(const_ready, 1)
            pool.wait_ge(const_ready, 1)
            pool.affine_select(out=selr[:, :, :], in_=selr[:, :, :], compare_op=ALU.not_equal, fill=1.0, base=0,
                               pattern=[[-1, E], [0, D]], channel_multiplier=1).then_inc(const_ready, 1)

            def root(b):
                pool.wait_ge(mv_ready, b + 1)
                ch = Chain(pool, pool_chain, b * NPOOL)
                if gelu:
                    ch(pool.tensor_tensor(rs2[:, :], mv[:, :, 1], epst[:, 0:mv.shape[1]], ALU.add))
                else:
                    ch(pool.tensor_tensor(rs[:, :], mv[:, :, 0], mv[:, :, 0], ALU.mult))
                    ch(pool.tensor_tensor(rs2[:, :], rs[:, :], mv[:, :, 1], ALU.add))
                    ch(pool.tensor_tensor(rs[:, :], rs2[:, :], epst[:, :], ALU.add))
                pool.tensor_tensor(rs[:, :], (rs2 if gelu else rs)[:, :], half[:, :], ALU.pow).then_inc(rstd_ready, 1)
                assert ch.n == NPOOL
                if gelu:
                    pool.wait_ge(xn_ready, b + 1)
                    pool.tensor_tensor(XB[:, b + 1, :, :], XB[:, b + 1, :, :], xn[:, :, :], ALU.add).then_inc(xadd_done, 1)

            def exponentials(b, steps):
                k = 1 if gelu else 2
                for j in steps:
                    pool.wait_ge(lx_ready, b * k + j + 1)
                    pool.tensor_tensor(ex[:, :, :], econst[:, :, :], l2[:, :, :], ALU.pow).then_inc(ex_ready, 1)

            pool.memset(spare2[:, :], 0.0).then_inc(xadd_done, 1)
            root(0)
            exponentials(0, range(1 if gelu else 2))
            if gelu:
                with pool.Fori(0, NBLK) as b:
                    root(b + 1)
                    exponentials(b + 1, range(1))
                return

            def accumulate(b, e, q):
                pool.wait_ge(tmp_ready, b * E + e + 1)
                pool.wait_ge(acc_step, b * E + e + 2)
                pool.tensor_tensor(acc[:, q, :], acc[:, q, :], tmp[:, e % 2, :], ALU.add).then_inc(acc_step, 1)

            with pool.Fori(0, NBLK // 2) as i:
                for p in range(2):
                    b = i * 2 + p
                    accumulate(b - 1, E, 1 - p)
                    root(b + 1)
                    for e in range(1, E):
                        accumulate(b, e, p)
                        if e == 3:
                            exponentials(b + 1, [0])
                        elif e == 4:
                            exponentials(b + 1, [1])
            accumulate(NBLK - 1, E, 1)

        @block.scalar
        def _(act):
            act.wait_ge(consts_in, NCIN)
            act.wait_ge(started, 1)

            def turn(b):
                act.wait_ge(xT_psum, b + 1)
                if gelu:
                    act.activation(xT[:, :], misc[:, :], ACT.Identity).then_inc(xT32_ready, 1)
                else:
                    act.activation(xT[:, :], misc[:, :], ACT.Identity, scale=nw[:, :]).then_inc(xT32_ready, 1)

            def high(b, n):
                act.wait_ge(hid_done, b * U + n + 1 + HB)
                act.wait_ge(g_free, b * U + n + 1)
                act.activation(gh[n % R][:, :], g32[:, n % R, :], ACT.Identity).then_inc(hi_done, 1)

            def spread(b, e):
                act.wait_ge(wb_psum, b * E + e)
                act.wait_ge(out_free, b * (E + 1) + e - 1 + 2)
                act.activation(wbc[:, e % 2, :], wbb[:, :], ACT.Identity).then_inc(wb_copied, 1)

            turn(0)
            with act.Fori(0, NBLK // 2) as i:
                for p in range(2):
                    b = i * 2 + p
                    for n in range(U):
                        e, c = divmod(n, CH)
                        act.wait_ge(h_psum if gelu else gate_psum, b * U + n + 1)
                        if gelu:
                            act.wait_ge(g_free, b * U + n + 1)
                            act.activation(g32[:, n % R, :], hb[n % HB][:, :], ACT.Gelu_apprx_tanh, bias=b1[:, n:n + 1])
                            act.activation(gh[n % R][:, :], hb[n % HB][:, :], ACT.Gelu_apprx_tanh,
                                           bias=b1[:, n:n + 1]).then_inc(hid_done, 1)
                        else:
                            act.activation(s32[:, n % 2, :], hb[n % HB][:, 0:512], ACT.Silu).then_inc(silu_done, 1)
                            if n >= 1:
                                high(b, n - 1)
                            if c == 1 and e >= 1:
                                spread(b, e)
                        if n == (13 if gelu else 8):
                            turn(b + 1)
                    if not gelu:
                        high(b, U - 1)

        @block.vector
        def _(dve):
            for j, s in enumerate([hid_done] * HB + [g_free] * R + [out_free] * (2 if gelu else 1) + [wb_copied] + [acc_step] * (1 if gelu else 2)):
                dve.memset(credit[:, j:j + 1], 0.0).then_inc(s, 1)
            if not gelu:
                dve.memset(outb[1][:, :], 0.0)
                dve.memset(wbc[:, 0, :], 0.0)
            dve.memset(acc[:, :, :], 0.0).then_inc(started, 1)
            dve.wait_ge(consts_in, NCIN)
            dve.wait_ge(const_ready, 2)
            dve.tensor_copy(gwh[:, :], gwr[:, :])
            dve.tensor_copy(selE[:, :, :], selr[:, :, :]).then_inc(split_ready, 1)
            if gelu:
                dve.tensor_copy(eb2h[:, :], eb2r[:, :]).then_inc(split_ready, 1)
            dve.wait_ge(split_ready, 2 if gelu else 1)
            dve.tensor_tensor(gwl[:, :], gwr[:, :], gwh[:, :].bitcast(F32), ALU.subtract).then_inc(split_ready, 1)
            if gelu:
                dve.tensor_tensor(eb2l[:, :], eb2r[:, :], eb2h[:, :].bitcast(F32), ALU.subtract).then_inc(split_ready, 1)

            def stat(b):
                ch = Chain(dve, prep_chain, b * NPREP)
                for t in range(TPB):
                    last = dve.bn_stats(stats[:, t, :], SB_[:, b + 1, t, :])
                ch(last)
                dve.memset(spare[:, :], 0.0)
                for t in range(TPB):
                    last = dve.bn_aggr(mv[:, t, :], stats[:, t, :])
                last.then_inc(mv_ready, 1)

            def norm(b):
                dve.wait_ge(rstd_ready, b + 1)
                for t in range(TPB):
                    if gelu:
                        last = dve.tensor_scalar(xn[:, t, :], SB_[:, b + 1, t, :], mv[:, t, 0:1], rs[:, t:t + 1], ALU.subtract, ALU.mult)
                    else:
                        last = dve.tensor_scalar(xn[:, t, :], SB_[:, b + 1, t, :], rs[:, t:t + 1], None, ALU.mult)
                last.then_inc(xn_ready, 1)

            def split_x(b, q):
                dve.wait_ge(xT32_ready, b + 1)
                dve.tensor_copy(xh[q][:, :], xT[:, :]).then_inc(xhigh_ready, 1)
                dve.wait_ge(xhigh_ready, b + 1)
                dve.tensor_tensor(xl[q][:, :], xT[:, :], xh[q][:, :].bitcast(F32), ALU.subtract).then_inc(xT_ready, 1)

            def bc(a):
                return a.unsqueeze(2).to_broadcast([P, TPB, E])

            def route1(b, first=1, last=13):
                if first == 1:
                    ch = Chain(dve, prep_chain, b * NPREP + 1)
                    dve.wait_ge(logits_psum, b + 1)
                    lp = misc[:, 0:TPB * E].rearrange("p (t e) -> p t e", e=E)
                    if gelu:
                        ch(dve.tensor_tensor(lg[:, :, :], lp, gb[:, :].unsqueeze(1).to_broadcast([P, TPB, E]), ALU.add))
                    else:
                        ch(dve.tensor_copy(lg[:, :, :], lp))
                    ch(dve.reduce_max(r1[:, :], lg[:, :, :], AX))
                    dve.tensor_tensor(l2[:, :, :], lg[:, :, :], bc(r1[:, :]), ALU.subtract).then_inc(lx_ready, 1)
                    ch(dve.tensor_tensor(cc[:, :, :], lg[:, :, :], bc(r1[:, :]), ALU.is_equal))
                    ch(dve.tensor_tensor(o1[:, :, :], cc[:, :, :], rank[:, :, :], ALU.mult))
                if first <= 5 and last >= 8:
                    ch = Chain(dve, prep_chain, b * NPREP + 5)
                    ch(dve.reduce_max(r2[:, :], o1[:, :, :], AX))
                    ch(dve.tensor_tensor(cc[:, :, :], o1[:, :, :], bc(r2[:, :]), ALU.is_equal))
                    ch(dve.scalar_tensor_tensor(o2[:, :, :], cc[:, :, :], -3e38, lg[:, :, :], ALU.mult, ALU.add))
                    ch(dve.reduce_max(r1[:, :], o2[:, :, :], AX))
                if last == 13:
                    ch = Chain(dve, prep_chain, b * NPREP + 9)
                    ch(dve.tensor_tensor(o1[:, :, :], o2[:, :, :], bc(r1[:, :]), ALU.is_equal))
                    ch(dve.tensor_tensor(o2[:, :, :], o1[:, :, :], rank[:, :, :], ALU.mult))
                    ch(dve.reduce_max(r2[:, :], o2[:, :, :], AX))
                    ch(dve.tensor_tensor(o1[:, :, :], o2[:, :, :], bc(r2[:, :]), ALU.is_equal))
                    ch(dve.tensor_tensor(sel[:, :, :], o1[:, :, :], cc[:, :, :], ALU.add))
                    assert ch.n == 5

            def route2(b):
                ch = Chain(dve, prep_chain, b * NPREP + 14)
                k = 1 if gelu else 2
                dve.wait_ge(ex_ready, b * k + 1)
                ch(dve.reduce_sum(r1[:, :], ex[:, :, :], AX))
                if gelu:
                    ch(dve.tensor_tensor(cc[:, :, :], ex[:, :, :], sel[:, :, :], ALU.mult))
                    ch(dve.reduce_sum(r2[:, :], cc[:, :, :], AX))
                    ch(dve.scalar_tensor_tensor(r3[:, :], r1[:, :], 1e-9, r2[:, :], ALU.mult, ALU.add))
                    ch(dve.reciprocal(r1[:, :], r3[:, :]))
                else:
                    ch(dve.reciprocal(r2[:, :], r1[:, :]))
                    ch(dve.tensor_tensor(cc[:, :, :], ex[:, :, :], bc(r2[:, :]), ALU.mult))
                    dve.tensor_tensor(l2[:, :, :], cc[:, :, :], bc(r2[:, :]), ALU.subtract).then_inc(lx_ready, 1)
                    return
                dve.tensor_tensor(comb[:, :, :], cc[:, :, :], bc(r1[:, :]), ALU.mult).then_inc(comb_ready, 1)
                assert ch.n == NPREP - 14

            def route3(b):
                if not gelu:
                    ch = Chain(dve, prep_chain, b * NPREP + 17)
                    dve.wait_ge(ex_ready, b * 2 + 2)
                    ch(dve.tensor_tensor(cc[:, :, :], ex[:, :, :], sel[:, :, :], ALU.mult))
                    ch(dve.reduce_sum(r2[:, :], cc[:, :, :], AX))
                    ch(dve.reciprocal(r1[:, :], r2[:, :]))
                    dve.tensor_tensor(comb[:, :, :], cc[:, :, :], bc(r1[:, :]), ALU.mult).then_inc(comb_ready, 1)
                    assert ch.n == NPREP - 17

            def split_comb(b, q):
                dve.wait_ge(combT_psum, b + 1)
                dve.tensor_copy(cTh[q][:, :], misc[0:E, :]).then_inc(chigh_ready, 1)
                dve.wait_ge(chigh_ready, b + 1)
                dve.tensor_tensor(cTl[q][:, :], misc[0:E, :], cTh[q][:, :].bitcast(F32), ALU.subtract).then_inc(combT_ready, 1)

            def spread(b, e):
                dve.wait_ge(wb_psum, b * E + e)
                dve.wait_ge(out_free, b * (E + 1) + e - 1 + 2)
                dve.tensor_copy(wbc[:, e % 2, :], wbb[:, :]).then_inc(wb_copied, 1)

            def combine(b, e, q):
                ob = b * (E + 1) + e
                dve.wait_ge(g_free, b * U + (e + 1) * CH + R)
                if e == 0:
                    if gelu:
                        ins = dve.tensor_scalar(acc[:, q, :], outb[(q + e) % 2][:, :], b2[:, :], None, ALU.add)
                    else:
                        ins = dve.tensor_copy(acc[:, q, :], outb[(q + e) % 2][:, :])
                    ins.then_inc(out_free, 1)
                else:
                    dve.wait_ge(acc_step, b * E + e + (0 if gelu else 1))
                    dve.wait_ge(wb_copied, b * E + e + 1)
                    dve.tensor_tensor(tmp[:, e % 2, :], outb[(q + e) % 2][:, :], wbc[:, e % 2, :], ALU.mult).then_inc(out_free, 1)
                    if not gelu:
                        dve.wait_ge(out_free, ob + 1 + 2)
                        dve.memset(credit[:, 14:15], 0.0).then_inc(tmp_ready, 1)
                        return
                    dve.wait_ge(out_free, ob + 1 + 2)
                    dve.tensor_tensor(acc[:, q, :], acc[:, q, :], tmp[:, e % 2, :], ALU.add).then_inc(acc_step, 1)

            def low(b, n):
                dve.wait_ge(hi_done, b * U + n + 1)
                dve.tensor_tensor(gl[n % R][:, :], g32[:, n % R, :], gh[n % R][:, :].bitcast(F32), ALU.subtract).then_inc(lo_done, 1)

            def finish(k):
                dve.wait_ge(fin_psum, k + 1)
                if gelu:
                    dve.wait_ge(xadd_done, k + 1)
                dve.tensor_tensor(XB[:, k, :, :], XB[:, k, :, :], misc[:, :].rearrange("p (t d) -> p t d", d=D), ALU.add).then_inc(fin_done, 1)

            stat(0)
            norm(0)
            split_x(0, 0)
            route1(0)
            route2(0)
            route3(0)
            split_comb(0, 0)
            with dve.Fori(0, NBLK // 2) as i:
                for p in range(2):
                    b = i * 2 + p
                    for n in range(U):
                        e, c = divmod(n, CH)
                        if gelu:
                            dve.wait_ge(hid_done, b * U + n + 1 + HB)
                            dve.tensor_tensor(gl[n % R][:, :], g32[:, n % R, :], gh[n % R][:, :].bitcast(F32), ALU.subtract).then_inc(lo_done, 1)
                            if c == 2 and e + 1 <= E:
                                spread(b, e + 1)
                            if c == 1 and e >= 1:
                                combine(b, e - 1, p)
                            at = {5: 0, 8: 1, 11: 2, 15: 3, 19: 4, 23: 5, 27: 6}.get(n)
                        else:
                            dve.wait_ge(silu_done, b * U + n + 1)
                            dve.wait_ge(h_psum, b * U + n + 1)
                            dve.tensor_tensor(g32[:, n % R, :], s32[:, n % 2, :], hb[n % HB][:, 512:1024], ALU.mult).then_inc(hid_done, 1)
                            if n >= 1:
                                low(b, n - 1)
                            if n == 1:
                                combine(b - 1, E, 1 - p)
                            elif c == 0 and e >= 2:
                                combine(b, e - 2, p)
                            at = {4: 0, 2: 1, 5: 2, 8: 3, 10: 7, 11: 8, 12: 9, 13: 5, 16: 10}.get(n)
                        if at == 0:
                            finish(b)
                        elif at == 1:
                            stat(b + 1)
                        elif at == 2:
                            norm(b + 1)
                        elif at == 3:
                            split_x(b + 1, 1 - p)
                        elif at == 4:
                            route1(b + 1)
                        elif at == 5:
                            route2(b + 1)
                        elif at == 6:
                            split_comb(b + 1, 1 - p)
                        elif at == 7:
                            route1(b + 1, 1, 4)
                        elif at == 8:
                            route1(b + 1, 5, 8)
                        elif at == 9:
                            route1(b + 1, 9, 13)
                        elif at == 10:
                            route3(b + 1)
                    if gelu:
                        combine(b, E, p)
                    else:
                        low(b, U - 1)
                        combine(b, E - 1, p)
                        split_comb(b + 1, 1 - p)
            if not gelu:
                combine(NBLK - 1, E, 1)
            finish(NBLK)

        @block.tensor
        def _(pe):
            pe.wait_ge(split_ready, 4 if gelu else 2)
            pe.wait_ge(started, 1)

            def product(out, pairs, first=True, last=True):
                for k, (sh, sl, mh, ml) in enumerate(pairs):
                    pe.matmul(out, sh, mh, start=first and k == 0, stop=False)
                    pe.matmul(out, sh, ml, start=False, stop=False)
                    ins = pe.matmul(out, sl, mh, start=False, stop=last and k == len(pairs) - 1)
                return ins

            def turn(b):
                pe.wait_ge(xn_ready, b + 1)
                for t in range(TPB):
                    last = pe.transpose(misc[:, t * P:(t + 1) * P], xn[:, t, :], ident[:, :])
                last.then_inc(xT_psum, 1)

            def route(b, q):
                pe.wait_ge(xT_ready, b + 1)
                for t in range(TPB):
                    c = slice(t * P, (t + 1) * P)
                    last = product(misc[:, t * E:(t + 1) * E], [(xh[q][:, c], xl[q][:, c], gwh[:, :], gwl[:, :])])
                last.then_inc(logits_psum, 1)

            def turn_comb(b):
                pe.wait_ge(comb_ready, b + 1)
                for t in range(TPB):
                    last = pe.transpose(misc[0:E, t * P:(t + 1) * P], comb[:, t, :], ident[:, :])
                last.then_inc(combT_psum, 1)

            def first(b, n, q):
                pe.wait_ge(hid_done, b * U + n + 1)
                e, c = divmod(n, CH)
                o = e * EW + c * P
                last = product(hb[n % HB][:, 0:512], [(WH[:, o:o + P], WL[:, o:o + P], xh[q][:, :], xl[q][:, :])])
                if not gelu:
                    last.then_inc(gate_psum, 1)
                    o += CH * P
                    last = product(hb[n % HB][:, 512:1024], [(WH[:, o:o + P], WL[:, o:o + P], xh[q][:, :], xl[q][:, :])])
                last.then_inc(h_psum, 1)

            def second(b, n, q):
                e, c = divmod(n, CH)
                ob = b * (E + 1) + e
                o = outb[(q + e) % 2][:, :]
                if c == 0:
                    pe.wait_ge(out_free, ob + 1)
                pe.wait_ge(lo_done, b * U + n + 1)
                k = e * EW + (EW - CH * P) + c * P
                bias = gelu and e == 0 and c == 0
                if bias:
                    product(o, [(eb2h[:, :], eb2l[:, :], cTh[q][:, :], cTl[q][:, :])], True, False)
                last = product(o, [(WH[:, k:k + P], WL[:, k:k + P], gh[n % R][:, :], gl[n % R][:, :])],
                               c == 0 and not bias, c == CH - 1)
                last.then_inc(g_free, 1)

            def spread(b, e, q):
                pe.wait_ge(wb_copied, b * E + e)
                if e == 1 and not gelu:
                    pe.wait_ge(combT_ready, b + 1)
                pe.matmul(wbb[:, :], selE[:, e - 1, :], cTh[q][:, :], start=True, stop=False)
                pe.matmul(wbb[:, :], selE[:, e - 1, :], cTl[q][:, :], start=False, stop=True).then_inc(wb_psum, 1)

            def finish(k, q):
                pe.wait_ge(acc_step, k * E + (1 if gelu else 3))
                for t in range(TPB):
                    last = pe.transpose(misc[:, t * P:(t + 1) * P], acc[:, q, t * P:(t + 1) * P], ident[:, :])
                last.then_inc(fin_psum, 1)

            turn(0)
            route(0, 0)
            turn_comb(0)
            pe.wait_ge(combT_ready, 1)
            for n in range(LAG):
                first(0, n, 0)
            with pe.Fori(0, NBLK // 2) as i:
                for p in range(2):
                    b = i * 2 + p
                    for n in range(U):
                        e, c = divmod(n, CH)
                        if n + LAG < U:
                            first(b, n + LAG, p)
                        else:
                            first(b + 1, n + LAG - U, 1 - p)
                        second(b, n, p)
                        if c == (1 if gelu else 0) and e + 1 <= E:
                            spread(b, e + 1, p)
                        at = ({4: 0, 12: 1, 17: 2, 25: 3} if gelu else {2: 0, 5: 1, 7: 2, 15: 3}).get(n)
                        if at == 0:
                            finish(b, 1 - p)
                        elif at == 1:
                            pe.wait_ge(fin_done, b + 1)
                            turn(b + 1)
                        elif at == 2:
                            route(b + 1, 1 - p)
                        elif at == 3:
                            turn_comb(b + 1)
                    if gelu:
                        pe.wait_ge(combT_ready, b + 2)
            finish(NBLK, 1)
    st.close()


def make_globals(nc, ctx):
    G = {}
    G["X"] = ctx.enter_context(nc.sbuf_tensor("X", [P, NT, D], F32))
    G["Y"] = ctx.enter_context(nc.sbuf_tensor("Y", [P, NT, D], F32))
    G["ident"] = ctx.enter_context(nc.sbuf_tensor("ident", [P, P], F32))
    return G


def weight_memory(nc, ctx, G, tag, width):
    G["WH"] = ctx.enter_context(nc.sbuf_tensor(f"{tag}_WH", [P, (E + 1) * width], F32R))
    G["WL"] = ctx.enter_context(nc.sbuf_tensor(f"{tag}_WL", [P, (E + 1) * width], F32R))


def init_globals(nc, G, x, y=None):
    st = Stage(nc)
    loaded, cleared = st.sem("init_loaded"), st.sem("init_cleared")
    X, Y, ident = G["X"], G["Y"], G["ident"]
    with nc.Block() as block:
        @block.sync
        def _(sp):
            sp.dma_start(X[:, PAD:NT - PAD, :], x.rearrange("(t p) d -> p t d", p=P)).then_inc(loaded, 16)
            if y is not None:
                sp.dma_start(Y[:, PAD:NT - PAD, :], y.rearrange("(t p) d -> p t d", p=P)).then_inc(loaded, 16)
            sp.wait_ge(loaded, 16 if y is None else 32)

        @block.vector
        def _(dve):
            for T in (X, Y):
                dve.memset(T[:, 0:PAD, :], 0.0)
                dve.memset(T[:, NT - PAD:NT, :], 0.0)

        @block.gpsimd
        def _(pool):
            pool.memset(ident[:, :], 0.0).then_inc(cleared, 1)
            pool.wait_ge(cleared, 1)
            pool.affine_select(out=ident[:, :], in_=ident[:, :], compare_op=ALU.not_equal, fill=1.0, base=0,
                               pattern=[[-1, P]], channel_multiplier=1).then_inc(cleared, 1)
    st.close()


def store(nc, G, out):
    st = Stage(nc)
    stored = st.sem("stored")
    with nc.Block() as block:
        @block.sync
        def _(sp):
            sp.dma_start(out.rearrange("(t p) d -> p t d", p=P), G["X"][:, PAD:NT - PAD, :]).then_inc(stored, 16)
            sp.wait_ge(stored, 16)
    st.close()


def load_gelu_experts(nc, tag, G, a):
    parts = []
    for e in range(E + 1):
        w1 = a["L0_ffn_sh_w1"] if e == 0 else a["L0_ffn_ew1"][e - 1]
        w2 = a["L0_ffn_sh_w2"] if e == 0 else a["L0_ffn_ew2"][e - 1]
        cols = slice(e * 1024, (e + 1) * 1024)
        parts.append(([((0, 512), w1), ((512, 1024), w2.rearrange("(c p) d -> p c d", p=P))],
                      G["WH"][:, cols], G["WL"][:, cols]))
    split_weights(nc, tag, parts, 1024)


def load_swiglu_experts(nc, tag, G, a):
    parts = []
    for e in range(E + 1):
        wg, wu, wd = [a[f"L1_ffn_sh_{n}"] if e == 0 else a[f"L1_ffn_e_{n}"][e - 1] for n in ("gate", "up", "down")]
        cols = slice(e * 768, (e + 1) * 768)
        parts.append(([((0, 256), wg), ((256, 512), wu), ((512, 768), wd.rearrange("(c p) d -> p c d", p=P))],
                      G["WH"][:, cols], G["WL"][:, cols]))
    split_weights(nc, tag, parts, 768)


def gelu_args(a):
    return {k: a[f"L0_ffn_{k}"] for k in ("gate_w", "gate_b", "sh_b1", "eb1", "sh_b2", "eb2")} | {"eps": 1e-5}


def swiglu_args(a):
    return {"gate_w": a["L1_ffn_router_w"], "norm_w": a["L1_ffn_norm2_w"], "eps": 1e-6}


def attention_stage(nc, tag, kind, G, w):
    X, Y, ident = G["X"], G["Y"], G["ident"]
    diff, full, masked = kind == "diff", kind == "full", kind != "full"
    NMAP, QUAD, NQ = 16, 4, 4
    DH, DV = (16, 32) if diff else (8, 8)
    GR = 64 if diff else 32
    NTL = NMAP * GR // P
    HPT = P // GR
    QT = QUAD // HPT
    KR = 3 * DH + 2
    NV = NMAP // 2 if diff else NMAP
    VW = NV * DV
    NC = VW // P
    OV = DV + 1
    VG = 64 if diff else 32
    NS = 2 if diff else 1
    PW = 384 if masked else 512
    NKU = NTL // 2
    SCALE = float(DH) ** -0.5
    XS = X[:, :, :].rearrange("p (s t) d -> p s t d", t=TPS)
    YS = Y[:, :, :].rearrange("p (s t) d -> p s t d", t=TPS)
    S0 = PAD // TPS

    st = Stage(nc)
    sb, sem = (lambda n, s, d=F32: st.sb(f"{tag}_{n}", s, d)), (lambda n: st.sem(f"{tag}_{n}"))
    spare = sb("spare", [P, 1])
    epst = sb("epst", [P, 4])
    stats, mv = sb("stats", [P, TPS, 6]), sb("mv", [P, TPS, 2])
    rs, rs2, rs3 = sb("rs", [P, TPS]), sb("rs2", [P, TPS]), sb("rs3", [P, TPS])
    half, epsr = sb("half", [P, 32]), sb("epsr", [P, TPS])
    nil, inv_dv, eps_dv = sb("nil", [P, TPS * QUAD]), sb("inv_dv", [P, 16]), sb("eps_dv", [P, 16])
    xn = sb("xn", [P, TPS, D])
    xh, xl = sb("xh", [P, SEQ], F32R), sb("xl", [P, SEQ], F32R)
    hi2 = sb("hi2", [P, 512], F32R)
    Q1 = [sb(f"Q1_{k}", [P, NTL * SEQ], F32R) for k in range(2)]
    kst = [sb(f"kst{k}", [P, 512], F32R) for k in range(2)]
    KB = [sb(f"KB_{k}", [P, HPT, NTL * SEQ], F32R) for k in range(2)]
    Q2 = [sb(f"Q2_{k}", [P, QT * SEQ], F32R) for k in range(2)]
    V = [sb(f"V_{k}", [P, TPS, NV, VG]) for k in range(2)]
    Pm = [sb(f"Pm{k}", [P, QUAD, PW]) for k in range(2)]
    OT = sb("OT", [P, NS * SEQ])
    mx = [sb(f"mx{k}", [P, TPS, QUAD]) for k in range(2)]
    mh = sb("mh", [P, TPS, QUAD], F32R)
    padm = sb("padm", [P, QT, TPS, HPT, GR])
    O = sb("O", [P, TPS, NMAP, OV])
    rec = sb("rec", [P, TPS, NMAP])
    ctx = sb("ctx", [P, TPS, VW])
    cTh, cTl = sb("cTh", [P, NC * SEQ], F32R), sb("cTl", [P, NC * SEQ], F32R)
    credit = sb("credit", [P, 16])
    if diff:
        T2 = sb("T2", [P, TPS, NMAP, DV])
        Dd = sb("Dd", [P, TPS, NV, DV])
        ss, sm, sm2, rr = [sb(n, [P, TPS * NV]) for n in ("ss", "sm", "sm2", "rr")]
        lamr = sb("lamr", [P, 4, NV * DH])
        lamp = sb("lamp", [P, 2, NV * DH])
        lams, lame, econst = sb("lams", [P, 2 * NV]), sb("lame", [P, 2 * NV]), sb("econst", [P, 2 * NV])
        wmap = sb("wmap", [P, NV, 2])
    raw = sb("raw", [P, 2 * NMAP * DH + VW + NC * D])
    wqk = [[sb(f"w{n}{k}", [P, NTL * P], F32R) for k in "hl"] for n in "qk"]
    wv = [sb(f"wv{k}", [P, VW], F32R) for k in "hl"]
    wo = [sb(f"wo{k}", [P, NC * D], F32R) for k in "hl"]
    rows = sb("rows", [P, 3, HPT])
    rvec = sb("rvec", [P, 3])
    colc = sb("colc", [P, 3])
    insc = sb("insc", [P, 1])
    outsc = sb("outsc", [P, 1])
    if masked:
        mf = Pm[0][:, :, :].rearrange("p j k -> p (j k)")[:, 0:5 * P].rearrange("p (c k) -> p c k", k=P)
        identb, maskS, maskT = sb("identb", [P, P], BF16), sb("maskS", [P, 3, P], BF16), sb("maskT", [P, 2, P], BF16)
    SB = 3
    sbank = [st.bank(f"{tag}_s{k}") for k in range(SB)]
    tbank = [st.bank(f"{tag}_t{k}") for k in range(2)]
    misc = st.bank(f"{tag}_misc")
    mbank, obank = st.bank(f"{tag}_mt"), st.bank(f"{tag}_ot")

    w_in, c_pool, w_step, started = sem("w_in"), sem("c_pool"), sem("w_step"), sem("started")
    mv_ready, rstd_ready, xhat_ready, xn_ready, xhigh = [sem(n) for n in ("mv_ready", "rstd_ready", "xhat_ready", "xn_ready", "xhigh")]
    misc_full, misc_read = sem("misc_full"), sem("misc_read")
    qk_high = sem("qk_high")
    s_psum, s_free, m_ready, pool_chain = sem("s_psum"), sem("s_free"), sem("m_ready"), sem("pool_chain")
    t_psum, t_free, p_used, o_free = sem("t_psum"), sem("t_free"), sem("p_used"), sem("o_free")
    ot_read, ob_full, mt_full, mt_read = sem("ot_read"), sem("ob_full"), sem("mt_full"), sem("mt_read")
    o_set = sem("o_set")
    k_spread = [sem(f"k_spread{k}") for k in range(2)]
    norm_chain, ss_ready, rr_ready, ctx_ready = sem("norm_chain"), sem("ss_ready"), sem("rr_ready"), sem("ctx_ready")
    chigh, cT_ready, y_done = sem("chigh"), sem("cT_ready"), sem("y_done")
    m_high, ss_mean, stat_step = sem("m_high"), sem("ss_mean"), sem("stat_step")

    QK = [f"QK{k}" for k in range(NTL)]
    pos = lambda x: (x // QUAD, x % QUAD)
    cfg = dict(q=[0, 1, 2, 4, 6, 7, 9, 10], t=14, c=12, y=15, v=11, r=5, m=7, d=8, e=9, f=11, s=13, st=6, n=10, n2=12, lag=0, tm=1, w=[2, 2], wm=2, pr=2) if diff else dict(q=[0, 2, 4, 6], t=14, c=8, y=10, v=12, r=5, m=6, s=9, n=10, n2=11, st=4, lag=1, tm=1, w=[1, 2], wm=2, pr=2)
    at = dict(zip([pos(x) for x in cfg["q"]], QK)) | {pos(cfg["t"]): "T", pos(cfg["c"]): "ctxT", pos(cfg["y"]): "y", pos(cfg["v"]): "V"}
    before = ["T"] + QK + ["V", "T1"]
    order = [at[key] for key in sorted(at)]
    NM, N0 = len(order), len(before)
    lead = {n: k for k, n in enumerate(before)}

    def use(b, name):
        return b * NM + N0 + order.index(name)

    KDMA = 16 * HPT * NKU // 2
    NROOT = 5 if full else 1
    NNORM = 5 if diff else 1

    with nc.Block() as block:
        @block.sync
        def _(sp):
            n = NMAP * DH
            sp.dma_start(raw[:, 0:n], w["wq"]).then_inc(w_in, 16)
            sp.dma_start(raw[:, n:2 * n], w["wk"]).then_inc(w_in, 16)
            sp.dma_start(raw[:, 2 * n:2 * n + VW], w["wv"]).then_inc(w_in, 16)
            sp.dma_start(raw[:, 2 * n + VW:].rearrange("p (c d) -> p c d", d=D), w["wo"].rearrange("(c p) d -> p c d", p=P)).then_inc(w_in, 16)
            if diff:
                for k, name in enumerate(("lambda_q1", "lambda_q2", "lambda_k1", "lambda_k2")):
                    sp.dma_start(lamr[:, k, :], w[name].rearrange("h d -> (h d)").unsqueeze(0).to_broadcast([P, NV * DH])).then_inc(w_in, 16)
                for k in range(P // DV):
                    sp.dma_start(outsc[k * DV:(k + 1) * DV, :], w["rms_scale"].rearrange("(p a) -> p a", a=1)).then_inc(w_in, 16)
            if full:
                sp.dma_start(insc[:, :], w["norm_w"].rearrange("(p a) -> p a", a=1)).then_inc(w_in, 16)

            def spread(m, k, q):
                sp.wait_ge(misc_read, m + 1)
                for r in range(HPT):
                    sp.dma_start(KB[q][r * GR:(r + 1) * GR, r, k * 512:(k + 1) * 512].bitcast(F32), kst[k % 2][r * GR:(r + 1) * GR, :].bitcast(F32)).then_inc(k_spread[k % 2], 16)

            for k in range(NKU):
                spread(lead[f"QK{2 * k + 1}"], k, 0)
            with sp.Fori(0, NSEQ // 2) as i:
                for p in range(2):
                    for k in range(NKU):
                        spread(use(i * 2 + p, f"QK{2 * k + 1}"), k, 1 - p)
            for k in range(2):
                sp.wait_ge(k_spread[k], (NSEQ + 1) * KDMA)

        NWIN = 16 * (4 + (4 + P // DV if diff else 0) + (1 if full else 0))

        @block.gpsimd
        def _(pool):
            pool.memset(epst[:, :], 1e-5)
            pool.memset(half[:, :], -0.5)
            pool.memset(padm[:, :, :, :, :], 0.0)
            pool.memset(epsr[:, :], 1e-6)
            pool.memset(nil[:, :], 0.0)
            pool.memset(inv_dv[:, :], 1.0 / DV)
            pool.memset(eps_dv[:, :], 1e-5)
            pool.memset(rows[:, :, :], -1.0)
            if diff:
                pool.memset(econst[:, :], E_CONST)
            if masked:
                pool.memset(mf[:, 0:2, :], 0.0)
                pool.memset(mf[:, 3:5, :], 0.0)
                pool.memset(mf[:, 2:3, :], -BIG)
            pool.memset(credit[:, 15:16], 0.0).then_inc(c_pool, 1)
            pool.wait_ge(c_pool, 1)
            for k, (a, z) in enumerate(((DH, 2 * DH), (2 * DH, 3 * DH), (3 * DH, 3 * DH + 2))):
                pool.affine_select(out=rows[:, k, :], in_=rows[:, k, :], compare_op=ALU.is_ge, fill=0.0, base=-a,
                                   pattern=[[-GR, HPT]], channel_multiplier=1).then_inc(c_pool, 1)
            pool.wait_ge(c_pool, 4)
            for k, (a, z) in enumerate(((DH, 2 * DH), (2 * DH, 3 * DH), (3 * DH, 3 * DH + 2))):
                pool.affine_select(out=rows[:, k, :], in_=rows[:, k, :], compare_op=ALU.is_ge, fill=0.0, base=z - 1,
                                   pattern=[[GR, HPT]], channel_multiplier=-1)
            if masked:
                pool.affine_select(out=mf[:, 0:2, :], in_=mf[:, 0:2, :],
                                   compare_op=ALU.is_ge, fill=-BIG, base=0, pattern=[[0, 2], [-1, P]], channel_multiplier=1)
                pool.affine_select(out=mf[:, 3:5, :], in_=mf[:, 3:5, :],
                                   compare_op=ALU.is_ge, fill=-BIG, base=0, pattern=[[0, 2], [1, P]], channel_multiplier=-1)
            pool.memset(credit[:, 14:15], 0.0).then_inc(c_pool, 1)
            if diff:
                pool.wait_ge(w_step, 4)
                pool.tensor_tensor(lame[:, :], econst[:, :], lams[:, :], ALU.pow).then_inc(c_pool, 1)
            pool.wait_ge(started, 1)

            def root(b):
                pool.wait_ge(mv_ready, b + 1)
                ch = Chain(pool, pool_chain, b * NROOT)
                ch(pool.tensor_tensor(rs2[:, :], mv[:, :, 1], epst[:, 0:mv.shape[1]], ALU.add))
                last = pool.tensor_tensor(rs[:, :], rs2[:, :], half[:, 0:TPS], ALU.pow)
                if full:
                    ch(last)
                    ch(pool.tensor_tensor(rs2[:, :], rs[:, :], rs[:, :], ALU.mult))
                    ch(pool.tensor_tensor(rs3[:, :], rs2[:, :], mv[:, :, 1], ALU.mult))
                    ch(pool.tensor_tensor(rs2[:, :], rs3[:, :], epsr[:, :], ALU.add))
                    last = pool.tensor_tensor(rs3[:, :], rs2[:, :], half[:, 0:TPS], ALU.pow)
                last.then_inc(rstd_ready, 1)

            def maxima(q, r):
                pool.wait_ge(s_free, SB + (q + 1) * QUAD)
                pool.wait_ge(mt_full, q + 1)
                pool.tensor_tensor(mh[:, :, :], mx[r][:, :, :], nil[:, :].rearrange("p (t j) -> p t j", t=TPS), ALU.add).then_inc(m_high, 1)
                pool.wait_ge(m_high, q + 1)
                src = mh[:, :, :].bitcast(F32).rearrange("p q (t r) -> p t q r", r=HPT)
                raw_m = mx[r][:, :, :].rearrange("p q (t r) -> p t q r", r=HPT)
                pool.tensor_tensor(padm[:, :, :, :, 3 * DH], src, nil[:, :].rearrange("p (t q r) -> p t q r", t=QT, q=TPS), ALU.add)
                pool.tensor_tensor(padm[:, :, :, :, 3 * DH + 1], raw_m, src, ALU.subtract).then_inc(m_ready, 1)

            def head_root(k):
                pool.wait_ge(ss_ready, k + 1)
                pool.tensor_tensor(sm[:, :], ss[:, :], inv_dv[:, :], ALU.mult).then_inc(ss_mean, 1)
                pool.wait_ge(ss_mean, k * 2 + 1)
                pool.tensor_tensor(sm2[:, :], sm[:, :], eps_dv[:, :], ALU.add).then_inc(ss_mean, 1)
                pool.wait_ge(ss_mean, k * 2 + 2)
                pool.tensor_tensor(rr[:, :], sm2[:, :], half[:, 0:TPS * NV], ALU.pow).then_inc(rr_ready, 1)

            root(0)
            root(1)
            maxima(0, 0)
            with pool.Fori(0, NSEQ) as b:
                for g in range(NQ):
                    maxima(b * NQ + g + 1, (g + 1) % 2)
                    if g == 1:
                        root(b + 2)
                    elif g == 2 and diff:
                        head_root(b)
                if full:
                    pool.wait_ge(misc_read, use(b, "y") + 1)
                    pool.tensor_tensor(XS[:, b + S0 - 1, :, :], XS[:, b + S0 - 1, :, :], YS[:, b + S0 - 1, :, :], ALU.add)
            if diff:
                head_root(NSEQ)
            if full:
                pool.wait_ge(misc_read, NSEQ * NM + N0 + 2)
                pool.tensor_tensor(XS[:, NSEQ + S0 - 1, :, :], XS[:, NSEQ + S0 - 1, :, :], YS[:, NSEQ + S0 - 1, :, :], ALU.add)

        @block.scalar
        def _(act):
            act.wait_ge(started, 1)

            def turned(m):
                act.wait_ge(misc_full, m + 1)
                act.activation(xh[:, :], misc[:, 0:SEQ], ACT.Identity, scale=insc[:, :] if full else 1.0).then_inc(xhigh, 1)

            def high(m, k, nqk):
                act.wait_ge(misc_full, m + 1)
                if k % 2:
                    act.activation(hi2[:, :], misc[:, :], ACT.Identity, bias=colc[:, 2:3]).then_inc(qk_high, 1)
                else:
                    act.activation(hi2[:, :], misc[:, :], ACT.Identity).then_inc(qk_high, 1)

            def values(m, q):
                act.wait_ge(misc_full, m + 1)
                act.activation(V[q][:, :, :, 0:DV], misc[:, 0:TPS * VW].rearrange("p (t h d) -> p t h d", t=TPS, d=DV),
                               ACT.Identity).then_inc(misc_read, 1)

            def exp(n, j, r):
                act.wait_ge(t_psum, n * QUAD + j + 1)
                if j == 0:
                    act.wait_ge(p_used, n + 1)
                act.activation(Pm[r][:, j, :], tbank[j % 2][:, 0:PW], ACT.Exp, scale=SCALE).then_inc(t_free, 1)

            def products(n):
                act.wait_ge(p_used, n + 2)
                act.wait_ge(ob_full, n + 1)
                act.activation(OT[:, :], obank[:, 0:NS * SEQ], ACT.Identity).then_inc(ot_read, 1)

            def context(n, g, k):
                act.wait_ge(ob_full, n + 1)
                if g == 0:
                    act.wait_ge(norm_chain, k * NNORM + 4) if diff else act.wait_ge(ctx_ready, k + 1)
                for s in range(NS):
                    last = act.activation(O[:, :, g * QUAD:(g + 1) * QUAD, :].rearrange("p t (h s) d -> p s t h d", s=NS)[:, s],
                                          obank[:, s * SEQ:(s + 1) * SEQ].rearrange("p (t h d) -> p t h d", t=TPS, d=VG)[:, :, :, 0:OV],
                                          ACT.Identity)
                last.then_inc(o_free, 1)

            def ctx_turned(m):
                act.wait_ge(misc_full, m + 1)
                act.activation(cTh[:, :], misc[:, 0:NC * SEQ], ACT.Identity, scale=outsc[:, :] if diff else 1.0).then_inc(chigh, 1)

            turned(lead["T"])
            for k in range(NTL):
                high(lead[f"QK{k}"], k, k)
            values(lead["V"], 0)
            turned(lead["T1"])
            with act.Fori(0, NSEQ // 2) as i:
                for p in range(2):
                    b = i * 2 + p
                    for g in range(NQ):
                        gq = b * NQ + g
                        for j in range(QUAD):
                            exp(gq, j, g % 2)
                            if j == 0:
                                context(gq, (g + 2) % 4, b)
                            elif j == cfg["pr"]:
                                products(gq)
                            name = at.get((g, j), "")
                            if name == "T":
                                turned(use(b, name))
                            elif name == "ctxT":
                                ctx_turned(use(b, name))
                            elif name == "V":
                                values(use(b, name), 1 - p)
                            elif name.startswith("QK"):
                                high(use(b, name), int(name[2:]), None)
            context(NSEQ * NQ, 2, None)
            products(NSEQ * NQ)
            context(NSEQ * NQ + 1, 3, None)
            ctx_turned(NSEQ * NM + N0)

        @block.vector
        def _(dve):
            for j, s in enumerate([s_free] * SB + [t_free] * 2 + [p_used, o_free, ot_read, mt_full, mt_read]):
                dve.memset(credit[:, j:j + 1], 0.0).then_inc(s, 1)
            for k in range(2):
                dve.memset(V[k][:, :, :, DV:VG], 0.0)
                dve.memset(KB[k][:, :, :].bitcast(F32), 0.0)
            dve.memset(V[1][:, :, :, 0:DV], 0.0).then_inc(o_set, 1)
            dve.memset(O[:, :, :, :], 1.0)
            dve.memset(OT[:, :], 1.0)
            dve.memset(Pm[1][:, :, :], 1.0)
            dve.wait_ge(o_set, 1)
            for k in range(2):
                dve.memset(V[k][:, :, :, DV:OV], 1.0)
            for n in range(2):
                for k in range(2):
                    dve.memset(wqk[n][k][:, :].bitcast(F32), 0.0)
            dve.wait_ge(w_in, NWIN)
            dve.wait_ge(c_pool, 5)
            if masked:
                dve.tensor_copy(identb[:, :], ident[:, :])
                dve.tensor_copy(maskS[:, :, :], mf[:, 0:3, :])
                dve.tensor_copy(maskT[:, :, :], mf[:, 3:5, :])
            dve.tensor_copy(wv[0][:, :], raw[:, 2 * NMAP * DH:2 * NMAP * DH + VW])
            dve.tensor_copy(wo[0][:, :], raw[:, 2 * NMAP * DH + VW:])
            dve.reduce_sum(rvec[:, :], rows[:, :, :], AX).then_inc(w_step, 1)
            dve.wait_ge(w_step, 1)
            for n in range(2):
                src = raw[:, n * NMAP * DH:(n + 1) * NMAP * DH].rearrange("p (h d) -> p h d", d=DH)
                for rep in range(3):
                    last = dve.tensor_copy(wqk[n][0][:, :].rearrange("p (h g) -> p h g", g=GR)[:, :, rep * DH:(rep + 1) * DH], src)
            last.then_inc(w_step, 1)
            dve.wait_ge(w_step, 2)
            for n in range(2):
                src = raw[:, n * NMAP * DH:(n + 1) * NMAP * DH].rearrange("p (h d) -> p h d", d=DH)
                for rep in range(3):
                    sl = (slice(None), slice(None), slice(rep * DH, (rep + 1) * DH))
                    dve.tensor_tensor(wqk[n][1][:, :].rearrange("p (h g) -> p h g", g=GR)[sl], src,
                                      wqk[n][0][:, :].bitcast(F32).rearrange("p (h g) -> p h g", g=GR)[sl], ALU.subtract)
            dve.tensor_tensor(wv[1][:, :], raw[:, 2 * NMAP * DH:2 * NMAP * DH + VW], wv[0][:, :].bitcast(F32), ALU.subtract)
            dve.tensor_tensor(wo[1][:, :], raw[:, 2 * NMAP * DH + VW:], wo[0][:, :].bitcast(F32), ALU.subtract)
            dve.tensor_copy(colc[:, 0:1], rvec[:, 0:1])
            dve.tensor_tensor(colc[:, 1:2], rvec[:, 1:2], rvec[:, 2:3], ALU.subtract)
            dve.tensor_copy(colc[:, 2:3], rvec[:, 2:3])
            if diff:
                dve.tensor_tensor(lamp[:, :, :], lamr[:, 0:2, :], lamr[:, 2:4, :], ALU.mult).then_inc(w_step, 1)
                dve.wait_ge(w_step, 3)
                dve.reduce_sum(lams[:, :], lamp[:, :, :].rearrange("p a (h d) -> p (a h) d", d=DH), AX).then_inc(w_step, 1)
                dve.memset(wmap[:, :, 0:1], 1.0)
                dve.wait_ge(c_pool, 6)
                dve.tensor_tensor(lamp[:, 0, 0:NV], lame[:, NV:2 * NV], lame[:, 0:NV], ALU.subtract).then_inc(w_step, 1)
                dve.wait_ge(w_step, 5)
                dve.tensor_scalar(wmap[:, :, 1], lamp[:, 0, 0:NV], 0.8, None, ALU.subtract)
                dve.tensor_scalar(outsc[:, :], outsc[:, :], 1.0 - 0.8, None, ALU.mult)
            dve.memset(credit[:, 13:14], 0.0).then_inc(started, 1)
            dve.wait_ge(started, 1)

            def stat(b):
                for t in range(TPS):
                    last = dve.bn_stats(stats[:, t, :], XS[:, b + S0, t, :])
                last.then_inc(stat_step, 1)
                dve.wait_ge(stat_step, b + 1)
                dve.memset(spare[:, :], 0.0)
                for t in range(TPS):
                    last = dve.bn_aggr(mv[:, t, :], stats[:, t, :])
                last.then_inc(mv_ready, 1)

            def norm(b):
                dve.wait_ge(rstd_ready, b + 1)
                for t in range(TPS):
                    last = dve.tensor_scalar(YS[:, b + S0, t, :] if full else xn[:, t, :], XS[:, b + S0, t, :], mv[:, t, 0:1], rs[:, t:t + 1], ALU.subtract, ALU.mult)
                last.then_inc(xhat_ready if full else xn_ready, 1)

            def norm2(b):
                if full:
                    dve.wait_ge(xhat_ready, b + 1)
                    for t in range(TPS):
                        last = dve.tensor_scalar(xn[:, t, :], YS[:, b + S0, t, :], rs3[:, t:t + 1], None, ALU.mult)
                    last.then_inc(xn_ready, 1)

            def split_x(b):
                dve.wait_ge(xhigh, b + 1)
                if full:
                    last = dve.scalar_tensor_tensor(xl[:, :], misc[:, 0:SEQ], insc[:, :], xh[:, :].bitcast(F32), ALU.mult, ALU.subtract)
                else:
                    last = dve.tensor_tensor(xl[:, :], misc[:, 0:SEQ], xh[:, :].bitcast(F32), ALU.subtract)
                last.then_inc(misc_read, 1)

            def stack(b, m, k, q, lead_in=False):
                dve.wait_ge(qk_high, b * NTL + k + 1)
                n, c = k % 2, slice((k // 2) * 512, (k // 2 + 1) * 512)
                if n:
                    u = k // 2
                    if u >= 2 or not lead_in:
                        dve.wait_ge(k_spread[u % 2], b * KDMA + u // 2 * 16 * HPT)
                    dve.scalar_tensor_tensor(kst[u % 2][:, :], hi2[:, :].bitcast(F32), colc[:, 1:2], misc[:, :], ALU.mult, ALU.add).then_inc(misc_read, 1)
                else:
                    dve.scalar_tensor_tensor(Q1[q][:, c], hi2[:, :].bitcast(F32), colc[:, 0:1], misc[:, :], ALU.mult, ALU.add).then_inc(misc_read, 1)

            def top(n, j, r, use_, lead_in=False):
                dve.wait_ge(s_psum, n * QUAD + j + 1)
                if j == 0 and not lead_in:
                    dve.wait_ge(m_ready, n - 1)
                dve.reduce_max(mx[r][:, :, j], sbank[use_ % SB][:, :].rearrange("p (t k) -> p t k", t=TPS), AX).then_inc(s_free, 1)

            def with_max(n, g, q):
                dve.wait_ge(mt_full, n + 2)
                c = slice(g * QT * SEQ, (g + 1) * QT * SEQ)
                dve.tensor_tensor(Q2[g % 2][:, :], Q1[q][:, c].bitcast(F32), mbank[:, 0:QT * SEQ], ALU.add).then_inc(mt_read, 1)

            def reciprocals(k):
                dve.wait_ge(o_free, 3 + k * NQ)
                dve.reciprocal(rec[:, :, :], O[:, :, :, DV]).then_inc(norm_chain, 1)

            def weights(k):
                dve.wait_ge(norm_chain, k * NNORM + 1)
                dve.tensor_tensor(rec[:, :, :], rec[:, :, :], wmap[:, :, :].rearrange("p h s -> p (h s)").unsqueeze(1).to_broadcast([P, TPS, NMAP]), ALU.mult).then_inc(norm_chain, 1)
                dve.wait_ge(norm_chain, k * NNORM + 2)
                dve.tensor_tensor(T2[:, :, :, :], O[:, :, :, 0:DV], rec[:, :, :].unsqueeze(3).to_broadcast([P, TPS, NMAP, DV]), ALU.mult).then_inc(norm_chain, 1)

            def difference(k):
                tv = T2[:, :, :, :].rearrange("p t (h s) d -> p (t h) s d", s=2)
                dve.wait_ge(norm_chain, k * NNORM + 3)
                dve.tensor_tensor(dv_, tv[:, :, 0, :], tv[:, :, 1, :], ALU.add).then_inc(norm_chain, 1)

            def squares(k):
                dve.wait_ge(norm_chain, k * NNORM + 4)
                dve.tensor_tensor(T2[:, 0, :, :], dv_, dv_, ALU.mult).then_inc(norm_chain, 1)

            def square_sums(k):
                dve.wait_ge(norm_chain, k * NNORM + 5)
                dve.reduce_sum(ss[:, :], T2[:, 0, :, :], AX).then_inc(ss_ready, 1)

            def context(k):
                if diff:
                    dve.wait_ge(rr_ready, k + 1)
                    dve.tensor_tensor(ctx[:, :, :].rearrange("p t (h d) -> p (t h) d", d=DV), dv_,
                                      rr[:, :].unsqueeze(2).to_broadcast([P, TPS * NV, DV]), ALU.mult).then_inc(ctx_ready, 1)
                else:
                    dve.wait_ge(norm_chain, k + 1)
                    dve.tensor_tensor(ctx[:, :, :].rearrange("p t (h d) -> p t h d", d=DV), O[:, :, :, 0:DV],
                                      rec[:, :, :].unsqueeze(3).to_broadcast([P, TPS, NMAP, DV]), ALU.mult).then_inc(ctx_ready, 1)

            def split_ctx(k):
                dve.wait_ge(chigh, k + 1)
                if diff:
                    last = dve.scalar_tensor_tensor(cTl[:, :], misc[:, 0:NC * SEQ], outsc[:, :], cTh[:, :].bitcast(F32), ALU.mult, ALU.subtract)
                else:
                    last = dve.tensor_tensor(cTl[:, :], misc[:, 0:NC * SEQ], cTh[:, :].bitcast(F32), ALU.subtract)
                last.then_inc(misc_read, 1)

            def add_y(k, m):
                dve.wait_ge(misc_full, m + 1)
                y = misc[:, 0:SEQ].rearrange("p (t d) -> p t d", d=D)
                if full:
                    dve.tensor_tensor(YS[:, k + S0 - 1, :, :], y, YS[:, k + S0 - 1, :, :], ALU.add).then_inc(misc_read, 1)
                else:
                    dve.tensor_tensor(XS[:, k + S0 - 1, :, :], XS[:, k + S0 - 1, :, :], y, ALU.add).then_inc(misc_read, 1)

            if diff:
                dv_ = Dd[:, :, :, :].rearrange("p t h d -> p (t h) d")
                steps = {pos(cfg["r"]): (reciprocals,), pos(cfg["m"]): (weights,), pos(cfg["d"]): (difference, squares), pos(cfg["e"]): (square_sums,), pos(cfg["f"]): (context,)}
            else:
                steps = {pos(cfg["r"]): (reciprocals,), pos(cfg["m"]): (context,)}
            after_turn, lag = pos(cfg["s"]), cfg["lag"]
            stat(0)
            norm(0)
            norm2(0)
            split_x(0)
            for k in range(NTL):
                stack(0, lead[f"QK{k}"], k, 0, lead_in=True)
            dve.wait_ge(misc_full, lead["T"] + 1)
            stat(1)
            norm(1)
            norm2(1)
            split_x(1)
            for n in range(2):
                for j in range(QUAD):
                    top(n, j, n, n * QUAD + j + 1, lead_in=True)
            with_max(0, 0, 0)
            with dve.Fori(0, NSEQ // 2) as i:
                for p in range(2):
                    b = i * 2 + p
                    for g in range(NQ):
                        gq = b * NQ + g
                        for j in range(QUAD):
                            top(gq + 2, j, g % 2, (p * NQ + g) * QUAD + j)
                            if j == cfg["wm"]:
                                with_max(gq + 1, (g + 1) % NQ, p if g < NQ - 1 else 1 - p)
                            for step in steps.get((g, j), ()):
                                step(b)
                            name = at.get((g, j), "")
                            if (g, j) == pos(cfg["t"] + 1):
                                split_x(b + 2)
                            if (g, j) == pos(cfg["st"]):
                                stat(b + 2)
                            elif (g, j) == pos(cfg["n"]):
                                norm(b + 2)
                            elif (g, j) == pos(cfg["n2"]):
                                norm2(b + 2)
                            if (g, j) == after_turn:
                                split_ctx(b)
                            if name == "y":
                                add_y(b, use(b, name))
                            name = at.get(((g * QUAD + j - lag) // QUAD, (j - lag) % QUAD), "")
                            if name.startswith("QK"):
                                stack(b + 1, use(b, name), int(name[2:]), 1 - p)
            for key in sorted(steps):
                for step in steps[key]:
                    step(NSEQ)
            split_ctx(NSEQ)
            add_y(NSEQ, NSEQ * NM + N0 + 1)

        @block.tensor
        def _(pe):
            pe.wait_ge(started, 1)

            def product(out, pairs):
                for k, (sh, sl, mh_, ml) in enumerate(pairs):
                    pe.matmul(out, sh, mh_, start=k == 0, stop=False)
                    pe.matmul(out, sh, ml, start=False, stop=False)
                    ins = pe.matmul(out, sl, mh_, start=False, stop=k == len(pairs) - 1)
                return ins

            def free_bank(m):
                pe.wait_ge(misc_read, m)

            def turn(b, m):
                free_bank(m)
                pe.wait_ge(xn_ready, b + 1)
                for t in range(TPS):
                    last = pe.transpose(misc[:, t * P:(t + 1) * P], xn[:, t, :], ident[:, :])
                last.then_inc(misc_full, 1)

            def project(b, m, k):
                free_bank(m)
                n = k % 2
                for r in range(2):
                    c = slice((k // 2 * 2 + r) * P, (k // 2 * 2 + r + 1) * P)
                    last = product(misc[:, r * SEQ:(r + 1) * SEQ], [(wqk[n][0][:, c], wqk[n][1][:, c], xh[:, :], xl[:, :])])
                last.then_inc(misc_full, 1)

            def values(b, m):
                free_bank(m)
                for t in range(TPS):
                    c = slice(t * P, (t + 1) * P)
                    last = product(misc[:, t * VW:(t + 1) * VW], [(xh[:, c], xl[:, c], wv[0][:, :], wv[1][:, :])])
                last.then_inc(misc_full, 1)

            def keys_spread(b, g):
                k = g * QT // 2
                pe.wait_ge(k_spread[k % 2], b * KDMA + (k // 2 + 1) * 16 * HPT)

            def score(n, g, j, q, use_):
                pe.wait_ge(s_free, n * QUAD + j + (2 if use_ < 2 else 1))
                o = sbank[use_ % SB]
                c0 = (g * QT + j // HPT) * SEQ
                if masked:
                    pe.matmul(o[:, :].rearrange("p (c k) -> p c k", k=P)[:, 0::3, :], identb[:, :], maskS[:, 0:2, :], start=True, stop=True)
                for t in range(TPS):
                    nk = P if masked and t == 0 else SEQ
                    last = pe.matmul(o[:, t * SEQ:t * SEQ + nk], Q1[q][:, c0 + t * P:c0 + (t + 1) * P], KB[q][:, j % HPT, c0:c0 + nk],
                                     start=not masked, stop=True, skip_group_check=masked)
                last.then_inc(s_psum, 1)

            def score_t(n, g, j, q):
                pe.wait_ge(t_free, n * QUAD + j + 1)
                if j == 0:
                    pe.wait_ge(mt_read, n + 2)
                o = tbank[j % 2]
                c0 = (g * QT + j // HPT) * SEQ
                c2 = (j // HPT) * SEQ
                if masked:
                    pe.matmul(o[:, :].rearrange("p (c k) -> p c k", k=P)[:, 0::2, :], identb[:, :], maskT[:, :, :], start=True, stop=True)
                for t in range(TPS):
                    q0 = P if masked and t == 1 else 0
                    last = pe.matmul(o[:, t * SEQ:(t + 1) * SEQ - q0], KB[q][:, j % HPT, c0 + t * P:c0 + (t + 1) * P], Q2[g % 2][:, c2 + q0:c2 + SEQ],
                                     start=not masked, stop=True, skip_group_check=masked)
                last.then_inc(t_psum, 1)

            def weigh(n, g, q, s):
                if s == 0:
                    pe.wait_ge(t_free, 2 + n * QUAD)
                    pe.wait_ge(o_free, n + 2)
                q0 = P if masked and s == 1 else 0
                for h in range(QUAD // NS):
                    last = pe.matmul(obank[h * VG:(h + 1) * VG, 0:NS * SEQ].rearrange("p (s q) -> p s q", s=NS)[:, :, q0:],
                                     V[q][:, s, g * QUAD // NS + h, :], Pm[g % 2][:, h * NS:(h + 1) * NS, s * SEQ:(s + 1) * SEQ - q0],
                                     start=s == 0, stop=True, skip_group_check=s > 0, tile_position=(0, h * VG))
                if s == TPS - 1:
                    last.then_inc(p_used, 1)

            def turn_back(n):
                pe.wait_ge(ot_read, n + 2)
                for c in range(NS * TPS):
                    last = pe.transpose(obank[:, c * P:(c + 1) * P], OT[:, c * P:(c + 1) * P], ident[:, :])
                last.then_inc(ob_full, 1)

            def turn_max(n):
                pe.wait_ge(mt_read, n + 1)
                pe.wait_ge(m_ready, n + 1)
                for u in range(QT):
                    for t in range(TPS):
                        c = (u * TPS + t) * P
                        last = pe.transpose(mbank[:, c:c + P], padm[:, u, t, :, :].rearrange("p r g -> p (r g)"), ident[:, :])
                last.then_inc(mt_full, 1)

            def turn_ctx(k, m):
                free_bank(m)
                pe.wait_ge(ctx_ready, k + 1)
                for c in range(NC):
                    for t in range(TPS):
                        last = pe.transpose(misc[:, (c * TPS + t) * P:(c * TPS + t + 1) * P], ctx[:, t, c * P:(c + 1) * P], ident[:, :])
                last.then_inc(misc_full, 1)

            def project_out(k, m):
                free_bank(m)
                for t in range(TPS):
                    last = product(misc[:, t * D:(t + 1) * D],
                                   [(cTh[:, c * SEQ + t * P:c * SEQ + (t + 1) * P], cTl[:, c * SEQ + t * P:c * SEQ + (t + 1) * P],
                                     wo[0][:, c * D:(c + 1) * D], wo[1][:, c * D:(c + 1) * D]) for c in range(NC)])
                last.then_inc(misc_full, 1)

            if masked:
                for k in range(SB):
                    pe.matmul(sbank[k][:, P:2 * P], identb[:, :], maskS[:, 2, :], start=True, stop=True)
            for c in range(NS * TPS):
                last = pe.transpose(obank[:, c * P:(c + 1) * P], OT[:, c * P:(c + 1) * P], ident[:, :])
            last.then_inc(ob_full, 1)
            turn(0, lead["T"])
            for k in range(NTL):
                project(0, lead[f"QK{k}"], k)
            values(0, lead["V"])
            turn(1, lead["T1"])
            for g in range(2):
                keys_spread(0, g)
                for j in range(QUAD):
                    score(g, g, j, 0, g * QUAD + j + SB + 1)
            turn_max(0)
            with pe.Fori(0, NSEQ // 2) as i:
                for p in range(2):
                    b = i * 2 + p
                    for g in range(NQ):
                        n = b * NQ + g
                        keys_spread(b if g < 2 else b + 1, (g + 2) % NQ)
                        for j in range(QUAD):
                            score(n + 2, (g + 2) % NQ, j, p if g < 2 else 1 - p, (p * NQ + g) * QUAD + j)
                            score_t(n, g, j, p)
                            if j == cfg["tm"]:
                                turn_max(n + 1)
                            for s in range(TPS):
                                if j == cfg["w"][s]:
                                    weigh(n, (g - 1) % NQ, p if g else 1 - p, s)
                            if j == 3:
                                turn_back(n)
                            name = at.get((g, j), "")
                            if name == "ctxT":
                                turn_ctx(b, use(b, name))
                            elif name == "y":
                                project_out(b, use(b, name))
                            elif name == "T":
                                turn(b + 2, use(b, name))
                            elif name == "V":
                                values(b + 1, use(b, name))
                            elif name.startswith("QK"):
                                project(b + 1, use(b, name), int(name[2:]))
            for s in range(TPS):
                weigh(NSEQ * NQ, 3, 1, s)
            turn_back(NSEQ * NQ)
            turn_ctx(NSEQ, NSEQ * NM + N0)
            project_out(NSEQ, NSEQ * NM + N0 + 1)
    st.close()


def attn_args(kind, a):
    if kind == "diff":
        return {k: a["L0_attn_a_" + n] for k, n in (("wq", "W_q"), ("wk", "W_k"), ("wv", "W_v"), ("wo", "W_o"), ("rms_scale", "rms_scale"),
                                                    ("lambda_q1", "lambda_q1"), ("lambda_k1", "lambda_k1"), ("lambda_q2", "lambda_q2"), ("lambda_k2", "lambda_k2"))}
    if kind == "causal":
        return {k: a["L0_attn_b_" + n] for k, n in (("wq", "Wq"), ("wk", "Wk"), ("wv", "Wv"), ("wo", "Wo"))}
    return {k: a["L1_ffn_" + n] for k, n in (("wq", "wq"), ("wk", "wk"), ("wv", "wv"), ("wo", "wo"), ("norm_w", "norm1_w"))}


def single_head_stage(nc, tag, G, w):
    X, ident = G["X"], G["ident"]
    XS = X[:, :, :].rearrange("p (s t) d -> p s t d", t=TPS)
    S0 = PAD // TPS
    SCALE = float(D) ** -0.5
    st = Stage(nc)
    sb, sem = (lambda n, s, d=F32: st.sb(f"{tag}_{n}", s, d)), (lambda n: st.sem(f"{tag}_{n}"))
    spare = sb("spare", [P, 1])
    epst = sb("epst", [P, 4])
    stats, mv, rs, rs2 = sb("stats", [P, TPS, 6]), sb("mv", [P, TPS, 2]), sb("rs", [P, TPS]), sb("rs2", [P, TPS])
    half = sb("half", [P, TPS])
    xn, xT = sb("xn", [P, TPS, D]), sb("xT", [P, SEQ])
    wq, wk, wv = sb("wq", [D, D]), sb("wk", [D, D]), sb("wv", [D, D])
    bq, bk, bv = sb("bq", [D, 1]), sb("bk", [D, 1]), sb("bv", [P, D])
    QT, KT, V = [sb(f"QT{k}", [P, SEQ]) for k in range(2)], [sb(f"KT{k}", [P, SEQ]) for k in range(2)], [sb(f"V{k}", [P, TPS, D]) for k in range(2)]
    m, nm, rsum, rinv = sb("m", [P, TPS]), sb("nm", [P, TPS]), sb("rsum", [P, TPS]), sb("rinv", [P, TPS])
    Pm, PT = sb("Pm", [P, TPS, SEQ]), sb("PT", [P, TPS, SEQ])
    xb, qkb, vb, scb, ptb, ob = [st.bank(f"{tag}_{n}") for n in ("xb", "qkb", "vb", "scb", "ptb", "ob")]
    w_in, half_set, stat_step, mv_ready, var_ready, rstd_ready, xn_ready = [sem(n) for n in ("w_in", "half_set", "stat_step", "mv_ready", "var_ready", "rstd_ready", "xn_ready")]
    xT_psum, xT_ready, qk_psum, qk_ready, v_psum, v_ready = [sem(n) for n in ("xT_psum", "xT_ready", "qk_psum", "qk_ready", "v_psum", "v_ready")]
    s_psum, m_ready, nm_ready, p_ready, pT_psum, pT_ready, rinv_ready, o_psum, x_done = [sem(n) for n in ("s_psum", "m_ready", "nm_ready", "p_ready", "pT_psum", "pT_ready", "rinv_ready", "o_psum", "x_done")]

    with nc.Block() as block:
        @block.sync
        def _(sp):
            for dst, src in ((wq, w["Wq"]), (wk, w["Wk"]), (wv, w["Wv"])):
                sp.dma_start(dst[:, :], src).then_inc(w_in, 16)
            sp.dma_start(bq[:, :], w["bq"].rearrange("(p a) -> p a", a=1)).then_inc(w_in, 16)
            sp.dma_start(bk[:, :], w["bk"].rearrange("(p a) -> p a", a=1)).then_inc(w_in, 16)
            sp.dma_start(bv[:, :], w["bv"].unsqueeze(0).to_broadcast([P, D])).then_inc(w_in, 16)

        @block.gpsimd
        def _(pool):
            pool.memset(epst[:, :], 1e-5)
            pool.memset(half[:, :], -0.5).then_inc(half_set, 1)
            pool.wait_ge(half_set, 1)

            def root(b):
                pool.wait_ge(mv_ready, b + 1)
                pool.tensor_tensor(rs2[:, :], mv[:, :, 1], epst[:, 0:mv.shape[1]], ALU.add).then_inc(var_ready, 1)
                pool.wait_ge(var_ready, b + 1)
                pool.tensor_tensor(rs[:, :], rs2[:, :], half[:, :], ALU.pow).then_inc(rstd_ready, 1)

            root(0)
            root(1)
            with pool.Fori(0, NSEQ) as b:
                root(b + 2)

        @block.scalar
        def _(act):
            act.wait_ge(w_in, 96)

            def turned(b):
                act.wait_ge(xT_psum, b + 1)
                act.activation(xT[:, :], xb[:, 0:SEQ], ACT.Identity).then_inc(xT_ready, 1)

            def queries_keys(b, q):
                act.wait_ge(qk_psum, b + 1)
                act.activation(QT[q][:, :], qkb[:, 0:SEQ], ACT.Identity, bias=bq[:, :])
                act.activation(KT[q][:, :], qkb[:, SEQ:2 * SEQ], ACT.Identity, bias=bk[:, :]).then_inc(qk_ready, 1)

            turned(0)
            queries_keys(0, 0)
            with act.Fori(0, NSEQ // 2) as i:
                for p in range(2):
                    b = i * 2 + p
                    turned(b + 1)
                    act.wait_ge(nm_ready, b + 1)
                    for t in range(TPS):
                        last = act.activation(Pm[:, t, :], scb[:, t * SEQ:(t + 1) * SEQ], ACT.Exp, bias=nm[:, t:t + 1],
                                              scale=SCALE, accum_out=rsum[:, t:t + 1])
                    last.then_inc(p_ready, 1)
                    queries_keys(b + 1, 1 - p)
                    act.wait_ge(pT_psum, b + 1)
                    act.activation(PT[:, :, :].rearrange("p k q -> p (k q)"), ptb[:, :], ACT.Identity).then_inc(pT_ready, 1)

        @block.vector
        def _(dve):
            dve.memset(spare[:, :], 0.0).then_inc(x_done, 1)
            dve.wait_ge(w_in, 96)

            def norm(b):
                for t in range(TPS):
                    last = dve.bn_stats(stats[:, t, :], XS[:, b + S0, t, :])
                last.then_inc(stat_step, 1)
                dve.wait_ge(stat_step, b + 1)
                dve.memset(spare[:, :], 0.0)
                for t in range(TPS):
                    last = dve.bn_aggr(mv[:, t, :], stats[:, t, :])
                last.then_inc(mv_ready, 1)

            def norm2(b):
                dve.wait_ge(rstd_ready, b + 1)
                for t in range(TPS):
                    last = dve.tensor_scalar(xn[:, t, :], XS[:, b + S0, t, :], mv[:, t, 0:1], rs[:, t:t + 1], ALU.subtract, ALU.mult)
                last.then_inc(xn_ready, 1)

            def values(b, q):
                dve.wait_ge(v_psum, b + 1)
                dve.tensor_tensor(V[q][:, :, :], vb[:, 0:SEQ].rearrange("p (t d) -> p t d", d=D),
                                  bv[:, :].unsqueeze(1).to_broadcast([P, TPS, D]), ALU.add).then_inc(v_ready, 1)

            norm(0)
            norm2(0)
            values(0, 0)
            norm(1)
            norm2(1)
            with dve.Fori(0, NSEQ // 2) as i:
                for p in range(2):
                    b = i * 2 + p
                    dve.wait_ge(s_psum, b + 1)
                    dve.reduce_max(m[:, :], scb[:, :].rearrange("p (t k) -> p t k", t=TPS), AX).then_inc(m_ready, 1)
                    dve.wait_ge(m_ready, b + 1)
                    dve.tensor_scalar(nm[:, :], m[:, :], -SCALE, None, ALU.mult).then_inc(nm_ready, 1)
                    values(b + 1, 1 - p)
                    norm(b + 2)
                    dve.wait_ge(p_ready, b + 1)
                    dve.reciprocal(rinv[:, :], rsum[:, :]).then_inc(rinv_ready, 1)
                    norm2(b + 2)
                    dve.wait_ge(rinv_ready, b + 1)
                    dve.wait_ge(o_psum, b + 1)
                    for t in range(TPS):
                        last = dve.scalar_tensor_tensor(XS[:, b + S0, t, :], ob[:, t * D:(t + 1) * D], rinv[:, t:t + 1], XS[:, b + S0, t, :], ALU.mult, ALU.add)
                    last.then_inc(x_done, 1)

        @block.tensor
        def _(pe):
            pe.wait_ge(w_in, 96)

            def turn(b):
                pe.wait_ge(xn_ready, b + 1)
                for t in range(TPS):
                    last = pe.transpose(xb[:, t * P:(t + 1) * P], xn[:, t, :], ident[:, :])
                last.then_inc(xT_psum, 1)

            def project(b):
                pe.wait_ge(xT_ready, b + 1)
                pe.matmul(qkb[:, 0:SEQ], wq[:, :], xT[:, :], start=True, stop=True)
                pe.matmul(qkb[:, SEQ:], wk[:, :], xT[:, :], start=True, stop=True).then_inc(qk_psum, 1)
                for t in range(TPS):
                    last = pe.matmul(vb[:, t * D:(t + 1) * D], xT[:, t * P:(t + 1) * P], wv[:, :], start=True, stop=True)
                last.then_inc(v_psum, 1)

            turn(0)
            project(0)
            with pe.Fori(0, NSEQ // 2) as i:
                for p in range(2):
                    b = i * 2 + p
                    pe.wait_ge(qk_ready, b + 1)
                    for t in range(TPS):
                        last = pe.matmul(scb[:, t * SEQ:(t + 1) * SEQ], QT[p][:, t * P:(t + 1) * P], KT[p][:, :], start=True, stop=True)
                    last.then_inc(s_psum, 1)
                    turn(b + 1)
                    pe.wait_ge(v_ready, b + 1)
                    project(b + 1)
                    pe.wait_ge(p_ready, b + 1)
                    for s in range(TPS):
                        for t in range(TPS):
                            last = pe.transpose(ptb[:, s * SEQ + t * P:s * SEQ + (t + 1) * P], Pm[:, t, s * P:(s + 1) * P], ident[:, :])
                    last.then_inc(pT_psum, 1)
                    pe.wait_ge(pT_ready, b + 1)
                    pe.wait_ge(x_done, b + 1)
                    for t in range(TPS):
                        for s in range(TPS):
                            last = pe.matmul(ob[:, t * D:(t + 1) * D], PT[:, s, t * P:(t + 1) * P], V[p][:, s, :], start=s == 0, stop=s == TPS - 1)
                    last.then_inc(o_psum, 1)
    st.close()


HID = 192
HC = HID // 2
CONV = 4


def recurrence_in_stage(nc, tag, G, w):
    X, Y, ident, GT, VT = G["X"], G["Y"], G["ident"], G["GT"], G["VT"]
    XB = X[:, :, :].rearrange("p (b t) d -> p b t d", t=TPB)
    YB = Y[:, :, :].rearrange("p (b t) d -> p b t d", t=TPB)
    GB = GT[:, :, :].rearrange("p c (b t) -> p b c t", t=BLK)
    VB = VT[:, :, :, :].rearrange("p c (b s) t -> p b c s t", s=2)
    st = Stage(nc)
    sb, sem = (lambda n, s, d=F32: st.sb(f"{tag}_{n}", s, d)), (lambda n: st.sem(f"{tag}_{n}"))
    spare, credit = sb("spare", [P, 1]), sb("credit", [P, 2])
    epst = sb("epst", [P, 4])
    stats, mv, half = sb("stats", [P, TPB, 6]), sb("mv", [P, TPB, 2]), sb("half", [P, TPB])
    rs, r2, r3, rq = [sb(n, [P, TPB]) for n in ("rs", "r2", "r3", "rq")]
    xn, xT = sb("xn", [P, TPB, D]), sb("xT", [P, BLK])
    win, g1 = sb("win", [D, 4 * HC]), sb("g1", [P, 1])
    xb = st.bank(f"{tag}_xb")
    ub = [st.bank(f"{tag}_u{k}") for k in range(4)]
    w_in, half_set, stat_step, mv_ready, pool_chain, rstd_ready, y_ready, xn_ready = [sem(n) for n in ("w_in", "half_set", "stat_step", "mv_ready", "pool_chain", "rstd_ready", "y_ready", "xn_ready")]
    xT_psum, xT_ready, gate_psum, gate_done, v_psum, v_done, zero_set = [sem(n) for n in ("xT_psum", "xT_ready", "gate_psum", "gate_done", "v_psum", "v_done", "zero_set")]

    with nc.Block() as block:
        @block.sync
        def _(sp):
            sp.dma_start(win[:, :], w["W_in"]).then_inc(w_in, 16)
            sp.dma_start(g1[:, :], w["gamma1"].rearrange("(p a) -> p a", a=1)).then_inc(w_in, 16)

        @block.gpsimd
        def _(pool):
            pool.memset(VT[:, :, :, 0:CONV - 1], 0.0)
            pool.memset(epst[:, :], 1e-5)
            pool.memset(half[:, :], -0.5).then_inc(half_set, 1)
            pool.wait_ge(half_set, 1)

            def root(b):
                pool.wait_ge(mv_ready, b + 1)
                ch = Chain(pool, pool_chain, b * 4)
                ch(pool.tensor_tensor(r2[:, :], mv[:, :, 1], epst[:, 0:mv.shape[1]], ALU.add))
                ch(pool.tensor_tensor(rs[:, :], r2[:, :], half[:, :], ALU.pow))
                ch(pool.tensor_tensor(r3[:, :], rs[:, :], rs[:, :], ALU.mult))
                ch(pool.tensor_tensor(r2[:, :], r3[:, :], mv[:, :, 1], ALU.mult))
                pool.tensor_tensor(rq[:, :], r2[:, :], half[:, :], ALU.pow).then_inc(rstd_ready, 1)

            root(0)
            with pool.Fori(1, NBLK) as b:
                root(b)

        @block.scalar
        def _(act):
            act.wait_ge(w_in, 32)

            def turned(b):
                act.wait_ge(xT_psum, b + 1)
                act.activation(xT[:, :], xb[:, :], ACT.Identity, scale=g1[:, :]).then_inc(xT_ready, 1)

            with act.Fori(0, NBLK) as b:
                turned(b)
                act.wait_ge(gate_psum, b + 1)
                for c in range(2):
                    last = act.activation(GB[:, b, c, :], ub[c][0:HC, :], ACT.Gelu)
                last.then_inc(gate_done, 1)

        @block.vector
        def _(dve):
            def stat(b):
                for t in range(TPB):
                    last = dve.bn_stats(stats[:, t, :], XB[:, b + 1, t, :])
                last.then_inc(stat_step, 1)
                dve.wait_ge(stat_step, b + 1)
                dve.memset(spare[:, :], 0.0)
                for t in range(TPB):
                    last = dve.bn_aggr(mv[:, t, :], stats[:, t, :])
                last.then_inc(mv_ready, 1)

            def norm(b):
                dve.wait_ge(rstd_ready, b + 1)
                for t in range(TPB):
                    last = dve.tensor_scalar(YB[:, b + 1, t, :], XB[:, b + 1, t, :], mv[:, t, 0:1], rs[:, t:t + 1], ALU.subtract, ALU.mult)
                last.then_inc(y_ready, 1)
                dve.wait_ge(y_ready, b + 1)
                for t in range(TPB):
                    last = dve.tensor_scalar(xn[:, t, :], YB[:, b + 1, t, :], rq[:, t:t + 1], None, ALU.mult)
                last.then_inc(xn_ready, 1)

            def take(b):
                dve.wait_ge(v_psum, b + 1)
                for c in range(2):
                    last = dve.tensor_copy(VB[:, b, c, :, CONV - 1:], ub[2 + c][0:HC, :].rearrange("p (s t) -> p s t", s=2))
                last.then_inc(v_done, 1)

            for k, s in enumerate((gate_done, v_done)):
                dve.memset(credit[:, k:k + 1], 0.0).then_inc(s, 1)
            stat(0)
            norm(0)
            with dve.Fori(1, NBLK) as b:
                stat(b)
                dve.wait_ge(xT_psum, b)
                norm(b)
                take(b - 1)
            take(NBLK - 1)

        @block.tensor
        def _(pe):
            pe.wait_ge(w_in, 32)

            with pe.Fori(0, NBLK) as b:
                pe.wait_ge(xn_ready, b + 1)
                for t in range(TPB):
                    last = pe.transpose(xb[:, t * P:(t + 1) * P], xn[:, t, :], ident[:, :])
                last.then_inc(xT_psum, 1)
                pe.wait_ge(xT_ready, b + 1)
                pe.wait_ge(gate_done, b + 1)
                pe.wait_ge(v_done, b + 1)
                for k in range(4):
                    last = pe.matmul(ub[k][0:HC, :], win[:, k * HC:(k + 1) * HC], xT[:, :], start=True, stop=True)
                    if k % 2:
                        last.then_inc((gate_psum, v_psum)[k // 2], 1)
    st.close()


def recurrence_stage(nc, tag, G, w):
    Y, GT, VT = G["Y"], G["GT"], G["VT"]
    YB = Y[:, :, :].rearrange("p (b t) d -> p b t d", t=TPB)
    GB = GT[:, :, :].rearrange("p c (b t) -> p b c t", t=BLK)
    VB = VT[:, :, :, :].rearrange("p c (b s) t -> p b c s t", s=2)
    st = Stage(nc)
    sb, sem = (lambda n, s, d=F32: st.sb(f"{tag}_{n}", s, d)), (lambda n: st.sem(f"{tag}_{n}"))
    wg, wout = sb("wg", [HC, 2, 4 * HC]), sb("wout", [HC, 2, D])
    cw, cb, bg, fb = sb("cw", [HC, 2, CONV]), sb("cb", [HC, 2]), sb("bg", [HC, 4]), sb("fb", [HC, 2])
    nbg, sp_, ca, eps = sb("nbg", [HC, 4]), sb("sp", [HC, 4]), sb("ca", [HC, 2]), sb("eps", [HC, 2])
    vc = [sb(f"vc{k}", [HC, 2, BLK]) for k in range(2)]
    credit = sb("credit", [HC, 6])
    eps2 = sb("eps2", [HC, 1])
    ex, al, be, t1, xg, hh = [sb(n, [HC, 4 if n == "ex" else 2, BLK]) for n in ("ex", "al", "be", "t1", "xg", "hh")]
    gb = [st.bank(f"{tag}_g{k}") for k in range(4)]
    yb = st.bank(f"{tag}_y")
    w_in, prep, vc_step, vc_ready, g_psum, ex_ready, sg_step, sg_ready = [sem(n) for n in ("w_in", "prep", "vc_step", "vc_ready", "g_psum", "ex_ready", "sg_step", "sg_ready")]
    al_ready, one_ready, be_step, be_ready, xi_ready, xg_ready, h_ready, gh_ready, y_psum, y_done = [sem(n) for n in ("al_ready", "one_ready", "be_step", "be_ready", "xi_ready", "xg_ready", "h_ready", "gh_ready", "y_psum", "y_done")]

    with nc.Block() as block:
        @block.sync
        def _(sp):
            sp.dma_start(wg[:, :, :], w["W_gates"].rearrange("(c p) g -> p c g", p=HC)).then_inc(w_in, 16)
            sp.dma_start(wout[:, :, :], w["W_out"].rearrange("(c p) d -> p c d", p=HC)).then_inc(w_in, 16)
            sp.dma_start(cw[:, :, :], w["conv_w"].rearrange("(c p) a k -> p c (a k)", p=HC)).then_inc(w_in, 16)
            for dst, src in ((cb, "conv_b"), (bg, "b_gates"), (fb, "forget_base")):
                sp.dma_start(dst[:, :], w[src].rearrange("(c p) -> p c", p=HC), allow_slow_non_contiguous=True).then_inc(w_in, 16)

        @block.gpsimd
        def _(pool):
            with pool.Fori(0, NBLK) as b:
                pool.wait_ge(sg_ready, b + 1)
                pool.tensor_tensor(xg[:, :, :], ex[:, 2:4, :], vc[0][:, :, :], ALU.mult).then_inc(xi_ready, 1)

        @block.scalar
        def _(act):
            act.wait_ge(prep, 1)
            act.activation(sp_[:, 0:2], fb[:, :], ACT.Abs).then_inc(prep, 1)
            act.wait_ge(prep, 2)
            act.activation(sp_[:, 2:4], sp_[:, 0:2], ACT.Exp, scale=-1.0).then_inc(prep, 1)
            act.wait_ge(prep, 3)
            act.activation(sp_[:, 0:2], sp_[:, 2:4], ACT.Ln, bias=eps[:, 1:2]).then_inc(prep, 1)
            with act.Fori(0, NBLK) as b:
                act.wait_ge(g_psum, b + 1)
                act.wait_ge(xi_ready, b + 1)
                act.wait_ge(al_ready, b * 2 + 1)
                for k in range(4):
                    last = act.activation(ex[:, k, :], gb[k][0:HC, :], ACT.Exp, scale=-1.0, bias=nbg[:, k:k + 1])
                last.then_inc(ex_ready, 1)
                act.wait_ge(sg_ready, b + 1)
                act.wait_ge(h_ready, b + 1)
                for c in range(2):
                    last = act.activation(al[:, c, :], ex[:, c, :], ACT.Exp, scale=ca[:, c:c + 1])
                last.then_inc(al_ready, 1)
                act.wait_ge(al_ready, b * 2 + 2)
                act.activation(t1[:, :, :], al[:, :, :], ACT.Square).then_inc(al_ready, 1)
                act.wait_ge(one_ready, b + 1)
                act.activation(be[:, :, :], t1[:, :, :], ACT.Ln, bias=eps[:, 0:1]).then_inc(be_step, 1)
                act.wait_ge(be_step, b + 1)
                act.activation(t1[:, :, :], be[:, :, :], ACT.Exp, scale=0.5).then_inc(be_ready, 1)

        @block.vector
        def _(dve):
            for k, s in enumerate((xi_ready, h_ready, ex_ready, y_psum, y_done, al_ready)):
                dve.memset(credit[:, k:k + 1], 0.0).then_inc(s, 1)
            dve.memset(eps[:, 0:1], 1e-6)
            dve.memset(eps[:, 1:2], 1.0)
            dve.wait_ge(w_in, 96)
            dve.tensor_scalar(nbg[:, :], bg[:, :], -1.0, None, ALU.mult).then_inc(prep, 1)
            dve.wait_ge(prep, 4)
            dve.tensor_scalar(ca[:, :], fb[:, :], 0.0, None, ALU.max).then_inc(vc_step, 1)
            dve.wait_ge(vc_step, 1)
            dve.tensor_tensor(ca[:, :], ca[:, :], sp_[:, 0:2], ALU.add).then_inc(vc_step, 1)
            dve.wait_ge(vc_step, 2)
            dve.tensor_scalar(ca[:, :], ca[:, :], -8.0, None, ALU.mult).then_inc(vc_step, 1)
            dve.wait_ge(vc_step, 3)

            def conv(b):
                ch = Chain(dve, vc_step, b * 4 + 3)
                out = vc[1][:, :, :].rearrange("p c (s t) -> p c s t", s=2)
                for c in range(2):
                    last = dve.tensor_scalar(out[:, c, :, :], VB[:, b, c, :, 0:SEQ], cw[:, c, 0:1], cb[:, c:c + 1], ALU.mult, ALU.add)
                ch(last)
                for k in range(1, CONV):
                    dst = (vc[0] if k == CONV - 1 else vc[1])[:, :, :].rearrange("p c (s t) -> p c s t", s=2)
                    for c in range(2):
                        last = dve.scalar_tensor_tensor(dst[:, c, :, :], VB[:, b, c, :, k:k + SEQ], cw[:, c, k:k + 1], out[:, c, :, :], ALU.mult, ALU.add)
                    ch(last)
                dve.tensor_copy(eps2[:, 0:1], eps[:, 0:1]).then_inc(vc_ready, 1)

            with dve.Fori(0, NBLK) as b:
                dve.wait_ge(xi_ready, b + 1)
                conv(b)
                dve.wait_ge(ex_ready, b + 2)
                dve.tensor_scalar(ex[:, :, :], ex[:, :, :], 1.0, None, ALU.add).then_inc(sg_step, 1)
                dve.wait_ge(sg_step, b + 1)
                dve.reciprocal(ex[:, :, :], ex[:, :, :]).then_inc(sg_ready, 1)
                dve.wait_ge(al_ready, b * 2 + 3)
                dve.tensor_scalar(t1[:, :, :], t1[:, :, :], -1.0, 1.0, ALU.mult, ALU.add).then_inc(one_ready, 1)
                dve.wait_ge(be_ready, b + 1)
                dve.wait_ge(xi_ready, b + 2)
                dve.tensor_tensor(xg[:, :, :], xg[:, :, :], t1[:, :, :], ALU.mult).then_inc(xg_ready, 1)
                dve.wait_ge(xg_ready, b + 1)
                dve.wait_ge(y_psum, b + 1)
                for c in range(2):
                    for s in range(2):
                        cols = slice(s * SEQ, (s + 1) * SEQ)
                        last = dve.tensor_tensor_scan(hh[:, c, cols], al[:, c, cols], xg[:, c, cols], 0.0, ALU.mult, ALU.add)
                last.then_inc(h_ready, 1)
                dve.wait_ge(h_ready, b + 2)
                dve.tensor_tensor(hh[:, :, :], hh[:, :, :], GB[:, b, :, :], ALU.mult).then_inc(gh_ready, 1)
                dve.wait_ge(y_psum, b + 2)
                dve.tensor_tensor(YB[:, b + 1, :, :], YB[:, b + 1, :, :], yb[:, :].rearrange("p (t d) -> p t d", d=D), ALU.add).then_inc(y_done, 1)

        @block.tensor
        def _(pe):
            pe.wait_ge(w_in, 96)
            with pe.Fori(0, NBLK) as b:
                pe.wait_ge(vc_ready, b + 1)
                pe.wait_ge(ex_ready, b + 1)
                for k in range(4):
                    for c in range(2):
                        last = pe.matmul(gb[k][0:HC, :], wg[:, c, k * HC:(k + 1) * HC], vc[0][:, c, :], start=c == 0, stop=c == 1)
                last.then_inc(g_psum, 1)
                pe.wait_ge(gh_ready, b + 1)
                pe.wait_ge(y_done, b + 1)
                for t in range(TPB):
                    for c in range(2):
                        last = pe.matmul(yb[:, t * D:(t + 1) * D], hh[:, c, t * P:(t + 1) * P], wout[:, c, :], start=c == 0, stop=c == 1)
                last.then_inc(y_psum, 1)
    st.close()


def gated_mlp_stage(nc, tag, G, w):
    X, Y, ident = G["X"], G["Y"], G["ident"]
    XB = X[:, :, :].rearrange("p (b t) d -> p b t d", t=TPB)
    YB = Y[:, :, :].rearrange("p (b t) d -> p b t d", t=TPB)
    st = Stage(nc)
    sb, sem = (lambda n, s, d=F32: st.sb(f"{tag}_{n}", s, d)), (lambda n: st.sem(f"{tag}_{n}"))
    spare, credit = sb("spare", [P, 1]), sb("credit", [P, 2])
    stats, mv, half = sb("stats", [P, TPB, 6]), sb("mv", [P, TPB, 2]), sb("half", [P, TPB])
    rs, r2, r3 = [sb(n, [P, TPB]) for n in ("rs", "r2", "r3")]
    xn, xT = sb("xn", [P, TPB, D]), sb("xT", [P, BLK])
    wgr, wsh, g2 = sb("wgr", [D, 4 * P]), sb("wsh", [P, 2, D]), sb("g2", [P, 1])
    gt, mm = sb("gt", [P, 2, BLK]), sb("mm", [P, 2, BLK])
    xb, ob = st.bank(f"{tag}_xb"), st.bank(f"{tag}_ob")
    ub = [st.bank(f"{tag}_u{k}") for k in range(4)]
    w_in, half_set, stat_step, mv_ready, pool_chain, rstd_ready, xn_ready, x_added = [sem(n) for n in ("w_in", "half_set", "stat_step", "mv_ready", "pool_chain", "rstd_ready", "xn_ready", "x_added")]
    xT_psum, xT_ready, u_psum, gate_ready, m_ready, o_psum, x_done = [sem(n) for n in ("xT_psum", "xT_ready", "u_psum", "gate_ready", "m_ready", "o_psum", "x_done")]

    with nc.Block() as block:
        @block.sync
        def _(sp):
            sp.dma_start(wgr[:, :], w["W_grow"]).then_inc(w_in, 16)
            sp.dma_start(wsh[:, :, :], w["W_shrink"].rearrange("(c p) d -> p c d", p=P)).then_inc(w_in, 16)
            sp.dma_start(g2[:, :], w["gamma2"].rearrange("(p a) -> p a", a=1)).then_inc(w_in, 16)

        @block.gpsimd
        def _(pool):
            pool.memset(half[:, :], -0.5).then_inc(half_set, 1)
            pool.wait_ge(half_set, 1)

            def root(b):
                pool.wait_ge(mv_ready, b + 1)
                ch = Chain(pool, pool_chain, b * 2)
                ch(pool.tensor_tensor(r2[:, :], mv[:, :, 0], mv[:, :, 0], ALU.mult))
                ch(pool.tensor_tensor(r3[:, :], r2[:, :], mv[:, :, 1], ALU.add))
                pool.tensor_tensor(rs[:, :], r3[:, :], half[:, :], ALU.pow).then_inc(rstd_ready, 1)
                pool.tensor_tensor(XB[:, b + 1, :, :], XB[:, b + 1, :, :], YB[:, b + 1, :, :], ALU.add).then_inc(x_added, 1)

            root(0)
            with pool.Fori(1, NBLK) as b:
                root(b)

        @block.scalar
        def _(act):
            act.wait_ge(w_in, 48)
            with act.Fori(0, NBLK) as b:
                act.wait_ge(xT_psum, b + 1)
                act.activation(xT[:, :], xb[:, :], ACT.Identity, scale=g2[:, :]).then_inc(xT_ready, 1)
                act.wait_ge(u_psum, b + 1)
                for c in range(2):
                    last = act.activation(gt[:, c, :], ub[c][:, :], ACT.Gelu)
                last.then_inc(gate_ready, 1)

        @block.vector
        def _(dve):
            def stat(b):
                for t in range(TPB):
                    last = dve.bn_stats(stats[:, t, :], YB[:, b + 1, t, :])
                last.then_inc(stat_step, 1)
                dve.wait_ge(stat_step, b + 1)
                dve.memset(spare[:, :], 0.0)
                for t in range(TPB):
                    last = dve.bn_aggr(mv[:, t, :], stats[:, t, :])
                last.then_inc(mv_ready, 1)

            def norm(b):
                dve.wait_ge(rstd_ready, b + 1)
                for t in range(TPB):
                    last = dve.tensor_scalar(xn[:, t, :], YB[:, b + 1, t, :], rs[:, t:t + 1], None, ALU.mult)
                last.then_inc(xn_ready, 1)

            def gate(b):
                dve.wait_ge(gate_ready, b + 1)
                for c in range(2):
                    last = dve.tensor_tensor(mm[:, c, :], gt[:, c, :], ub[2 + c][:, :], ALU.mult)
                last.then_inc(m_ready, 1)

            def add(b):
                dve.wait_ge(o_psum, b + 1)
                dve.wait_ge(x_added, b + 1)
                dve.tensor_tensor(XB[:, b + 1, :, :], XB[:, b + 1, :, :], ob[:, :].rearrange("p (t d) -> p t d", d=D), ALU.add).then_inc(x_done, 1)

            for k, s in enumerate((m_ready, x_done)):
                dve.memset(credit[:, k:k + 1], 0.0).then_inc(s, 1)
            stat(0)
            norm(0)
            with dve.Fori(1, NBLK) as b:
                stat(b)
                dve.wait_ge(xT_psum, b)
                norm(b)
                gate(b - 1)
                add(b - 1)
            gate(NBLK - 1)
            add(NBLK - 1)

        @block.tensor
        def _(pe):
            pe.wait_ge(w_in, 48)
            with pe.Fori(0, NBLK) as b:
                pe.wait_ge(xn_ready, b + 1)
                for t in range(TPB):
                    last = pe.transpose(xb[:, t * P:(t + 1) * P], xn[:, t, :], ident[:, :])
                last.then_inc(xT_psum, 1)
                pe.wait_ge(xT_ready, b + 1)
                pe.wait_ge(m_ready, b + 1)
                for k in range(4):
                    last = pe.matmul(ub[k][:, :], wgr[:, k * P:(k + 1) * P], xT[:, :], start=True, stop=True)
                last.then_inc(u_psum, 1)
                pe.wait_ge(m_ready, b + 2)
                pe.wait_ge(x_done, b + 1)
                for t in range(TPB):
                    for c in range(2):
                        last = pe.matmul(ob[:, t * D:(t + 1) * D], mm[:, c, t * P:(t + 1) * P], wsh[:, c, :], start=c == 0, stop=c == 1)
                last.then_inc(o_psum, 1)
    st.close()


def recurrence_layer(nc, G, a):
    w = {k: a["L1_attn_b_" + k] for k in ("gamma1", "W_in", "conv_w", "conv_b", "W_gates", "b_gates", "forget_base", "W_out", "gamma2", "W_grow", "W_shrink")}
    with nc.sbuf_tensor("GT", [HC, 2, NSEQ * SEQ], F32) as GT, nc.sbuf_tensor("VT", [HC, 2, NSEQ, CONV - 1 + SEQ], F32) as VT:
        H = G | {"GT": GT, "VT": VT}
        recurrence_in_stage(nc, "RI", H, w)
        recurrence_stage(nc, "RR", H, w)
    gated_mlp_stage(nc, "RM", G, w)


def network(nc, a, out):
    with ExitStack() as ctx:
        G = make_globals(nc, ctx)
        init_globals(nc, G, a["L0_attn_a_X"].rearrange("b s d -> (b s) d"))
        attention_stage(nc, "A1", "diff", G, attn_args("diff", a))
        with ExitStack() as weights:
            weight_memory(nc, weights, G, "L0", 1024)
            load_gelu_experts(nc, "W0", G, a)
            expert_stage(nc, "F1", "gelu", G, gelu_args(a))
            attention_stage(nc, "A2", "causal", G, attn_args("causal", a))
            expert_stage(nc, "F2", "gelu", G, gelu_args(a))
        single_head_stage(nc, "A3", G, {k: a["L1_attn_a_" + k] for k in ("Wq", "bq", "Wk", "bk", "Wv", "bv")})
        weight_memory(nc, ctx, G, "L1", 768)
        load_swiglu_experts(nc, "W1", G, a)
        attention_stage(nc, "A4", "full", G, attn_args("full", a))
        expert_stage(nc, "F3", "swiglu", G, swiglu_args(a))
        recurrence_layer(nc, G, a)
        attention_stage(nc, "A5", "full", G, attn_args("full", a))
        expert_stage(nc, "F4", "swiglu", G, swiglu_args(a))
        store(nc, G, out.rearrange("b s d -> (b s) d"))


_TURNED = ("L0_attn_b_Wq", "L0_attn_b_Wk", "L0_attn_b_Wv", "L0_attn_b_Wo", "L1_attn_a_Wq", "L1_attn_a_Wk", "L1_attn_a_Wv",
           "L1_attn_b_W_in", "L1_attn_b_W_gates", "L1_attn_b_W_out", "L1_attn_b_W_grow", "L1_attn_b_W_shrink")


def kernel(**inputs):
    import numpy as _np
    import concourse.bacc as _bacc
    from concourse import mybir as _mybir
    from concourse.bass_utils import run_bass_kernel_spmd as _run

    nc = _bacc.Bacc("TRN2", target_bir_lowering=False, num_devices=1)
    arrays, args = {}, {}
    for name, a in inputs.items():
        a = _np.asarray(a)
        a = _np.ascontiguousarray(a.T if name in _TURNED else a)
        arrays[f"in_{name}"] = a
        args[name] = nc.dram_tensor(f"in_{name}", a.shape, _mybir.dt.from_np(a.dtype), kind="ExternalInput").ap()
    out = nc.dram_tensor("out", (NSEQ, SEQ, D), F32, kind="ExternalOutput").ap()
    network(nc, args, out)
    r = _run(nc, [arrays], core_ids=[0])
    return r.results[0]["out"]
```

```python
from contextlib import ExitStack

import concourse.bass as bass
from concourse import mybir

F32 = mybir.dt.float32
F32R = mybir.dt.float32r
BF16 = mybir.dt.bfloat16
ALU = mybir.AluOpType
ACT = mybir.ActivationFunctionType
AX = mybir.AxisListType.X

P = 128
D = 128
SEQ = 256
NSEQ = 16
TPS = SEQ // P
BLK = 512
TPB = BLK // P
NBLK = NSEQ * SEQ // BLK
PAD = TPB
NT = NSEQ * TPS + 2 * PAD
E = 8
E_CONST = 2.718281828459045
BIG = 1e30


class Chain:

    def __init__(self, eng, sem, base):
        self.eng, self.sem, self.base, self.n = eng, sem, base, 0

    def __call__(self, ins):
        self.n += 1
        ins.then_inc(self.sem, 1)
        self.eng.wait_ge(self.sem, self.base + self.n)


class Stage:

    def __init__(self, nc):
        self.nc, self.ctx, self.sems = nc, ExitStack(), []

    def sb(self, name, shape, dt=F32):
        return self.ctx.enter_context(self.nc.sbuf_tensor(name, shape, dt))

    def bank(self, name, banks=1):
        return self.ctx.enter_context(self.nc.psum_tensor(name, [P, 512 * banks], F32))

    def sem(self, name):
        s = self.nc.alloc_semaphore(name)
        self.sems.append(s)
        return s

    def close(self):
        self.nc.clear_and_free_semaphores(self.sems)
        self.nc.all_engine_barrier()
        self.ctx.close()


def split_weights(nc, tag, parts, width):
    st = Stage(nc)
    RING = 3
    raw = st.sb(f"{tag}_raw", [P, RING, width])
    loaded = [st.sem(f"{tag}_loaded{k}") for k in range(RING)]
    high_done = st.sem(f"{tag}_high")
    low_done = st.sem(f"{tag}_low")
    with nc.Block() as block:
        @block.sync
        def _(sp):
            for n, (loads, _, _) in enumerate(parts):
                if n >= RING:
                    sp.wait_ge(low_done, n - RING + 1)
                for (c0, c1), src in loads:
                    sp.dma_start(raw[:, n % RING, c0:c1] if len(src.shape) == 2 else
                                 raw[:, n % RING, c0:c1].rearrange("p (a b) -> p a b", a=src.shape[1]),
                                 src).then_inc(loaded[n % RING], 16)

        @block.scalar
        def _(act):
            for n, (loads, high, _) in enumerate(parts):
                act.wait_ge(loaded[n % RING], 16 * len(loads) * (n // RING + 1))
                act.activation(high, raw[:, n % RING, :], ACT.Copy).then_inc(high_done, 1)

        @block.vector
        def _(dve):
            for n, (loads, high, low) in enumerate(parts):
                dve.wait_ge(high_done, n + 1)
                dve.tensor_tensor(low, raw[:, n % RING, :], high.bitcast(F32), ALU.subtract).then_inc(low_done, 1)
    st.close()


def expert_stage(nc, tag, kind, G, w):
    X, ident, WH, WL = G["X"], G["ident"], G["WH"], G["WL"]
    gelu = kind == "gelu"
    SRC = X if gelu else G["Y"]
    EW = 1024 if gelu else 768
    CH = 4 if gelu else 2
    U = (E + 1) * CH
    R = 4 if gelu else 3
    HB = 4 if gelu else 2
    TS = 4
    LAG = 3 if gelu else 2
    XB = X[:, :, :].rearrange("p (b t) d -> p b t d", t=TPB)
    SB_ = SRC[:, :, :].rearrange("p (b t) d -> p b t d", t=TPB)

    st = Stage(nc)
    sb, sem = (lambda n, s, d=F32: st.sb(f"{tag}_{n}", s, d)), (lambda n: st.sem(f"{tag}_{n}"))
    spare, spare2 = sb("spare", [P, 1]), sb("spare2", [P, 1])
    epst = sb("epst", [P, 4])
    stats = sb("stats", [P, TPB, 6])
    mv = sb("mv", [P, TPB, 2])
    rs = sb("rs", [P, TPB])
    rs2 = sb("rs2", [P, TPB])
    xn = sb("xn", [P, TPB, D])
    xT = sb("xT", [P, BLK])
    xh = [sb(f"xh{k}", [P, BLK], F32R) for k in range(2)]
    xl = [sb(f"xl{k}", [P, BLK], F32R) for k in range(2)]
    lg, l2, o1, o2, cc, ex, sel, comb = [sb(n, [P, TPB, E]) for n in ("lg", "l2", "o1", "o2", "cc", "ex", "sel", "comb")]
    r1, r2, r3 = [sb(n, [P, TPB]) for n in ("r1", "r2", "r3")]
    rank = sb("rank", [P, TPB, E])
    econst = sb("econst", [P, TPB, E])
    half = sb("half", [P, TPB])
    gwr = sb("gwr", [P, E])
    gwh = sb("gwh", [P, E], F32R)
    gwl = sb("gwl", [P, E], F32R)
    LOW = 32
    cT = [sb(f"cT{k}", [LOW + E, BLK], F32R) for k in range(2)]
    selr = sb("selr", [LOW + E, E, D])
    selE = sb("selE", [LOW + E, E, D], F32R)
    wbc = sb("wbc", [P, 2, BLK])
    acc = sb("acc", [P, 2, BLK])
    tmp = sb("tmp", [P, TS, BLK])
    credit = sb("credit", [P, 16])
    g32 = sb("g32", [P, R, BLK])
    gh = [sb(f"gh{k}", [P, BLK], F32R) for k in range(R)]
    gl = [sb(f"gl{k}", [P, BLK], F32R) for k in range(R)]
    if gelu:
        b1 = sb("b1", [P, (E + 1) * CH])
        b2 = sb("b2", [P, 1])
        gb = sb("gb", [P, E])
        eb2r = sb("eb2r", [E, D])
        eb2h = sb("eb2h", [LOW + E, D], F32R)
        eb2l = sb("eb2l", [E, D], F32R)
    else:
        s32 = sb("s32", [P, 2, BLK])
        nw = sb("nw", [P, 1])
    hb = [st.bank(f"{tag}_hb{k}", 1 if gelu else 2) for k in range(HB)]
    outb = [st.bank(f"{tag}_out{k}") for k in range(2)]
    misc = st.bank(f"{tag}_misc")
    wbb = st.bank(f"{tag}_wbb")

    started = sem("started")
    consts_in, const_ready, split_ready = sem("consts_in"), sem("const_ready"), sem("split_ready")
    mv_ready, rstd_ready, xn_ready, xadd_done = sem("mv_ready"), sem("rstd_ready"), sem("xn_ready"), sem("xadd_done")
    xT_psum, xT32_ready, xhigh_ready, xT_ready = sem("xT_psum"), sem("xT32_ready"), sem("xhigh_ready"), sem("xT_ready")
    logits_psum, lx_ready, ex_ready, comb_ready = sem("logits_psum"), sem("lx_ready"), sem("ex_ready"), sem("comb_ready")
    combT_psum, chigh_ready, combT_ready = sem("combT_psum"), sem("chigh_ready"), sem("combT_ready")
    prep_chain, pool_chain = sem("prep_chain"), sem("pool_chain")
    h_psum, silu_done, hid_done, hi_done, lo_done, g_free = [sem(n) for n in ("h_psum", "silu_done", "hid_done", "hi_done", "lo_done", "g_free")]
    wb_psum, wb_copied, out_free, acc_step = [sem(n) for n in ("wb_psum", "wb_copied", "out_free", "acc_step")]
    gate_psum, tmp_ready = sem("gate_psum"), sem("tmp_ready")
    fin_psum, fin_done = sem("fin_psum"), sem("fin_done")
    NPREP = 19 if gelu else 20
    NPOOL = 1 if gelu else 3

    with nc.Block() as block:
        @block.sync
        def _(sp):
            sp.dma_start(gwr[:, :], w["gate_w"]).then_inc(consts_in, 16)
            if gelu:
                sp.dma_start(b1[:, 0:CH], w["sh_b1"].rearrange("(c p) -> p c", p=P), allow_slow_non_contiguous=True).then_inc(consts_in, 16)
                sp.dma_start(b1[:, CH:].rearrange("p (e c) -> p e c", e=E), w["eb1"].rearrange("e (c p) -> p e c", p=P), allow_slow_non_contiguous=True).then_inc(consts_in, 16)
                sp.dma_start(b2[:, :], w["sh_b2"].rearrange("(p a) -> p a", a=1)).then_inc(consts_in, 16)
                sp.dma_start(gb[:, :], w["gate_b"].rearrange("(a e) -> a e", a=1).to_broadcast([P, E])).then_inc(consts_in, 16)
                sp.dma_start(eb2r[:, :], w["eb2"]).then_inc(consts_in, 16)
            else:
                sp.dma_start(nw[:, :], w["norm_w"].rearrange("(p a) -> p a", a=1)).then_inc(consts_in, 16)

        NCIN = 16 * (6 if gelu else 2)

        @block.gpsimd
        def _(pool):
            pool.memset(econst[:, :, :], E_CONST)
            pool.memset(epst[:, :], w["eps"])
            pool.memset(half[:, :], -0.5)
            for e in range(E):
                pool.memset(rank[:, :, e:e + 1], float(E - e))
            pool.memset(selr[:, :, :], 0.0).then_inc(const_ready, 1)
            def root(b):
                pool.wait_ge(mv_ready, b + 1)
                ch = Chain(pool, pool_chain, b * NPOOL)
                if gelu:
                    ch(pool.tensor_tensor(rs2[:, :], mv[:, :, 1], epst[:, 0:mv.shape[1]], ALU.add))
                else:
                    ch(pool.tensor_tensor(rs[:, :], mv[:, :, 0], mv[:, :, 0], ALU.mult))
                    ch(pool.tensor_tensor(rs2[:, :], rs[:, :], mv[:, :, 1], ALU.add))
                    ch(pool.tensor_tensor(rs[:, :], rs2[:, :], epst[:, :], ALU.add))
                pool.tensor_tensor(rs[:, :], (rs2 if gelu else rs)[:, :], half[:, :], ALU.pow).then_inc(rstd_ready, 1)
                assert ch.n == NPOOL
                if gelu:
                    pool.wait_ge(xn_ready, b + 1)
                    pool.tensor_tensor(XB[:, b + 1, :, :], XB[:, b + 1, :, :], xn[:, :, :], ALU.add).then_inc(xadd_done, 1)

            def exponentials(b, steps):
                k = 1 if gelu else 2
                for j in steps:
                    pool.wait_ge(lx_ready, b * k + j + 1)
                    pool.tensor_tensor(ex[:, :, :], econst[:, :, :], l2[:, :, :], ALU.pow).then_inc(ex_ready, 1)

            pool.memset(spare2[:, :], 0.0).then_inc(xadd_done, 1)
            pool.wait_ge(const_ready, 1)
            root(0)
            pool.affine_select(out=selr[:, :, :], in_=selr[:, :, :], compare_op=ALU.not_equal, fill=1.0, base=0,
                               pattern=[[-1, E], [0, D]], channel_multiplier=1).then_inc(const_ready, 1)
            pool.wait_ge(const_ready, 2)
            pool.affine_select(out=selr[:, :, :], in_=selr[:, :, :], compare_op=ALU.not_equal, fill=1.0, base=-LOW,
                               pattern=[[-1, E], [0, D]], channel_multiplier=1).then_inc(const_ready, 1)
            def accumulate(b, e, q):
                pool.wait_ge(tmp_ready, b * E + e + 1)
                pool.wait_ge(acc_step, b * E + e + TS)
                pool.tensor_tensor(acc[:, q, :], acc[:, q, :], tmp[:, e % TS, :], ALU.add).then_inc(acc_step, 1)

            with pool.Fori(0, NBLK // 2) as i:
                for p in range(2):
                    b = i * 2 + p
                    accumulate(b - 1, E, 1 - p)
                    root(b + 1)
                    for e in range(1, E):
                        accumulate(b, e, p)
                        if e == (3 if gelu else 2):
                            exponentials(b + 1, [0])
                        if e == 4 and not gelu:
                            exponentials(b + 1, [1])
            accumulate(NBLK - 1, E, 1)

        @block.scalar
        def _(act):
            if not gelu:
                act.wait_ge(consts_in, NCIN)
            act.wait_ge(started, 1)

            def turn(b):
                act.wait_ge(xT_psum, b + 1)
                if gelu:
                    act.activation(xT[:, :], misc[:, :], ACT.Identity).then_inc(xT32_ready, 1)
                else:
                    act.activation(xT[:, :], misc[:, :], ACT.Identity, scale=nw[:, :]).then_inc(xT32_ready, 1)

            def high(b, n):
                act.wait_ge(hid_done, b * U + n + 1 + HB)
                act.wait_ge(g_free, b * U + n + 1)
                act.activation(gh[n % R][:, :], g32[:, n % R, :], ACT.Identity).then_inc(hi_done, 1)

            def spread(b, e):
                act.wait_ge(wb_psum, b * E + e)
                act.wait_ge(out_free, b * (E + 1) + e - 1 + 2)
                act.activation(wbc[:, e % 2, :], wbb[:, :], ACT.Identity).then_inc(wb_copied, 1)

            turn(0)
            if gelu:
                act.wait_ge(consts_in, NCIN)
            for j in range(1 if gelu else 2):
                act.wait_ge(lx_ready, j + 1)
                act.activation(ex[:, :, :], l2[:, :, :], ACT.Exp).then_inc(ex_ready, 1)
            with act.Fori(0, NBLK // 2) as i:
                for p in range(2):
                    b = i * 2 + p
                    for n in range(U):
                        e, c = divmod(n, CH)
                        act.wait_ge(h_psum if gelu else gate_psum, b * U + n + 1)
                        if gelu:
                            act.wait_ge(g_free, b * U + n + 1)
                            act.activation(g32[:, n % R, :], hb[n % HB][:, :], ACT.Gelu_apprx_tanh, bias=b1[:, n:n + 1])
                            act.activation(gh[n % R][:, :], hb[n % HB][:, :], ACT.Gelu_apprx_tanh,
                                           bias=b1[:, n:n + 1]).then_inc(hid_done, 1)
                        else:
                            act.activation(s32[:, n % 2, :], hb[n % HB][:, 0:512], ACT.Silu).then_inc(silu_done, 1)
                            if n >= 1:
                                high(b, n - 1)
                            if c == 1 and e >= 1:
                                spread(b, e)
                        if n == (14 if gelu else 6):
                            turn(b + 1)
                    if not gelu:
                        high(b, U - 1)

        @block.vector
        def _(dve):
            for j, s in enumerate([hid_done] * HB + [g_free] * R + [out_free, wb_copied] + [acc_step] * TS):
                dve.memset(credit[:, j:j + 1], 0.0).then_inc(s, 1)
            dve.memset(outb[1][:, :], 0.0)
            dve.memset(wbc[:, 0, :], 0.0)
            for k in range(2):
                dve.memset(cT[k][:, :].bitcast(F32), 0.0)
            if gelu:
                dve.memset(eb2h[:, :].bitcast(F32), 0.0)
            dve.memset(acc[:, :, :], 0.0).then_inc(started, 1)
            dve.wait_ge(started, 1)
            def stat(b):
                ch = Chain(dve, prep_chain, b * NPREP)
                for t in range(TPB):
                    last = dve.bn_stats(stats[:, t, :], SB_[:, b + 1, t, :])
                ch(last)
                dve.memset(spare[:, :], 0.0)
                for t in range(TPB):
                    last = dve.bn_aggr(mv[:, t, :], stats[:, t, :])
                last.then_inc(mv_ready, 1)

            def norm(b):
                dve.wait_ge(rstd_ready, b + 1)
                for t in range(TPB):
                    if gelu:
                        last = dve.tensor_scalar(xn[:, t, :], SB_[:, b + 1, t, :], mv[:, t, 0:1], rs[:, t:t + 1], ALU.subtract, ALU.mult)
                    else:
                        last = dve.tensor_scalar(xn[:, t, :], SB_[:, b + 1, t, :], rs[:, t:t + 1], None, ALU.mult)
                last.then_inc(xn_ready, 1)

            stat(0)
            norm(0)
            dve.wait_ge(consts_in, NCIN)
            dve.wait_ge(const_ready, 3)
            dve.tensor_copy(gwh[:, :], gwr[:, :])
            dve.tensor_copy(selE[:, :, :], selr[:, :, :]).then_inc(split_ready, 1)
            if gelu:
                dve.tensor_copy(eb2h[0:E, :], eb2r[:, :])
                dve.tensor_copy(eb2h[LOW:LOW + E, :], eb2r[:, :]).then_inc(split_ready, 1)
            dve.wait_ge(split_ready, 2 if gelu else 1)
            dve.tensor_tensor(gwl[:, :], gwr[:, :], gwh[:, :].bitcast(F32), ALU.subtract).then_inc(split_ready, 1)
            if gelu:
                dve.tensor_tensor(eb2l[:, :], eb2r[:, :], eb2h[0:E, :].bitcast(F32), ALU.subtract).then_inc(split_ready, 1)

            def split_x(b, q):
                dve.wait_ge(xT32_ready, b + 1)
                dve.tensor_copy(xh[q][:, :], xT[:, :]).then_inc(xhigh_ready, 1)
                dve.wait_ge(xhigh_ready, b + 1)
                dve.tensor_tensor(xl[q][:, :], xT[:, :], xh[q][:, :].bitcast(F32), ALU.subtract).then_inc(xT_ready, 1)

            def bc(a):
                return a.unsqueeze(2).to_broadcast([P, TPB, E])

            def route1(b, first=1, last=13):
                if first == 1:
                    ch = Chain(dve, prep_chain, b * NPREP + 1)
                    dve.wait_ge(logits_psum, b + 1)
                    lp = misc[:, 0:TPB * E].rearrange("p (t e) -> p t e", e=E)
                    if gelu:
                        ch(dve.tensor_tensor(lg[:, :, :], lp, gb[:, :].unsqueeze(1).to_broadcast([P, TPB, E]), ALU.add))
                    else:
                        ch(dve.tensor_copy(lg[:, :, :], lp))
                    ch(dve.reduce_max(r1[:, :], lg[:, :, :], AX))
                    dve.tensor_tensor(l2[:, :, :], lg[:, :, :], bc(r1[:, :]), ALU.subtract).then_inc(lx_ready, 1)
                    ch(dve.tensor_tensor(cc[:, :, :], lg[:, :, :], bc(r1[:, :]), ALU.is_equal))
                    ch(dve.tensor_tensor(o1[:, :, :], cc[:, :, :], rank[:, :, :], ALU.mult))
                if first <= 5 and last >= 8:
                    ch = Chain(dve, prep_chain, b * NPREP + 5)
                    ch(dve.reduce_max(r2[:, :], o1[:, :, :], AX))
                    ch(dve.tensor_tensor(cc[:, :, :], o1[:, :, :], bc(r2[:, :]), ALU.is_equal))
                    ch(dve.scalar_tensor_tensor(o2[:, :, :], cc[:, :, :], -3e38, lg[:, :, :], ALU.mult, ALU.add))
                    ch(dve.reduce_max(r1[:, :], o2[:, :, :], AX))
                if last == 13:
                    ch = Chain(dve, prep_chain, b * NPREP + 9)
                    ch(dve.tensor_tensor(o1[:, :, :], o2[:, :, :], bc(r1[:, :]), ALU.is_equal))
                    ch(dve.tensor_tensor(o2[:, :, :], o1[:, :, :], rank[:, :, :], ALU.mult))
                    ch(dve.reduce_max(r2[:, :], o2[:, :, :], AX))
                    ch(dve.tensor_tensor(o1[:, :, :], o2[:, :, :], bc(r2[:, :]), ALU.is_equal))
                    ch(dve.tensor_tensor(sel[:, :, :], o1[:, :, :], cc[:, :, :], ALU.add))
                    assert ch.n == 5

            def route2(b):
                ch = Chain(dve, prep_chain, b * NPREP + 14)
                k = 1 if gelu else 2
                dve.wait_ge(ex_ready, b * k + 1)
                ch(dve.reduce_sum(r1[:, :], ex[:, :, :], AX))
                if gelu:
                    ch(dve.tensor_tensor(cc[:, :, :], ex[:, :, :], sel[:, :, :], ALU.mult))
                    ch(dve.reduce_sum(r2[:, :], cc[:, :, :], AX))
                    ch(dve.scalar_tensor_tensor(r3[:, :], r1[:, :], 1e-9, r2[:, :], ALU.mult, ALU.add))
                    ch(dve.reciprocal(r1[:, :], r3[:, :]))
                else:
                    ch(dve.reciprocal(r2[:, :], r1[:, :]))
                    ch(dve.tensor_tensor(cc[:, :, :], ex[:, :, :], bc(r2[:, :]), ALU.mult))
                    dve.tensor_tensor(l2[:, :, :], cc[:, :, :], bc(r2[:, :]), ALU.subtract).then_inc(lx_ready, 1)
                    return
                dve.tensor_tensor(comb[:, :, :], cc[:, :, :], bc(r1[:, :]), ALU.mult).then_inc(comb_ready, 1)
                assert ch.n == NPREP - 14

            def route3(b):
                if not gelu:
                    ch = Chain(dve, prep_chain, b * NPREP + 17)
                    dve.wait_ge(ex_ready, b * 2 + 2)
                    ch(dve.tensor_tensor(cc[:, :, :], ex[:, :, :], sel[:, :, :], ALU.mult))
                    ch(dve.reduce_sum(r2[:, :], cc[:, :, :], AX))
                    ch(dve.reciprocal(r1[:, :], r2[:, :]))
                    dve.tensor_tensor(comb[:, :, :], cc[:, :, :], bc(r1[:, :]), ALU.mult).then_inc(comb_ready, 1)
                    assert ch.n == NPREP - 17

            def split_comb(b, q):
                dve.wait_ge(combT_psum, b + 1)
                dve.tensor_copy(cT[q][0:E, :], misc[0:E, :]).then_inc(chigh_ready, 1)
                dve.wait_ge(chigh_ready, b + 1)
                dve.tensor_tensor(cT[q][LOW:LOW + E, :], misc[0:E, :], cT[q][0:E, :].bitcast(F32), ALU.subtract).then_inc(combT_ready, 1)

            def spread(b, e):
                dve.wait_ge(wb_psum, b * E + e)
                dve.wait_ge(out_free, b * (E + 1) + e - 1 + 2)
                dve.tensor_copy(wbc[:, e % 2, :], wbb[:, :]).then_inc(wb_copied, 1)

            def combine(b, e, q):
                ob = b * (E + 1) + e
                dve.wait_ge(g_free, b * U + (e + 1) * CH + R)
                if e == 0:
                    if gelu:
                        ins = dve.tensor_scalar(acc[:, q, :], outb[(q + e) % 2][:, :], b2[:, :], None, ALU.add)
                    else:
                        ins = dve.tensor_copy(acc[:, q, :], outb[(q + e) % 2][:, :])
                    ins.then_inc(out_free, 1)
                else:
                    dve.wait_ge(acc_step, b * E + e + 1)
                    dve.wait_ge(wb_copied, b * E + e + 1)
                    dve.tensor_tensor(tmp[:, e % TS, :], outb[(q + e) % 2][:, :], wbc[:, e % 2, :], ALU.mult).then_inc(out_free, 1)
                    dve.wait_ge(out_free, ob + 1 + 2)
                    dve.memset(credit[:, 14:15], 0.0).then_inc(tmp_ready, 1)

            def low(b, n):
                dve.wait_ge(hi_done, b * U + n + 1)
                dve.tensor_tensor(gl[n % R][:, :], g32[:, n % R, :], gh[n % R][:, :].bitcast(F32), ALU.subtract).then_inc(lo_done, 1)

            def finish(k):
                dve.wait_ge(fin_psum, k + 1)
                if gelu:
                    dve.wait_ge(xadd_done, k + 1)
                dve.tensor_tensor(XB[:, k, :, :], XB[:, k, :, :], misc[:, :].rearrange("p (t d) -> p t d", d=D), ALU.add).then_inc(fin_done, 1)

            split_x(0, 0)
            route1(0)
            route2(0)
            route3(0)
            split_comb(0, 0)
            with dve.Fori(0, NBLK // 2) as i:
                for p in range(2):
                    b = i * 2 + p
                    for n in range(U):
                        e, c = divmod(n, CH)
                        if gelu:
                            dve.wait_ge(hid_done, b * U + n + 1 + HB)
                            dve.tensor_tensor(gl[n % R][:, :], g32[:, n % R, :], gh[n % R][:, :].bitcast(F32), ALU.subtract).then_inc(lo_done, 1)
                            if c == 2 and e + 1 <= E:
                                spread(b, e + 1)
                            if n == 1:
                                combine(b - 1, E, 1 - p)
                            elif c == 1:
                                combine(b, e - 1, p)
                            step = {7: "finish", 8: "stat", 11: "norm", 15: "split_x", 19: "route1a", 20: "route1b", 23: "route1c", 24: "route2", 29: "split_comb"}.get(n)
                        else:
                            dve.wait_ge(silu_done, b * U + n + 1)
                            dve.wait_ge(h_psum, b * U + n + 1)
                            dve.tensor_tensor(g32[:, n % R, :], s32[:, n % 2, :], hb[n % HB][:, 512:1024], ALU.mult).then_inc(hid_done, 1)
                            if n >= 1:
                                low(b, n - 1)
                            if n == 1:
                                combine(b - 1, E, 1 - p)
                            elif c == 0 and e >= 2:
                                combine(b, e - 2, p)
                            step = {3: "stat", 4: "finish", 5: "norm", 7: "split_x", 9: "route1a", 10: "route1b", 11: "route1c", 13: "route2", 17: "route3"}.get(n)
                        if step == "finish":
                            finish(b)
                        elif step == "stat":
                            stat(b + 1)
                        elif step == "norm":
                            norm(b + 1)
                        elif step == "split_x":
                            split_x(b + 1, 1 - p)
                        elif step == "route2":
                            route2(b + 1)
                        elif step == "split_comb":
                            split_comb(b + 1, 1 - p)
                        elif step == "route1a":
                            route1(b + 1, 1, 4)
                        elif step == "route1b":
                            route1(b + 1, 5, 8)
                        elif step == "route1c":
                            route1(b + 1, 9, 13)
                        elif step == "route3":
                            route3(b + 1)
                    if not gelu:
                        low(b, U - 1)
                        combine(b, E - 1, p)
                        split_comb(b + 1, 1 - p)
            combine(NBLK - 1, E, 1)
            finish(NBLK)

        @block.tensor
        def _(pe):
            pe.wait_ge(started, 1)

            def product(out, pairs, first=True, last=True):
                for k, (sh, sl, mh, ml) in enumerate(pairs):
                    pe.matmul(out, sh, mh, start=first and k == 0, stop=False)
                    pe.matmul(out, sh, ml, start=False, stop=False)
                    ins = pe.matmul(out, sl, mh, start=False, stop=last and k == len(pairs) - 1)
                return ins

            def turn(b):
                pe.wait_ge(xn_ready, b + 1)
                for t in range(TPB):
                    last = pe.transpose(misc[:, t * P:(t + 1) * P], xn[:, t, :], ident[:, :])
                last.then_inc(xT_psum, 1)

            def route(b, q):
                pe.wait_ge(xT_ready, b + 1)
                for t in range(TPB):
                    c = slice(t * P, (t + 1) * P)
                    last = product(misc[:, t * E:(t + 1) * E], [(xh[q][:, c], xl[q][:, c], gwh[:, :], gwl[:, :])])
                last.then_inc(logits_psum, 1)

            def turn_comb(b):
                pe.wait_ge(comb_ready, b + 1)
                for t in range(TPB):
                    last = pe.transpose(misc[0:E, t * P:(t + 1) * P], comb[:, t, :], ident[:, :])
                last.then_inc(combT_psum, 1)

            def first(b, n, q):
                pe.wait_ge(hid_done, b * U + n + 1)
                e, c = divmod(n, CH)
                o = e * EW + c * P
                last = product(hb[n % HB][:, 0:512], [(WH[:, o:o + P], WL[:, o:o + P], xh[q][:, :], xl[q][:, :])])
                if not gelu:
                    last.then_inc(gate_psum, 1)
                    o += CH * P
                    last = product(hb[n % HB][:, 512:1024], [(WH[:, o:o + P], WL[:, o:o + P], xh[q][:, :], xl[q][:, :])])
                last.then_inc(h_psum, 1)

            def second(b, n, q):
                e, c = divmod(n, CH)
                ob = b * (E + 1) + e
                o = outb[(q + e) % 2][:, :]
                if c == 0:
                    pe.wait_ge(out_free, ob + 1)
                pe.wait_ge(lo_done, b * U + n + 1)
                k = e * EW + (EW - CH * P) + c * P
                bias = gelu and e == 0 and c == 0
                if bias:
                    pe.matmul(o, eb2h[:, :], cT[q][:, :], start=True, stop=False)
                    pe.matmul(o, eb2l[:, :], cT[q][0:E, :], start=False, stop=False)
                last = product(o, [(WH[:, k:k + P], WL[:, k:k + P], gh[n % R][:, :], gl[n % R][:, :])],
                               c == 0 and not bias, c == CH - 1)
                last.then_inc(g_free, 1)

            def spread(b, e, q):
                pe.wait_ge(wb_copied, b * E + e)
                if e == 1 and not gelu:
                    pe.wait_ge(combT_ready, b + 1)
                pe.matmul(wbb[:, :], selE[:, e - 1, :], cT[q][:, :], start=True, stop=True).then_inc(wb_psum, 1)

            def finish(k, q):
                pe.wait_ge(acc_step, k * E + 1 + TS)
                for t in range(TPB):
                    last = pe.transpose(misc[:, t * P:(t + 1) * P], acc[:, q, t * P:(t + 1) * P], ident[:, :])
                last.then_inc(fin_psum, 1)

            turn(0)
            pe.wait_ge(split_ready, 4 if gelu else 2)
            route(0, 0)
            for n in range(LAG):
                first(0, n, 0)
            turn_comb(0)
            if gelu:
                pe.wait_ge(combT_ready, 1)
            with pe.Fori(0, NBLK // 2) as i:
                for p in range(2):
                    b = i * 2 + p
                    for n in range(U):
                        e, c = divmod(n, CH)
                        if n + LAG < U:
                            first(b, n + LAG, p)
                        else:
                            first(b + 1, n + LAG - U, 1 - p)
                        second(b, n, p)
                        if c == 0 and e + 1 <= E:
                            spread(b, e + 1, p)
                        step = ({4: "finish", 12: "turn", 17: "route", 26: "turn_comb"} if gelu
                                else {1: "finish", 4: "turn", 7: "route", 16: "turn_comb"}).get(n)
                        if step == "finish":
                            finish(b, 1 - p)
                        elif step == "turn":
                            pe.wait_ge(fin_done, b + 1)
                            turn(b + 1)
                        elif step == "route":
                            route(b + 1, 1 - p)
                        elif step == "turn_comb":
                            turn_comb(b + 1)
                    if gelu:
                        pe.wait_ge(combT_ready, b + 2)
            finish(NBLK, 1)
    st.close()


def make_globals(nc, ctx):
    G = {}
    G["X"] = ctx.enter_context(nc.sbuf_tensor("X", [P, NT, D], F32))
    G["Y"] = ctx.enter_context(nc.sbuf_tensor("Y", [P, NT, D], F32))
    G["ident"] = ctx.enter_context(nc.sbuf_tensor("ident", [P, P], F32))
    return G


def weight_memory(nc, ctx, G, tag, width):
    G["WH"] = ctx.enter_context(nc.sbuf_tensor(f"{tag}_WH", [P, (E + 1) * width], F32R))
    G["WL"] = ctx.enter_context(nc.sbuf_tensor(f"{tag}_WL", [P, (E + 1) * width], F32R))


def init_globals(nc, G, x, y=None):
    st = Stage(nc)
    loaded, cleared = st.sem("init_loaded"), st.sem("init_cleared")
    X, Y, ident = G["X"], G["Y"], G["ident"]
    with nc.Block() as block:
        @block.sync
        def _(sp):
            sp.dma_start(X[:, PAD:NT - PAD, :], x.rearrange("(t p) d -> p t d", p=P)).then_inc(loaded, 16)
            if y is not None:
                sp.dma_start(Y[:, PAD:NT - PAD, :], y.rearrange("(t p) d -> p t d", p=P)).then_inc(loaded, 16)
            sp.wait_ge(loaded, 16 if y is None else 32)

        @block.vector
        def _(dve):
            for T in (X, Y):
                dve.memset(T[:, 0:PAD, :], 0.0)
                dve.memset(T[:, NT - PAD:NT, :], 0.0)

        @block.gpsimd
        def _(pool):
            pool.memset(ident[:, :], 0.0).then_inc(cleared, 1)
            pool.wait_ge(cleared, 1)
            pool.affine_select(out=ident[:, :], in_=ident[:, :], compare_op=ALU.not_equal, fill=1.0, base=0,
                               pattern=[[-1, P]], channel_multiplier=1).then_inc(cleared, 1)
    st.close()


def store(nc, G, out):
    st = Stage(nc)
    stored = st.sem("stored")
    with nc.Block() as block:
        @block.sync
        def _(sp):
            sp.dma_start(out.rearrange("(t p) d -> p t d", p=P), G["X"][:, PAD:NT - PAD, :]).then_inc(stored, 16)
            sp.wait_ge(stored, 16)
    st.close()


def load_gelu_experts(nc, tag, G, a):
    parts = []
    for e in range(E + 1):
        w1 = a["L0_ffn_sh_w1"] if e == 0 else a["L0_ffn_ew1"][e - 1]
        w2 = a["L0_ffn_sh_w2"] if e == 0 else a["L0_ffn_ew2"][e - 1]
        cols = slice(e * 1024, (e + 1) * 1024)
        parts.append(([((0, 512), w1), ((512, 1024), w2.rearrange("(c p) d -> p c d", p=P))],
                      G["WH"][:, cols], G["WL"][:, cols]))
    split_weights(nc, tag, parts, 1024)


def swiglu_expert_parts(a):
    parts = []
    for e in range(E + 1):
        for k, n in enumerate(("gate", "up", "down")):
            src = a[f"L1_ffn_sh_{n}"] if e == 0 else a[f"L1_ffn_e_{n}"][e - 1]
            c0 = e * 768 + k * 256
            parts.append(((c0, c0 + 256), src.rearrange("(c p) d -> p c d", p=P) if n == "down" else src))
    return parts


def gelu_args(a):
    return {k: a[f"L0_ffn_{k}"] for k in ("gate_w", "gate_b", "sh_b1", "eb1", "sh_b2", "eb2")} | {"eps": 1e-5}


def swiglu_args(a):
    return {"gate_w": a["L1_ffn_router_w"], "norm_w": a["L1_ffn_norm2_w"], "eps": 1e-6}


def attention_stage(nc, tag, kind, G, w):
    X, Y, ident = G["X"], G["Y"], G["ident"]
    diff, full, masked = kind == "diff", kind == "full", kind != "full"
    NMAP, QUAD, NQ = 16, 4, 4
    DH, DV = (16, 32) if diff else (8, 8)
    GR = 64 if diff else 32
    NTL = NMAP * GR // P
    HPT = P // GR
    QT = QUAD // HPT
    NV = NMAP // 2 if diff else NMAP
    VW = NV * DV
    NC = VW // P
    OV = DV + 1
    VG = 64 if diff else 32
    NS = 2 if diff else 1
    PW = 384 if masked else 512
    NKU = NTL // 2
    SCALE = float(DH) ** -0.5
    XS = X[:, :, :].rearrange("p (s t) d -> p s t d", t=TPS)
    YS = Y[:, :, :].rearrange("p (s t) d -> p s t d", t=TPS)
    S0 = PAD // TPS

    st = Stage(nc)
    sb, sem = (lambda n, s, d=F32: st.sb(f"{tag}_{n}", s, d)), (lambda n: st.sem(f"{tag}_{n}"))
    spare = sb("spare", [P, 1])
    epst = sb("epst", [P, 4])
    stats, mv = sb("stats", [P, TPS, 6]), sb("mv", [P, TPS, 2])
    rs, rs2, rs3 = sb("rs", [P, TPS]), sb("rs2", [P, TPS]), sb("rs3", [P, TPS])
    half, epsr = sb("half", [P, 32]), sb("epsr", [P, TPS])
    nil, inv_dv, eps_dv = sb("nil", [P, TPS * QUAD]), sb("inv_dv", [P, 16]), sb("eps_dv", [P, 16])
    xn = sb("xn", [P, TPS, D])
    xh, xl = sb("xh", [P, SEQ], F32R), sb("xl", [P, SEQ], F32R)
    hi2 = [sb(f"hi2_{k}", [P, 512], F32R) for k in range(2)]
    Q1 = [sb(f"Q1_{k}", [P, NTL * SEQ], F32R) for k in range(2)]
    kst = [sb(f"kst{k}", [P, 512], F32R) for k in range(2)]
    KB = [sb(f"KB_{k}", [P, HPT, NTL * SEQ], F32R) for k in range(2)]
    Q2 = [sb(f"Q2_{k}", [P, QT * SEQ], F32R) for k in range(2)]
    V = [sb(f"V_{k}", [P, TPS, NV, VG]) for k in range(2)]
    Pm = [sb(f"Pm{k}", [P, QUAD, PW]) for k in range(2)]
    OT = sb("OT", [P, NS * SEQ])
    mx = [sb(f"mx{k}", [P, TPS, QUAD]) for k in range(2)]
    mh = sb("mh", [P, TPS, QUAD], F32R)
    padm = sb("padm", [P, QT, TPS, HPT, GR])
    O = sb("O", [P, TPS, NMAP, OV])
    rec = sb("rec", [P, TPS, NMAP])
    ctx = sb("ctx", [P, TPS, VW])
    cTh, cTl = sb("cTh", [P, NC * SEQ], F32R), sb("cTl", [P, NC * SEQ], F32R)
    credit = sb("credit", [P, 16])
    if diff:
        T2 = sb("T2", [P, TPS, NMAP, DV])
        Dd = sb("Dd", [P, TPS, NV, DV])
        ss, sm, sm2, rr = [sb(n, [P, TPS * NV]) for n in ("ss", "sm", "sm2", "rr")]
        lamr = sb("lamr", [P, 4, NV * DH])
        lamp = sb("lamp", [P, 2, NV * DH])
        lams, lame, econst = sb("lams", [P, 2 * NV]), sb("lame", [P, 2 * NV]), sb("econst", [P, 2 * NV])
        wmap = sb("wmap", [P, NV, 2])
    raw = sb("raw", [P, 2 * NMAP * DH + VW + NC * D])
    wqk = [[sb(f"w{n}{k}", [P, NTL * P], F32R) for k in "hl"] for n in "qk"]
    wv = [sb(f"wv{k}", [P, VW], F32R) for k in "hl"]
    wo = [sb(f"wo{k}", [P, NC * D], F32R) for k in "hl"]
    rows = sb("rows", [P, 3, HPT])
    rvec = sb("rvec", [P, 3])
    colc = sb("colc", [P, 3])
    insc = sb("insc", [P, 1])
    outsc = sb("outsc", [P, 1])
    if masked:
        mf = Pm[0][:, :, :].rearrange("p j k -> p (j k)")[:, 0:5 * P].rearrange("p (c k) -> p c k", k=P)
        identb, maskS, maskT = sb("identb", [P, P], BF16), sb("maskS", [P, 3, P], BF16), sb("maskT", [P, 2, P], BF16)
    SB = 2
    sbank = [st.bank(f"{tag}_s{k}") for k in range(SB)]
    tbank = [st.bank(f"{tag}_t{k}") for k in range(2)]
    shared = [st.bank(f"{tag}_misc{k}") for k in range(2)]
    mbank, obank = st.bank(f"{tag}_mt"), st.bank(f"{tag}_ot")

    w_in, c_pool, w_step, started = sem("w_in"), sem("c_pool"), sem("w_step"), sem("started")
    mv_ready, rstd_ready, xhat_ready, xn_ready, xhigh = [sem(n) for n in ("mv_ready", "rstd_ready", "xhat_ready", "xn_ready", "xhigh")]
    misc_full, misc_read = sem("misc_full"), sem("misc_read")
    qk_high = sem("qk_high")
    s_psum, s_free, m_ready, pool_chain = sem("s_psum"), sem("s_free"), sem("m_ready"), sem("pool_chain")
    t_psum, t_free, p_used, o_free = sem("t_psum"), sem("t_free"), sem("p_used"), sem("o_free")
    ot_read, ob_full, mt_full, mt_read = sem("ot_read"), sem("ob_full"), sem("mt_full"), sem("mt_read")
    o_set, cleared = sem("o_set"), sem("cleared")
    k_spread = [sem(f"k_spread{k}") for k in range(2)]
    norm_chain, ss_ready, rr_ready, ctx_ready = sem("norm_chain"), sem("ss_ready"), sem("rr_ready"), sem("ctx_ready")
    chigh = sem("chigh")
    m_high, ss_mean, stat_step = sem("m_high"), sem("ss_mean"), sem("stat_step")

    QK = [f"QK{k}" for k in range(NTL)]
    pos = lambda x: (x // QUAD, x % QUAD)
    if diff:
        when = dict(projections=[0, 1, 2, 4, 6, 8, 9, 10], turn=14, turn_context=13, output=15, values=11, reciprocals=5, weights=6,
                    difference=7, square_sums=8, context=11, split_context=14, stat=0, norm=12,
                    norm2=13, stack_lag=1, turn_maxima=1, weigh=[2, 2], with_maxima=2, products=2)
    else:
        when = dict(projections=[0, 1, 4, 6], turn=14, turn_context=8, output=10, values=12, reciprocals=5,
                    weights=6, split_context=9, norm=10, norm2=13, stat=4, stack_lag=1, turn_maxima=1,
                    weigh=[1, 2], with_maxima=1, products=2)
    at = dict(zip([pos(x) for x in when["projections"]], QK)) | {pos(when["turn"]): "T", pos(when["turn_context"]): "ctxT", pos(when["output"]): "y", pos(when["values"]): "V"}
    before = ["T"] + QK + ["V", "T1"]
    order = [at[key] for key in sorted(at)]
    NM, N0 = len(order), len(before)
    lead = {n: k for k, n in enumerate(before)}

    def use(b, name):
        return b * NM + N0 + order.index(name)

    bank_of = {n: shared[(N0 + k) % 2] for k, n in enumerate(order)}
    lead_bank = {n: shared[k % 2] for k, n in enumerate(before)}
    assert NM % 2 == 0

    KDMA = 16 * HPT * NKU // 2
    NROOT = 5 if full else 1
    NNORM = 5 if diff else 1

    with nc.Block() as block:
        @block.sync
        def _(sp):
            n = NMAP * DH
            sp.dma_start(raw[:, 0:n], w["wq"]).then_inc(w_in, 16)
            sp.dma_start(raw[:, n:2 * n], w["wk"]).then_inc(w_in, 16)
            sp.dma_start(raw[:, 2 * n:2 * n + VW], w["wv"]).then_inc(w_in, 16)
            sp.dma_start(raw[:, 2 * n + VW:].rearrange("p (c d) -> p c d", d=D), w["wo"].rearrange("(c p) d -> p c d", p=P)).then_inc(w_in, 16)
            if diff:
                for k, name in enumerate(("lambda_q1", "lambda_q2", "lambda_k1", "lambda_k2")):
                    sp.dma_start(lamr[:, k, :], w[name].rearrange("h d -> (h d)").unsqueeze(0).to_broadcast([P, NV * DH])).then_inc(w_in, 16)
                for k in range(P // DV):
                    sp.dma_start(outsc[k * DV:(k + 1) * DV, :], w["rms_scale"].rearrange("(p a) -> p a", a=1)).then_inc(w_in, 16)
            if full:
                sp.dma_start(insc[:, :], w["norm_w"].rearrange("(p a) -> p a", a=1)).then_inc(w_in, 16)

            def spread(m, k, q):
                sp.wait_ge(misc_read, m + 1)
                for r in range(HPT):
                    sp.dma_start(KB[q][r * GR:(r + 1) * GR, r, k * 512:(k + 1) * 512].bitcast(F32), kst[k % 2][r * GR:(r + 1) * GR, :].bitcast(F32)).then_inc(k_spread[k % 2], 16)

            sp.wait_ge(cleared, 1)
            for k in range(NKU):
                spread(lead[f"QK{2 * k + 1}"], k, 0)
            sp.wait_ge(cleared, 2)
            with sp.Fori(0, NSEQ // 2) as i:
                for p in range(2):
                    for k in range(NKU):
                        spread(use(i * 2 + p, f"QK{2 * k + 1}"), k, 1 - p)
            for k in range(2):
                sp.wait_ge(k_spread[k], (NSEQ + 1) * KDMA)

        NWIN = 16 * (4 + (4 + P // DV if diff else 0) + (1 if full else 0))

        @block.gpsimd
        def _(pool):
            def root(b):
                pool.wait_ge(mv_ready, b + 1)
                ch = Chain(pool, pool_chain, b * NROOT)
                ch(pool.tensor_tensor(rs2[:, :], mv[:, :, 1], epst[:, 0:mv.shape[1]], ALU.add))
                last = pool.tensor_tensor(rs[:, :], rs2[:, :], half[:, 0:TPS], ALU.pow)
                if full:
                    ch(last)
                    ch(pool.tensor_tensor(rs2[:, :], rs[:, :], rs[:, :], ALU.mult))
                    ch(pool.tensor_tensor(rs3[:, :], rs2[:, :], mv[:, :, 1], ALU.mult))
                    ch(pool.tensor_tensor(rs2[:, :], rs3[:, :], epsr[:, :], ALU.add))
                    last = pool.tensor_tensor(rs3[:, :], rs2[:, :], half[:, 0:TPS], ALU.pow)
                last.then_inc(rstd_ready, 1)

            pool.memset(epst[:, :], 1e-5)
            pool.memset(half[:, :], -0.5)
            pool.memset(padm[:, :, :, :, :], 0.0)
            pool.memset(epsr[:, :], 1e-6)
            pool.memset(nil[:, :], 0.0)
            pool.memset(inv_dv[:, :], 1.0 / DV)
            pool.memset(eps_dv[:, :], 1e-5)
            pool.memset(rows[:, :, :], -1.0)
            if diff:
                pool.memset(econst[:, :], E_CONST)
            if masked:
                pool.memset(mf[:, 0:2, :], 0.0)
                pool.memset(mf[:, 3:5, :], 0.0)
                pool.memset(mf[:, 2:3, :], -BIG)
            pool.memset(credit[:, 15:16], 0.0).then_inc(c_pool, 1)
            pool.wait_ge(c_pool, 1)
            for k, (a, z) in enumerate(((DH, 2 * DH), (2 * DH, 3 * DH), (3 * DH, 3 * DH + 2))):
                pool.affine_select(out=rows[:, k, :], in_=rows[:, k, :], compare_op=ALU.is_ge, fill=0.0, base=-a,
                                   pattern=[[-GR, HPT]], channel_multiplier=1).then_inc(c_pool, 1)
            pool.wait_ge(c_pool, 4)
            for k, (a, z) in enumerate(((DH, 2 * DH), (2 * DH, 3 * DH), (3 * DH, 3 * DH + 2))):
                pool.affine_select(out=rows[:, k, :], in_=rows[:, k, :], compare_op=ALU.is_ge, fill=0.0, base=z - 1,
                                   pattern=[[GR, HPT]], channel_multiplier=-1)
            if masked:
                pool.affine_select(out=mf[:, 0:2, :], in_=mf[:, 0:2, :],
                                   compare_op=ALU.is_ge, fill=-BIG, base=0, pattern=[[0, 2], [-1, P]], channel_multiplier=1)
                pool.affine_select(out=mf[:, 3:5, :], in_=mf[:, 3:5, :],
                                   compare_op=ALU.is_ge, fill=-BIG, base=0, pattern=[[0, 2], [1, P]], channel_multiplier=-1)
            pool.memset(credit[:, 14:15], 0.0).then_inc(c_pool, 1)
            pool.wait_ge(c_pool, 5)
            root(0)
            pool.memset(KB[0][:, :, :].bitcast(F32), 0.0).then_inc(cleared, 1)
            pool.memset(KB[1][:, :, :].bitcast(F32), 0.0)
            pool.memset(Pm[1][:, :, :], 1.0).then_inc(cleared, 1)
            if diff:
                pool.wait_ge(w_step, 4)
                pool.tensor_tensor(lame[:, :], econst[:, :], lams[:, :], ALU.pow).then_inc(c_pool, 1)
            pool.wait_ge(started, 1)

            def maxima(q, r):
                pool.wait_ge(s_free, SB + (q + 1) * QUAD)
                pool.wait_ge(mt_full, q + 1)
                pool.tensor_tensor(mh[:, :, :], mx[r][:, :, :], nil[:, :].rearrange("p (t j) -> p t j", t=TPS), ALU.add).then_inc(m_high, 1)
                pool.wait_ge(m_high, q + 1)
                src = mh[:, :, :].bitcast(F32).rearrange("p q (t r) -> p t q r", r=HPT)
                raw_m = mx[r][:, :, :].rearrange("p q (t r) -> p t q r", r=HPT)
                pool.tensor_tensor(padm[:, :, :, :, 3 * DH], src, nil[:, :].rearrange("p (t q r) -> p t q r", t=QT, q=TPS), ALU.add)
                pool.tensor_tensor(padm[:, :, :, :, 3 * DH + 1], raw_m, src, ALU.subtract).then_inc(m_ready, 1)

            def head_root(k):
                pool.wait_ge(ss_ready, k + 1)
                pool.tensor_tensor(sm[:, :], ss[:, :], inv_dv[:, :], ALU.mult).then_inc(ss_mean, 1)
                pool.wait_ge(ss_mean, k * 2 + 1)
                pool.tensor_tensor(sm2[:, :], sm[:, :], eps_dv[:, :], ALU.add).then_inc(ss_mean, 1)
                pool.wait_ge(ss_mean, k * 2 + 2)
                pool.tensor_tensor(rr[:, :], sm2[:, :], half[:, 0:TPS * NV], ALU.pow).then_inc(rr_ready, 1)

            root(1)
            maxima(0, 0)
            with pool.Fori(0, NSEQ) as b:
                for g in range(NQ):
                    maxima(b * NQ + g + 1, (g + 1) % 2)
                    if g == 1:
                        root(b + 2)
                    elif g == 2 and diff:
                        head_root(b)
                if full:
                    pool.wait_ge(misc_read, use(b, "y") + 1)
                    pool.tensor_tensor(XS[:, b + S0 - 1, :, :], XS[:, b + S0 - 1, :, :], YS[:, b + S0 - 1, :, :], ALU.add)
            if diff:
                head_root(NSEQ)
            if full:
                pool.wait_ge(misc_read, NSEQ * NM + N0 + 2)
                pool.tensor_tensor(XS[:, NSEQ + S0 - 1, :, :], XS[:, NSEQ + S0 - 1, :, :], YS[:, NSEQ + S0 - 1, :, :], ALU.add)

        @block.scalar
        def _(act):
            act.wait_ge(started, 1)

            def turned(m, misc):
                act.wait_ge(misc_full, m + 1)
                act.activation(xh[:, :], misc[:, 0:SEQ], ACT.Identity, scale=insc[:, :] if full else 1.0).then_inc(xhigh, 1)

            def high(m, k, misc):
                act.wait_ge(misc_full, m + 1)
                if k % 2:
                    act.activation(hi2[k % 2][:, :], misc[:, :], ACT.Identity, bias=colc[:, 2:3]).then_inc(qk_high, 1)
                else:
                    act.activation(hi2[k % 2][:, :], misc[:, :], ACT.Identity).then_inc(qk_high, 1)

            def values(m, q, misc):
                act.wait_ge(misc_full, m + 1)
                act.wait_ge(misc_read, m)
                act.activation(V[q][:, :, :, 0:DV], misc[:, 0:TPS * VW].rearrange("p (t h d) -> p t h d", t=TPS, d=DV),
                               ACT.Identity).then_inc(misc_read, 1)

            def exp(n, j, r):
                act.wait_ge(t_psum, n * QUAD + j + 1)
                if j == 0:
                    act.wait_ge(p_used, n + 1)
                act.activation(Pm[r][:, j, :], tbank[j % 2][:, 0:PW], ACT.Exp, scale=SCALE).then_inc(t_free, 1)

            def products(n):
                act.wait_ge(p_used, n + 2)
                act.wait_ge(ob_full, n + 1)
                act.activation(OT[:, :], obank[:, 0:NS * SEQ], ACT.Identity).then_inc(ot_read, 1)

            def context(n, g, k):
                act.wait_ge(ob_full, n + 1)
                if g == 0:
                    act.wait_ge(norm_chain, k * NNORM + 4) if diff else act.wait_ge(ctx_ready, k + 1)
                for s in range(NS):
                    last = act.activation(O[:, :, g * QUAD:(g + 1) * QUAD, :].rearrange("p t (h s) d -> p s t h d", s=NS)[:, s],
                                          obank[:, s * SEQ:(s + 1) * SEQ].rearrange("p (t h d) -> p t h d", t=TPS, d=VG)[:, :, :, 0:OV],
                                          ACT.Identity)
                last.then_inc(o_free, 1)

            def ctx_turned(m, misc):
                act.wait_ge(misc_full, m + 1)
                act.activation(cTh[:, :], misc[:, 0:NC * SEQ], ACT.Identity, scale=outsc[:, :] if diff else 1.0).then_inc(chigh, 1)

            turned(lead["T"], lead_bank["T"])
            for k in range(NTL):
                high(lead[f"QK{k}"], k, lead_bank[f"QK{k}"])
            values(lead["V"], 0, lead_bank["V"])
            turned(lead["T1"], lead_bank["T1"])
            with act.Fori(0, NSEQ // 2) as i:
                for p in range(2):
                    b = i * 2 + p
                    for g in range(NQ):
                        gq = b * NQ + g
                        for j in range(QUAD):
                            exp(gq, j, g % 2)
                            if j == 0:
                                context(gq, (g + 2) % 4, b)
                            elif j == when["products"]:
                                products(gq)
                            name = at.get((g, j), "")
                            if name == "T":
                                turned(use(b, name), bank_of[name])
                            elif name == "ctxT":
                                ctx_turned(use(b, name), bank_of[name])
                            elif name == "V":
                                values(use(b, name), 1 - p, bank_of[name])
                            elif name.startswith("QK"):
                                high(use(b, name), int(name[2:]), bank_of[name])
            context(NSEQ * NQ, 2, None)
            products(NSEQ * NQ)
            context(NSEQ * NQ + 1, 3, None)
            ctx_turned(NSEQ * NM + N0, shared[N0 % 2])

        @block.vector
        def _(dve):
            for j, s in enumerate([s_free] * SB + [t_free] * 2 + [p_used, o_free, ot_read, mt_full, mt_read]):
                dve.memset(credit[:, j:j + 1], 0.0).then_inc(s, 1)
            def counted(m):
                if not isinstance(m, int) or m > 0:
                    dve.wait_ge(misc_read, m)

            def stat(b):
                for t in range(TPS):
                    last = dve.bn_stats(stats[:, t, :], XS[:, b + S0, t, :])
                last.then_inc(stat_step, 1)
                dve.wait_ge(stat_step, b + 1)
                dve.memset(spare[:, :], 0.0)
                for t in range(TPS):
                    last = dve.bn_aggr(mv[:, t, :], stats[:, t, :])
                last.then_inc(mv_ready, 1)

            def norm(b):
                dve.wait_ge(rstd_ready, b + 1)
                for t in range(TPS):
                    last = dve.tensor_scalar(YS[:, b + S0, t, :] if full else xn[:, t, :], XS[:, b + S0, t, :], mv[:, t, 0:1], rs[:, t:t + 1], ALU.subtract, ALU.mult)
                last.then_inc(xhat_ready if full else xn_ready, 1)

            def norm2(b):
                if full:
                    dve.wait_ge(xhat_ready, b + 1)
                    for t in range(TPS):
                        last = dve.tensor_scalar(xn[:, t, :], YS[:, b + S0, t, :], rs3[:, t:t + 1], None, ALU.mult)
                    last.then_inc(xn_ready, 1)

            stat(0)
            for k in range(2):
                dve.memset(V[k][:, :, :, DV:VG], 0.0)
            dve.memset(V[1][:, :, :, 0:DV], 0.0).then_inc(o_set, 1)
            dve.memset(O[:, :, :, :], 1.0)
            dve.memset(OT[:, :], 1.0)
            dve.wait_ge(o_set, 1)
            for k in range(2):
                dve.memset(V[k][:, :, :, DV:OV], 1.0)
            for n in range(2):
                for k in range(2):
                    dve.memset(wqk[n][k][:, :].bitcast(F32).rearrange("p (h g) -> p h g", g=GR)[:, :, 3 * DH:], 0.0)
            norm(0)
            norm2(0)
            dve.wait_ge(w_in, NWIN)
            dve.wait_ge(c_pool, 5)
            if masked:
                dve.tensor_copy(identb[:, :], ident[:, :])
                dve.tensor_copy(maskS[:, :, :], mf[:, 0:3, :])
                dve.tensor_copy(maskT[:, :, :], mf[:, 3:5, :])
            dve.tensor_copy(wv[0][:, :], raw[:, 2 * NMAP * DH:2 * NMAP * DH + VW])
            dve.tensor_copy(wo[0][:, :], raw[:, 2 * NMAP * DH + VW:])
            dve.reduce_sum(rvec[:, :], rows[:, :, :], AX).then_inc(w_step, 1)
            dve.wait_ge(w_step, 1)
            for n in range(2):
                src = raw[:, n * NMAP * DH:(n + 1) * NMAP * DH].rearrange("p (h d) -> p h d", d=DH)
                for rep in range(3):
                    last = dve.tensor_copy(wqk[n][0][:, :].rearrange("p (h g) -> p h g", g=GR)[:, :, rep * DH:(rep + 1) * DH], src)
            last.then_inc(w_step, 1)
            dve.wait_ge(w_step, 2)
            for n in range(2):
                src = raw[:, n * NMAP * DH:(n + 1) * NMAP * DH].rearrange("p (h d) -> p h d", d=DH)
                for rep in range(3):
                    sl = (slice(None), slice(None), slice(rep * DH, (rep + 1) * DH))
                    dve.tensor_tensor(wqk[n][1][:, :].rearrange("p (h g) -> p h g", g=GR)[sl], src,
                                      wqk[n][0][:, :].bitcast(F32).rearrange("p (h g) -> p h g", g=GR)[sl], ALU.subtract)
            dve.tensor_tensor(wv[1][:, :], raw[:, 2 * NMAP * DH:2 * NMAP * DH + VW], wv[0][:, :].bitcast(F32), ALU.subtract)
            dve.tensor_tensor(wo[1][:, :], raw[:, 2 * NMAP * DH + VW:], wo[0][:, :].bitcast(F32), ALU.subtract)
            dve.tensor_copy(colc[:, 0:1], rvec[:, 0:1])
            dve.tensor_tensor(colc[:, 1:2], rvec[:, 1:2], rvec[:, 2:3], ALU.subtract)
            dve.tensor_copy(colc[:, 2:3], rvec[:, 2:3])
            if diff:
                dve.tensor_tensor(lamp[:, :, :], lamr[:, 0:2, :], lamr[:, 2:4, :], ALU.mult).then_inc(w_step, 1)
                dve.wait_ge(w_step, 3)
                dve.reduce_sum(lams[:, :], lamp[:, :, :].rearrange("p a (h d) -> p (a h) d", d=DH), AX).then_inc(w_step, 1)
                dve.memset(wmap[:, :, 0:1], 1.0)
                dve.wait_ge(c_pool, 6)
                dve.tensor_tensor(lamp[:, 0, 0:NV], lame[:, NV:2 * NV], lame[:, 0:NV], ALU.subtract).then_inc(w_step, 1)
                dve.wait_ge(w_step, 5)
                dve.tensor_scalar(wmap[:, :, 1], lamp[:, 0, 0:NV], 0.8, None, ALU.subtract)
                dve.tensor_scalar(outsc[:, :], outsc[:, :], 1.0 - 0.8, None, ALU.mult)
            dve.memset(credit[:, 13:14], 0.0).then_inc(started, 1)
            dve.wait_ge(started, 1)

            def split_x(b, m, misc):
                counted(m)
                dve.wait_ge(xhigh, b + 1)
                if full:
                    last = dve.scalar_tensor_tensor(xl[:, :], misc[:, 0:SEQ], insc[:, :], xh[:, :].bitcast(F32), ALU.mult, ALU.subtract)
                else:
                    last = dve.tensor_tensor(xl[:, :], misc[:, 0:SEQ], xh[:, :].bitcast(F32), ALU.subtract)
                last.then_inc(misc_read, 1)

            def stack(b, m, k, q, misc, lead_in=False):
                dve.wait_ge(qk_high, b * NTL + k + 1)
                counted(m)
                n, c = k % 2, slice((k // 2) * 512, (k // 2 + 1) * 512)
                if n:
                    u = k // 2
                    if u >= 2 or not lead_in:
                        dve.wait_ge(k_spread[u % 2], b * KDMA + u // 2 * 16 * HPT)
                    dve.scalar_tensor_tensor(kst[u % 2][:, :], hi2[k % 2][:, :].bitcast(F32), colc[:, 1:2], misc[:, :], ALU.mult, ALU.add).then_inc(misc_read, 1)
                else:
                    dve.scalar_tensor_tensor(Q1[q][:, c], hi2[k % 2][:, :].bitcast(F32), colc[:, 0:1], misc[:, :], ALU.mult, ALU.add).then_inc(misc_read, 1)

            def top(n, j, r, use_, lead_in=False):
                dve.wait_ge(s_psum, n * QUAD + j + 1)
                if j == 0 and not lead_in:
                    dve.wait_ge(m_ready, n - 1)
                dve.reduce_max(mx[r][:, :, j], sbank[use_ % SB][:, :].rearrange("p (t k) -> p t k", t=TPS), AX).then_inc(s_free, 1)

            def with_max(n, g, q):
                dve.wait_ge(mt_full, n + 2)
                c = slice(g * QT * SEQ, (g + 1) * QT * SEQ)
                dve.tensor_tensor(Q2[g % 2][:, :], Q1[q][:, c].bitcast(F32), mbank[:, 0:QT * SEQ], ALU.add).then_inc(mt_read, 1)

            def reciprocals(k):
                dve.wait_ge(o_free, 3 + k * NQ)
                dve.reciprocal(rec[:, :, :], O[:, :, :, DV]).then_inc(norm_chain, 1)

            def weights(k):
                dve.wait_ge(norm_chain, k * NNORM + 1)
                dve.tensor_tensor(rec[:, :, :], rec[:, :, :], wmap[:, :, :].rearrange("p h s -> p (h s)").unsqueeze(1).to_broadcast([P, TPS, NMAP]), ALU.mult).then_inc(norm_chain, 1)
                dve.wait_ge(norm_chain, k * NNORM + 2)
                dve.tensor_tensor(T2[:, :, :, :], O[:, :, :, 0:DV], rec[:, :, :].unsqueeze(3).to_broadcast([P, TPS, NMAP, DV]), ALU.mult).then_inc(norm_chain, 1)

            def difference(k):
                tv = T2[:, :, :, :].rearrange("p t (h s) d -> p (t h) s d", s=2)
                dve.wait_ge(norm_chain, k * NNORM + 3)
                dve.tensor_tensor(dv_, tv[:, :, 0, :], tv[:, :, 1, :], ALU.add).then_inc(norm_chain, 1)

            def squares(k):
                dve.wait_ge(norm_chain, k * NNORM + 4)
                dve.tensor_tensor(T2[:, 0, :, :], dv_, dv_, ALU.mult).then_inc(norm_chain, 1)

            def square_sums(k):
                dve.wait_ge(norm_chain, k * NNORM + 5)
                dve.reduce_sum(ss[:, :], T2[:, 0, :, :], AX).then_inc(ss_ready, 1)

            def context(k):
                if diff:
                    dve.wait_ge(rr_ready, k + 1)
                    dve.tensor_tensor(ctx[:, :, :].rearrange("p t (h d) -> p (t h) d", d=DV), dv_,
                                      rr[:, :].unsqueeze(2).to_broadcast([P, TPS * NV, DV]), ALU.mult).then_inc(ctx_ready, 1)
                else:
                    dve.wait_ge(norm_chain, k + 1)
                    dve.tensor_tensor(ctx[:, :, :].rearrange("p t (h d) -> p t h d", d=DV), O[:, :, :, 0:DV],
                                      rec[:, :, :].unsqueeze(3).to_broadcast([P, TPS, NMAP, DV]), ALU.mult).then_inc(ctx_ready, 1)

            def split_ctx(k, m, misc):
                counted(m)
                dve.wait_ge(chigh, k + 1)
                if diff:
                    last = dve.scalar_tensor_tensor(cTl[:, :], misc[:, 0:NC * SEQ], outsc[:, :], cTh[:, :].bitcast(F32), ALU.mult, ALU.subtract)
                else:
                    last = dve.tensor_tensor(cTl[:, :], misc[:, 0:NC * SEQ], cTh[:, :].bitcast(F32), ALU.subtract)
                last.then_inc(misc_read, 1)

            def add_y(k, m, misc):
                dve.wait_ge(misc_full, m + 1)
                counted(m)
                y = misc[:, 0:SEQ].rearrange("p (t d) -> p t d", d=D)
                if full:
                    dve.tensor_tensor(YS[:, k + S0 - 1, :, :], y, YS[:, k + S0 - 1, :, :], ALU.add).then_inc(misc_read, 1)
                else:
                    dve.tensor_tensor(XS[:, k + S0 - 1, :, :], XS[:, k + S0 - 1, :, :], y, ALU.add).then_inc(misc_read, 1)

            if diff:
                dv_ = Dd[:, :, :, :].rearrange("p t h d -> p (t h) d")
                steps = {pos(when["reciprocals"]): (reciprocals,), pos(when["weights"]): (weights,), pos(when["difference"]): (difference, squares), pos(when["square_sums"]): (square_sums,), pos(when["context"]): (context,)}
            else:
                steps = {pos(when["reciprocals"]): (reciprocals,), pos(when["weights"]): (context,)}
            after_turn, lag = pos(when["split_context"]), when["stack_lag"]
            split_x(0, lead["T"], lead_bank["T"])
            for k in range(NTL):
                stack(0, lead[f"QK{k}"], k, 0, lead_bank[f"QK{k}"], lead_in=True)
            dve.wait_ge(misc_full, lead["T"] + 1)
            stat(1)
            for n in range(2):
                for j in range(QUAD):
                    top(n, j, n, j, lead_in=True)
                if n == 0:
                    norm(1)
                    norm2(1)
            with_max(0, 0, 0)
            split_x(1, lead["T1"], lead_bank["T1"])
            with dve.Fori(0, NSEQ // 2) as i:
                for p in range(2):
                    b = i * 2 + p
                    for g in range(NQ):
                        gq = b * NQ + g
                        for j in range(QUAD):
                            top(gq + 2, j, g % 2, j)
                            if j == when["with_maxima"]:
                                with_max(gq + 1, (g + 1) % NQ, p if g < NQ - 1 else 1 - p)
                            for step in steps.get((g, j), ()):
                                step(b)
                            name = at.get((g, j), "")
                            if (g, j) == pos(when["turn"] + 1):
                                split_x(b + 2, use(b, "T"), bank_of["T"])
                            if (g, j) == pos(when["stat"]):
                                stat(b + 2)
                            elif (g, j) == pos(when["norm"]):
                                norm(b + 2)
                            elif (g, j) == pos(when["norm2"]):
                                norm2(b + 2)
                            if (g, j) == after_turn:
                                split_ctx(b, use(b, "ctxT"), bank_of["ctxT"])
                            if name == "y":
                                add_y(b, use(b, name), bank_of[name])
                            name = at.get(((g * QUAD + j - lag) // QUAD, (j - lag) % QUAD), "")
                            if name.startswith("QK"):
                                stack(b + 1, use(b, name), int(name[2:]), 1 - p, bank_of[name])
            for key in sorted(steps):
                for step in steps[key]:
                    step(NSEQ)
            split_ctx(NSEQ, NSEQ * NM + N0, shared[N0 % 2])
            add_y(NSEQ, NSEQ * NM + N0 + 1, shared[(N0 + 1) % 2])

        @block.tensor
        def _(pe):
            pe.wait_ge(started, 1)

            def product(out, pairs):
                for k, (sh, sl, mh_, ml) in enumerate(pairs):
                    pe.matmul(out, sh, mh_, start=k == 0, stop=False)
                    pe.matmul(out, sh, ml, start=False, stop=False)
                    ins = pe.matmul(out, sl, mh_, start=False, stop=k == len(pairs) - 1)
                return ins

            def free_bank(m):
                if not isinstance(m, int) or m > 1:
                    pe.wait_ge(misc_read, m - 1)

            def turn(b, m, misc):
                free_bank(m)
                pe.wait_ge(xn_ready, b + 1)
                for t in range(TPS):
                    last = pe.transpose(misc[:, t * P:(t + 1) * P], xn[:, t, :], ident[:, :])
                last.then_inc(misc_full, 1)

            def project(b, m, k, misc):
                free_bank(m)
                if k == 0:
                    pe.wait_ge(misc_read, m)
                n = k % 2
                for r in range(2):
                    c = slice((k // 2 * 2 + r) * P, (k // 2 * 2 + r + 1) * P)
                    last = product(misc[:, r * SEQ:(r + 1) * SEQ], [(wqk[n][0][:, c], wqk[n][1][:, c], xh[:, :], xl[:, :])])
                last.then_inc(misc_full, 1)

            def values(b, m, misc):
                free_bank(m)
                for t in range(TPS):
                    c = slice(t * P, (t + 1) * P)
                    last = product(misc[:, t * VW:(t + 1) * VW], [(xh[:, c], xl[:, c], wv[0][:, :], wv[1][:, :])])
                last.then_inc(misc_full, 1)

            def keys_spread(b, g):
                k = g * QT // 2
                pe.wait_ge(k_spread[k % 2], b * KDMA + (k // 2 + 1) * 16 * HPT)

            def score(n, g, j, q, use_):
                pe.wait_ge(s_free, n * QUAD + j + 1)
                o = sbank[use_ % SB]
                c0 = (g * QT + j // HPT) * SEQ
                if masked:
                    pe.matmul(o[:, :].rearrange("p (c k) -> p c k", k=P)[:, 0::3, :], identb[:, :], maskS[:, 0:2, :], start=True, stop=True)
                for t in range(TPS):
                    nk = P if masked and t == 0 else SEQ
                    last = pe.matmul(o[:, t * SEQ:t * SEQ + nk], Q1[q][:, c0 + t * P:c0 + (t + 1) * P], KB[q][:, j % HPT, c0:c0 + nk],
                                     start=not masked, stop=True, skip_group_check=masked)
                last.then_inc(s_psum, 1)

            def score_t(n, g, j, q):
                pe.wait_ge(t_free, n * QUAD + j + 1)
                if j == 0:
                    pe.wait_ge(mt_read, n + 2)
                o = tbank[j % 2]
                c0 = (g * QT + j // HPT) * SEQ
                c2 = (j // HPT) * SEQ
                if masked:
                    pe.matmul(o[:, :].rearrange("p (c k) -> p c k", k=P)[:, 0::2, :], identb[:, :], maskT[:, :, :], start=True, stop=True)
                for t in range(TPS):
                    q0 = P if masked and t == 1 else 0
                    last = pe.matmul(o[:, t * SEQ:(t + 1) * SEQ - q0], KB[q][:, j % HPT, c0 + t * P:c0 + (t + 1) * P], Q2[g % 2][:, c2 + q0:c2 + SEQ],
                                     start=not masked, stop=True, skip_group_check=masked)
                last.then_inc(t_psum, 1)

            def weigh(n, g, q, s):
                if s == 0:
                    pe.wait_ge(t_free, 2 + n * QUAD)
                    pe.wait_ge(o_free, n + 2)
                q0 = P if masked and s == 1 else 0
                for h in range(QUAD // NS):
                    last = pe.matmul(obank[h * VG:(h + 1) * VG, 0:NS * SEQ].rearrange("p (s q) -> p s q", s=NS)[:, :, q0:],
                                     V[q][:, s, g * QUAD // NS + h, :], Pm[g % 2][:, h * NS:(h + 1) * NS, s * SEQ:(s + 1) * SEQ - q0],
                                     start=s == 0, stop=True, skip_group_check=s > 0, tile_position=(0, h * VG))
                if s == TPS - 1:
                    last.then_inc(p_used, 1)

            def turn_back(n):
                pe.wait_ge(ot_read, n + 2)
                for c in range(NS * TPS):
                    last = pe.transpose(obank[:, c * P:(c + 1) * P], OT[:, c * P:(c + 1) * P], ident[:, :])
                last.then_inc(ob_full, 1)

            def turn_max(n):
                pe.wait_ge(mt_read, n + 1)
                pe.wait_ge(m_ready, n + 1)
                for u in range(QT):
                    for t in range(TPS):
                        c = (u * TPS + t) * P
                        last = pe.transpose(mbank[:, c:c + P], padm[:, u, t, :, :].rearrange("p r g -> p (r g)"), ident[:, :])
                last.then_inc(mt_full, 1)

            def turn_ctx(k, m, misc):
                free_bank(m)
                pe.wait_ge(ctx_ready, k + 1)
                for c in range(NC):
                    for t in range(TPS):
                        last = pe.transpose(misc[:, (c * TPS + t) * P:(c * TPS + t + 1) * P], ctx[:, t, c * P:(c + 1) * P], ident[:, :])
                last.then_inc(misc_full, 1)

            def project_out(k, m, misc):
                pe.wait_ge(misc_read, m)
                for t in range(TPS):
                    last = product(misc[:, t * D:(t + 1) * D],
                                   [(cTh[:, c * SEQ + t * P:c * SEQ + (t + 1) * P], cTl[:, c * SEQ + t * P:c * SEQ + (t + 1) * P],
                                     wo[0][:, c * D:(c + 1) * D], wo[1][:, c * D:(c + 1) * D]) for c in range(NC)])
                last.then_inc(misc_full, 1)

            if masked:
                for k in range(SB):
                    pe.matmul(sbank[k][:, P:2 * P], identb[:, :], maskS[:, 2, :], start=True, stop=True)
            for c in range(NS * TPS):
                last = pe.transpose(obank[:, c * P:(c + 1) * P], OT[:, c * P:(c + 1) * P], ident[:, :])
            last.then_inc(ob_full, 1)
            turn(0, lead["T"], lead_bank["T"])
            for k in range(NTL):
                project(0, lead[f"QK{k}"], k, lead_bank[f"QK{k}"])
            values(0, lead["V"], lead_bank["V"])
            for g in range(2):
                keys_spread(0, g)
                for j in range(QUAD):
                    score(g, g, j, 0, j)
            turn_max(0)
            turn(1, lead["T1"], lead_bank["T1"])
            pe.wait_ge(cleared, 2)
            with pe.Fori(0, NSEQ // 2) as i:
                for p in range(2):
                    b = i * 2 + p
                    for g in range(NQ):
                        n = b * NQ + g
                        keys_spread(b if g < 2 else b + 1, (g + 2) % NQ)
                        for j in range(QUAD):
                            score(n + 2, (g + 2) % NQ, j, p if g < 2 else 1 - p, j)
                            score_t(n, g, j, p)
                            if j == when["turn_maxima"]:
                                turn_max(n + 1)
                            for s in range(TPS):
                                if j == when["weigh"][s]:
                                    weigh(n, (g - 1) % NQ, p if g else 1 - p, s)
                            if j == 3:
                                turn_back(n)
                            name = at.get((g, j), "")
                            if name == "ctxT":
                                turn_ctx(b, use(b, name), bank_of[name])
                            elif name == "y":
                                project_out(b, use(b, name), bank_of[name])
                            elif name == "T":
                                turn(b + 2, use(b, name), bank_of[name])
                            elif name == "V":
                                values(b + 1, use(b, name), bank_of[name])
                            elif name.startswith("QK"):
                                project(b + 1, use(b, name), int(name[2:]), bank_of[name])
            for s in range(TPS):
                weigh(NSEQ * NQ, 3, 1, s)
            turn_back(NSEQ * NQ)
            turn_ctx(NSEQ, NSEQ * NM + N0, shared[N0 % 2])
            project_out(NSEQ, NSEQ * NM + N0 + 1, shared[(N0 + 1) % 2])
    st.close()


def attn_args(kind, a):
    if kind == "diff":
        return {k: a["L0_attn_a_" + n] for k, n in (("wq", "W_q"), ("wk", "W_k"), ("wv", "W_v"), ("wo", "W_o"), ("rms_scale", "rms_scale"),
                                                    ("lambda_q1", "lambda_q1"), ("lambda_k1", "lambda_k1"), ("lambda_q2", "lambda_q2"), ("lambda_k2", "lambda_k2"))}
    if kind == "causal":
        return {k: a["L0_attn_b_" + n] for k, n in (("wq", "Wq"), ("wk", "Wk"), ("wv", "Wv"), ("wo", "Wo"))}
    return {k: a["L1_ffn_" + n] for k, n in (("wq", "wq"), ("wk", "wk"), ("wv", "wv"), ("wo", "wo"), ("norm_w", "norm1_w"))}


def single_head_stage(nc, tag, G, w, parts):
    WH, WL = G["WH"], G["WL"]
    high, low = [T[:, :].rearrange("p (e c) -> p e c", e=E + 1) for T in (WH, WL)]
    WCOLS = high.shape[2]
    X, ident = G["X"], G["ident"]
    XS = X[:, :, :].rearrange("p (s t) d -> p s t d", t=TPS)
    S0 = PAD // TPS
    SCALE = float(D) ** -0.5
    st = Stage(nc)
    sb, sem = (lambda n, s, d=F32: st.sb(f"{tag}_{n}", s, d)), (lambda n: st.sem(f"{tag}_{n}"))
    spare = sb("spare", [P, 1])
    epst = sb("epst", [P, 4])
    stats, mv, rs, rs2 = sb("stats", [P, TPS, 6]), sb("mv", [P, TPS, 2]), sb("rs", [P, TPS]), sb("rs2", [P, TPS])
    half = sb("half", [P, TPS])
    raw, nil = sb("raw", [P, (E + 1) * WCOLS]), sb("nil", [P, WCOLS])
    unsplit = raw[:, :].rearrange("p (e c) -> p e c", e=E + 1)
    xn, xT = sb("xn", [P, TPS, D]), sb("xT", [P, SEQ])
    wq, wk, wv = sb("wq", [D, D]), sb("wk", [D, D]), sb("wv", [D, D])
    bq, bk, bv = sb("bq", [D, 1]), sb("bk", [D, 1]), sb("bv", [P, D])
    QT, KT, V = [sb(f"QT{k}", [P, SEQ]) for k in range(2)], [sb(f"KT{k}", [P, SEQ]) for k in range(2)], [sb(f"V{k}", [P, TPS, D]) for k in range(2)]
    m, rinv = sb("m", [P, TPS]), sb("rinv", [P, TPS])
    nm, rsum = [sb(f"nm{k}", [P, TPS]) for k in range(2)], [sb(f"rsum{k}", [P, TPS]) for k in range(2)]
    Pm, PT = sb("Pm", [P, TPS, SEQ]), sb("PT", [P, TPS, SEQ])
    xb, qkb, vb, ptb, ob = [st.bank(f"{tag}_{n}") for n in ("xb", "qkb", "vb", "ptb", "ob")]
    scb = [st.bank(f"{tag}_scb{k}") for k in range(2)]
    w_in, half_set, stat_step, mv_ready, var_ready, rstd_ready, xn_ready = [sem(n) for n in ("w_in", "half_set", "stat_step", "mv_ready", "var_ready", "rstd_ready", "xn_ready")]
    experts_in, high_done, low_done = sem("experts_in"), sem("high_done"), sem("low_done")
    xT_psum, xT_ready, qk_psum, qk_ready, v_psum, v_ready = [sem(n) for n in ("xT_psum", "xT_ready", "qk_psum", "qk_ready", "v_psum", "v_ready")]
    s_psum, m_ready, nm_ready, p_ready, pT_psum, pT_ready, rinv_ready, o_psum, x_done = [sem(n) for n in ("s_psum", "m_ready", "nm_ready", "p_ready", "pT_psum", "pT_ready", "rinv_ready", "o_psum", "x_done")]

    with nc.Block() as block:
        @block.sync
        def _(sp):
            for dst, src in ((wq, w["Wq"]), (wk, w["Wk"]), (wv, w["Wv"])):
                sp.dma_start(dst[:, :], src).then_inc(w_in, 16)
            sp.dma_start(bq[:, :], w["bq"].rearrange("(p a) -> p a", a=1)).then_inc(w_in, 16)
            sp.dma_start(bk[:, :], w["bk"].rearrange("(p a) -> p a", a=1)).then_inc(w_in, 16)
            sp.dma_start(bv[:, :], w["bv"].unsqueeze(0).to_broadcast([P, D])).then_inc(w_in, 16)
            for (c0, c1), src in parts:
                dst = raw[:, c0:c1]
                sp.dma_start(dst if len(src.shape) == 2 else dst.rearrange("p (a b) -> p a b", a=src.shape[1]), src).then_inc(experts_in, 16)

        @block.gpsimd
        def _(pool):
            pool.memset(epst[:, :], 1e-5)
            pool.memset(nil[:, :], 0.0)
            pool.memset(half[:, :], -0.5).then_inc(half_set, 1)
            pool.wait_ge(half_set, 1)

            def root(b):
                pool.wait_ge(mv_ready, b + 1)
                pool.tensor_tensor(rs2[:, :], mv[:, :, 1], epst[:, 0:mv.shape[1]], ALU.add).then_inc(var_ready, 1)
                pool.wait_ge(var_ready, b + 1)
                pool.tensor_tensor(rs[:, :], rs2[:, :], half[:, :], ALU.pow).then_inc(rstd_ready, 1)

            def split(e):
                pool.tensor_tensor(high[:, e, :], unsplit[:, e, :], nil[:, :], ALU.add).then_inc(high_done, 1)
                pool.wait_ge(high_done, e + 1)
                pool.tensor_tensor(low[:, e, :], unsplit[:, e, :], high[:, e, :].bitcast(F32), ALU.subtract).then_inc(low_done, 1)

            FIRST = NSEQ - E
            with pool.Fori(0, FIRST - 1) as b:
                root(b)
            pool.wait_ge(experts_in, 16 * len(parts))
            with pool.Fori(FIRST - 1, NSEQ) as b:
                root(b)
                split(b - (FIRST - 1))
            root(NSEQ)
            pool.wait_ge(low_done, E + 1)

        @block.scalar
        def _(act):
            act.wait_ge(w_in, 96)

            def turned(b):
                act.wait_ge(xT_psum, b + 1)
                act.activation(xT[:, :], xb[:, 0:SEQ], ACT.Identity).then_inc(xT_ready, 1)

            def queries_keys(b, q):
                act.wait_ge(qk_psum, b + 1)
                act.activation(QT[q][:, :], qkb[:, 0:SEQ], ACT.Identity, bias=bq[:, :])
                act.activation(KT[q][:, :], qkb[:, SEQ:2 * SEQ], ACT.Identity, bias=bk[:, :]).then_inc(qk_ready, 1)

            def probabilities(b, q):
                act.wait_ge(nm_ready, b + 1)
                for t in range(TPS):
                    last = act.activation(Pm[:, t, :], scb[q][:, t * SEQ:(t + 1) * SEQ], ACT.Exp, bias=nm[q][:, t:t + 1],
                                          scale=SCALE, accum_out=rsum[q][:, t:t + 1])
                last.then_inc(p_ready, 1)

            turned(0)
            queries_keys(0, 0)
            turned(1)
            probabilities(0, 0)
            queries_keys(1, 1)

            def step(b, p, ahead=2):
                act.wait_ge(pT_psum, b + 1)
                act.activation(PT[:, :, :].rearrange("p k q -> p (k q)"), ptb[:, :], ACT.Identity).then_inc(pT_ready, 1)
                if ahead > 1:
                    turned(b + 2)
                if ahead > 0:
                    probabilities(b + 1, 1 - p)
                if ahead > 1:
                    queries_keys(b + 2, p)

            with act.Fori(0, NSEQ // 2 - 1) as i:
                for p in range(2):
                    step(i * 2 + p, p)
            for p in range(2):
                step(NSEQ - 2 + p, p, 1 - p)

        @block.vector
        def _(dve):
            dve.memset(spare[:, :], 0.0).then_inc(x_done, 1)
            dve.wait_ge(w_in, 96)

            def norm(b):
                for t in range(TPS):
                    last = dve.bn_stats(stats[:, t, :], XS[:, b + S0, t, :])
                last.then_inc(stat_step, 1)
                dve.wait_ge(stat_step, b + 1)
                dve.memset(spare[:, :], 0.0)
                for t in range(TPS):
                    last = dve.bn_aggr(mv[:, t, :], stats[:, t, :])
                last.then_inc(mv_ready, 1)

            def norm2(b):
                dve.wait_ge(rstd_ready, b + 1)
                for t in range(TPS):
                    last = dve.tensor_scalar(xn[:, t, :], XS[:, b + S0, t, :], mv[:, t, 0:1], rs[:, t:t + 1], ALU.subtract, ALU.mult)
                last.then_inc(xn_ready, 1)

            def values(b, q):
                dve.wait_ge(v_psum, b + 1)
                dve.tensor_tensor(V[q][:, :, :], vb[:, 0:SEQ].rearrange("p (t d) -> p t d", d=D),
                                  bv[:, :].unsqueeze(1).to_broadcast([P, TPS, D]), ALU.add).then_inc(v_ready, 1)

            def maxima(b, q):
                dve.wait_ge(s_psum, b + 1)
                dve.reduce_max(m[:, :], scb[q][:, :].rearrange("p (t k) -> p t k", t=TPS), AX).then_inc(m_ready, 1)
                dve.wait_ge(m_ready, b + 1)
                dve.tensor_scalar(nm[q][:, :], m[:, :], -SCALE, None, ALU.mult).then_inc(nm_ready, 1)

            norm(0)
            norm2(0)
            norm(1)
            values(0, 0)
            norm2(1)
            maxima(0, 0)
            norm(2)
            values(1, 1)
            norm2(2)

            def step(b, p, ahead=2):
                if ahead > 0:
                    maxima(b + 1, 1 - p)
                if ahead > 1:
                    norm(b + 3)
                if ahead == 0:
                    dve.wait_ge(x_done, b + 1)
                dve.wait_ge(p_ready, b + 1)
                dve.reciprocal(rinv[:, :], rsum[p][:, :]).then_inc(rinv_ready, 1)
                dve.wait_ge(rinv_ready, b + 1)
                dve.wait_ge(o_psum, b + 1)
                for t in range(TPS):
                    last = dve.scalar_tensor_tensor(XS[:, b + S0, t, :], ob[:, t * D:(t + 1) * D], rinv[:, t:t + 1], XS[:, b + S0, t, :], ALU.mult, ALU.add)
                last.then_inc(x_done, 1)
                if ahead > 1:
                    values(b + 2, p)
                    norm2(b + 3)

            with dve.Fori(0, NSEQ // 2 - 1) as i:
                for p in range(2):
                    step(i * 2 + p, p)
            for p in range(2):
                step(NSEQ - 2 + p, p, 1 - p)

        @block.tensor
        def _(pe):
            pe.wait_ge(w_in, 96)

            def turn(b):
                pe.wait_ge(xn_ready, b + 1)
                for t in range(TPS):
                    last = pe.transpose(xb[:, t * P:(t + 1) * P], xn[:, t, :], ident[:, :])
                last.then_inc(xT_psum, 1)

            def project(b):
                pe.wait_ge(xT_ready, b + 1)
                pe.matmul(qkb[:, 0:SEQ], wq[:, :], xT[:, :], start=True, stop=True)
                pe.matmul(qkb[:, SEQ:], wk[:, :], xT[:, :], start=True, stop=True).then_inc(qk_psum, 1)
                for t in range(TPS):
                    last = pe.matmul(vb[:, t * D:(t + 1) * D], xT[:, t * P:(t + 1) * P], wv[:, :], start=True, stop=True)
                last.then_inc(v_psum, 1)

            def score(b, q):
                pe.wait_ge(qk_ready, b + 1)
                for t in range(TPS):
                    last = pe.matmul(scb[q][:, t * SEQ:(t + 1) * SEQ], QT[q][:, t * P:(t + 1) * P], KT[q][:, :], start=True, stop=True)
                last.then_inc(s_psum, 1)

            turn(0)
            project(0)
            score(0, 0)
            turn(1)
            pe.wait_ge(v_ready, 1)
            project(1)

            def step(b, p, ahead=2):
                pe.wait_ge(p_ready, b + 1)
                for k in range(TPS):
                    for t in range(TPS):
                        last = pe.transpose(ptb[:, k * SEQ + t * P:k * SEQ + (t + 1) * P], Pm[:, t, k * P:(k + 1) * P], ident[:, :])
                last.then_inc(pT_psum, 1)
                if ahead > 0:
                    score(b + 1, 1 - p)
                if ahead > 1:
                    turn(b + 2)
                pe.wait_ge(pT_ready, b + 1)
                pe.wait_ge(x_done, b + 1)
                for t in range(TPS):
                    for k in range(TPS):
                        last = pe.matmul(ob[:, t * D:(t + 1) * D], PT[:, k, t * P:(t + 1) * P], V[p][:, k, :], start=k == 0, stop=k == TPS - 1)
                last.then_inc(o_psum, 1)
                if ahead > 1:
                    pe.wait_ge(v_ready, b + 2)
                    project(b + 2)

            with pe.Fori(0, NSEQ // 2 - 1) as i:
                for p in range(2):
                    step(i * 2 + p, p)
            for p in range(2):
                step(NSEQ - 2 + p, p, 1 - p)
    st.close()


HID = 192
HC = HID // 2
CONV = 4


def recurrence_in_stage(nc, tag, G, w):
    X, Y, ident, GT, VT = G["X"], G["Y"], G["ident"], G["GT"], G["VT"]
    XB = X[:, :, :].rearrange("p (b t) d -> p b t d", t=TPB)
    YB = Y[:, :, :].rearrange("p (b t) d -> p b t d", t=TPB)
    GB = GT[:, :, :].rearrange("p c (b t) -> p b c t", t=BLK)
    VB = VT[:, :, :, :].rearrange("p c (b s) t -> p b c s t", s=2)
    st = Stage(nc)
    sb, sem = (lambda n, s, d=F32: st.sb(f"{tag}_{n}", s, d)), (lambda n: st.sem(f"{tag}_{n}"))
    spare, credit = sb("spare", [P, 1]), sb("credit", [P, 2])
    epst = sb("epst", [P, 4])
    stats, mv, half = sb("stats", [P, TPB, 6]), sb("mv", [P, TPB, 2]), sb("half", [P, TPB])
    rs, r2, r3, rq = [sb(n, [P, TPB]) for n in ("rs", "r2", "r3", "rq")]
    xn, xT = sb("xn", [P, TPB, D]), sb("xT", [P, 2, BLK])
    win, g1 = sb("win", [D, 4 * HC]), sb("g1", [P, 1])
    xb = st.bank(f"{tag}_xb")
    ub = [st.bank(f"{tag}_u{k}") for k in range(4)]
    w_in, half_set, stat_step, mv_ready, pool_chain, rstd_ready, y_ready, xn_ready = [sem(n) for n in ("w_in", "half_set", "stat_step", "mv_ready", "pool_chain", "rstd_ready", "y_ready", "xn_ready")]
    xT_psum, xT_ready, gate_psum, gate_done, v_psum, v_done = [sem(n) for n in ("xT_psum", "xT_ready", "gate_psum", "gate_done", "v_psum", "v_done")]

    with nc.Block() as block:
        @block.sync
        def _(sp):
            sp.dma_start(win[:, :], w["W_in"]).then_inc(w_in, 16)
            sp.dma_start(g1[:, :], w["gamma1"].rearrange("(p a) -> p a", a=1)).then_inc(w_in, 16)

        @block.gpsimd
        def _(pool):
            pool.memset(VT[:, :, :, 0:CONV - 1], 0.0)
            pool.memset(epst[:, :], 1e-5)
            pool.memset(half[:, :], -0.5).then_inc(half_set, 1)
            pool.wait_ge(half_set, 1)

            def root(b):
                pool.wait_ge(mv_ready, b + 1)
                ch = Chain(pool, pool_chain, b * 4)
                ch(pool.tensor_tensor(r2[:, :], mv[:, :, 1], epst[:, 0:mv.shape[1]], ALU.add))
                ch(pool.tensor_tensor(rs[:, :], r2[:, :], half[:, :], ALU.pow))
                ch(pool.tensor_tensor(r3[:, :], rs[:, :], rs[:, :], ALU.mult))
                ch(pool.tensor_tensor(r2[:, :], r3[:, :], mv[:, :, 1], ALU.mult))
                pool.tensor_tensor(rq[:, :], r2[:, :], half[:, :], ALU.pow).then_inc(rstd_ready, 1)

            root(0)
            with pool.Fori(1, NBLK) as b:
                root(b)

        @block.scalar
        def _(act):
            with act.Fori(0, NBLK) as b:
                act.wait_ge(gate_psum, b + 1)
                for c in range(2):
                    last = act.activation(GB[:, b, c, :], ub[c][0:HC, :], ACT.Gelu)
                last.then_inc(gate_done, 1)

        @block.vector
        def _(dve):
            def stat(b):
                for t in range(TPB):
                    last = dve.bn_stats(stats[:, t, :], XB[:, b + 1, t, :])
                last.then_inc(stat_step, 1)
                dve.wait_ge(stat_step, b + 1)
                dve.memset(spare[:, :], 0.0)
                for t in range(TPB):
                    last = dve.bn_aggr(mv[:, t, :], stats[:, t, :])
                last.then_inc(mv_ready, 1)

            def norm(b):
                dve.wait_ge(rstd_ready, b + 1)
                for t in range(TPB):
                    last = dve.tensor_scalar(YB[:, b + 1, t, :], XB[:, b + 1, t, :], mv[:, t, 0:1], rs[:, t:t + 1], ALU.subtract, ALU.mult)
                last.then_inc(y_ready, 1)
                dve.wait_ge(y_ready, b + 1)
                for t in range(TPB):
                    last = dve.tensor_scalar(xn[:, t, :], YB[:, b + 1, t, :], rq[:, t:t + 1], None, ALU.mult)
                last.then_inc(xn_ready, 1)

            def take(b):
                dve.wait_ge(v_psum, b + 1)
                for c in range(2):
                    last = dve.tensor_copy(VB[:, b, c, :, CONV - 1:], ub[2 + c][0:HC, :].rearrange("p (s t) -> p s t", s=2))
                last.then_inc(v_done, 1)

            for k, s in enumerate((gate_done, v_done)):
                dve.memset(credit[:, k:k + 1], 0.0).then_inc(s, 1)
            def take_x(b, q):
                dve.wait_ge(xT_psum, b + 1)
                dve.tensor_scalar(xT[:, q, :], xb[:, :], g1[:, :], None, ALU.mult).then_inc(xT_ready, 1)

            stat(0)
            norm(0)
            stat(1)
            dve.wait_ge(w_in, 32)
            take_x(0, 0)
            norm(1)
            stat(2)

            def step(b, p, ahead=3):
                if ahead > 0:
                    take_x(b + 1, 1 - p)
                if ahead > 1:
                    norm(b + 2)
                if ahead > 2:
                    stat(b + 3)
                take(b)

            with dve.Fori(0, NBLK // 2 - 2) as i:
                for p in range(2):
                    step(i * 2 + p, p)
            for k in range(4):
                step(NBLK - 4 + k, k % 2, 3 - k)

        @block.tensor
        def _(pe):
            pe.wait_ge(w_in, 32)

            def turn(b):
                pe.wait_ge(xn_ready, b + 1)
                for t in range(TPB):
                    last = pe.transpose(xb[:, t * P:(t + 1) * P], xn[:, t, :], ident[:, :])
                last.then_inc(xT_psum, 1)

            def project(b, q, first, full):
                for k in (first, first + 1):
                    last = pe.matmul(ub[k][0:HC, :], win[:, k * HC:(k + 1) * HC], xT[:, q, :], start=True, stop=True)
                last.then_inc(full, 1)

            def step(b, p, ahead=True):
                pe.wait_ge(xT_ready, b + 1)
                pe.wait_ge(gate_done, b + 1)
                project(b, p, 0, gate_psum)
                if ahead:
                    turn(b + 1)
                pe.wait_ge(v_done, b + 1)
                project(b, p, 2, v_psum)

            turn(0)
            with pe.Fori(0, NBLK // 2 - 1) as i:
                for p in range(2):
                    step(i * 2 + p, p)
            for p in range(2):
                step(NBLK - 2 + p, p, p == 0)
    st.close()


def recurrence_stage(nc, tag, G, w):
    Y, GT, VT = G["Y"], G["GT"], G["VT"]
    YB = Y[:, :, :].rearrange("p (b t) d -> p b t d", t=TPB)
    GB = GT[:, :, :].rearrange("p c (b t) -> p b c t", t=BLK)
    VB = VT[:, :, :, :].rearrange("p c (b s) t -> p b c s t", s=2)
    st = Stage(nc)
    sb, sem = (lambda n, s, d=F32: st.sb(f"{tag}_{n}", s, d)), (lambda n: st.sem(f"{tag}_{n}"))
    wg, wout = sb("wg", [HC, 2, 4 * HC]), sb("wout", [HC, 2, D])
    cw, cb, bg, fb = sb("cw", [HC, 2, CONV]), sb("cb", [HC, 2]), sb("bg", [HC, 4]), sb("fb", [HC, 2])
    hbg, sp_, ca, one, quarter = sb("hbg", [HC, 4]), sb("sp", [HC, 4]), sb("ca", [HC, 2]), sb("one", [HC, 1]), sb("quarter", [HC, 1])
    taps = sb("taps", [HC, 2, BLK])
    vc, al = [[sb(f"{n}{k}", [HC, 2, BLK]) for k in range(2)] for n in ("vc", "al")]
    gates = sb("gates", [HC, 4, BLK])
    be, xg, hh, gh = [sb(n, [HC, 2, BLK]) for n in ("be", "xg", "hh", "gh")]
    credit = sb("credit", [HC, 8])
    gb = [st.bank(f"{tag}_g{k}") for k in range(4)]
    yb = st.bank(f"{tag}_y")
    w_in, prep, ca_step, tap_step, vc_ready, g_psum, gates_ready, al_ready = [sem(n) for n in ("w_in", "prep", "ca_step", "tap_step", "vc_ready", "g_psum", "gates_ready", "al_ready")]
    sq_ready, be_ready, xi_ready, xg_ready, h_ready, gh_ready, y_psum, y_done = [sem(n) for n in ("sq_ready", "be_ready", "xi_ready", "xg_ready", "h_ready", "gh_ready", "y_psum", "y_done")]

    with nc.Block() as block:
        @block.sync
        def _(sp):
            sp.dma_start(wg[:, :, :], w["W_gates"].rearrange("(c p) g -> p c g", p=HC)).then_inc(w_in, 16)
            sp.dma_start(wout[:, :, :], w["W_out"].rearrange("(c p) d -> p c d", p=HC)).then_inc(w_in, 16)
            sp.dma_start(cw[:, :, :], w["conv_w"].rearrange("(c p) a k -> p c (a k)", p=HC)).then_inc(w_in, 16)
            for dst, src in ((cb, "conv_b"), (bg, "b_gates"), (fb, "forget_base")):
                sp.dma_start(dst[:, :], w[src].rearrange("(c p) -> p c", p=HC), allow_slow_non_contiguous=True).then_inc(w_in, 16)

        @block.gpsimd
        def _(pool):
            with pool.Fori(0, NBLK) as b:
                pool.wait_ge(h_ready, b + 1)
                pool.wait_ge(y_psum, b + 1)
                pool.tensor_tensor(gh[:, :, :], hh[:, :, :], GB[:, b, :, :], ALU.mult).then_inc(gh_ready, 1)

        @block.scalar
        def _(act):
            act.wait_ge(prep, 1)
            act.activation(sp_[:, 0:2], fb[:, :], ACT.Abs).then_inc(prep, 1)
            act.wait_ge(prep, 2)
            act.activation(sp_[:, 2:4], sp_[:, 0:2], ACT.Exp, scale=-1.0).then_inc(prep, 1)
            act.wait_ge(prep, 3)
            act.activation(sp_[:, 0:2], sp_[:, 2:4], ACT.Ln, bias=one[:, :]).then_inc(prep, 1)
            act.wait_ge(ca_step, 3)

            def decay(b, q, first=False):
                act.wait_ge(g_psum, b + 1)
                act.wait_ge(xi_ready, b + 1)
                for k in range(4):
                    last = act.activation(gates[:, k, :], gb[k][0:HC, :], ACT.Tanh, scale=0.5, bias=hbg[:, k:k + 1])
                last.then_inc(gates_ready, 1)
                act.wait_ge(gates_ready, b + 2)
                if not first:
                    act.wait_ge(h_ready, b - 1)
                for c in range(2):
                    last = act.activation(al[q][:, c, :], gates[:, c, :], ACT.Exp, scale=ca[:, c:c + 1], bias=ca[:, c:c + 1])
                last.then_inc(al_ready, 1)
                act.wait_ge(al_ready, b + 1)
                act.wait_ge(xg_ready, b + 1)
                act.activation(be[:, :, :], al[q][:, :, :], ACT.Square).then_inc(sq_ready, 1)
                act.wait_ge(sq_ready, b + 1)
                act.activation(be[:, :, :], be[:, :, :], ACT.Sqrt, scale=-0.25, bias=quarter[:, :]).then_inc(be_ready, 1)

            decay(0, 0, first=True)
            decay(1, 1, first=True)
            with act.Fori(1, NBLK // 2) as i:
                for p in range(2):
                    decay(i * 2 + p, p)

        @block.vector
        def _(dve):
            for k, s in enumerate((xi_ready, xg_ready, gates_ready, y_psum, y_done)):
                dve.memset(credit[:, k:k + 1], 0.0).then_inc(s, 1)
            dve.memset(one[:, :], 1.0)
            dve.memset(quarter[:, :], 0.25 * (1.0 + 1e-6))
            dve.wait_ge(w_in, 96)
            dve.tensor_scalar(hbg[:, :], bg[:, :], 0.5, None, ALU.mult).then_inc(prep, 1)
            dve.wait_ge(prep, 4)
            dve.tensor_scalar(ca[:, :], fb[:, :], 0.0, None, ALU.max).then_inc(ca_step, 1)
            dve.wait_ge(ca_step, 1)
            dve.tensor_tensor(ca[:, :], ca[:, :], sp_[:, 0:2], ALU.add).then_inc(ca_step, 1)
            dve.wait_ge(ca_step, 2)
            dve.tensor_scalar(ca[:, :], ca[:, :], -8.0 / 2, None, ALU.mult).then_inc(ca_step, 1)

            def conv(b, q, earlier=2):
                ch = Chain(dve, tap_step, b * (CONV - 1))
                if earlier >= 1:
                    dve.wait_ge(vc_ready, b)
                if earlier >= 2:
                    dve.wait_ge(g_psum, b - 1)
                out = taps[:, :, :].rearrange("p c (s t) -> p c s t", s=2)
                for c in range(2):
                    last = dve.tensor_scalar(out[:, c, :, :], VB[:, b, c, :, 0:SEQ], cw[:, c, 0:1], cb[:, c:c + 1], ALU.mult, ALU.add)
                ch(last)
                for k in range(1, CONV):
                    dst = (vc[q] if k == CONV - 1 else taps)[:, :, :].rearrange("p c (s t) -> p c s t", s=2)
                    for c in range(2):
                        last = dve.scalar_tensor_tensor(dst[:, c, :, :], VB[:, b, c, :, k:k + SEQ], cw[:, c, k:k + 1], out[:, c, :, :], ALU.mult, ALU.add)
                    if k < CONV - 1:
                        ch(last)
                last.then_inc(vc_ready, 1)

            def scan(b, q, first=False):
                dve.wait_ge(gates_ready, b + 2)
                dve.scalar_tensor_tensor(xg[:, :, :], gates[:, 2:4, :], one[:, :], vc[q][:, :, :], ALU.add, ALU.mult).then_inc(xi_ready, 1)
                dve.wait_ge(xi_ready, b + 2)
                dve.wait_ge(be_ready, b + 1)
                dve.tensor_tensor(xg[:, :, :], xg[:, :, :], be[:, :, :], ALU.mult).then_inc(xg_ready, 1)
                dve.wait_ge(xg_ready, b + 2)
                if not first:
                    dve.wait_ge(h_ready, b)
                    dve.wait_ge(gh_ready, b)
                for c in range(2):
                    for s in range(2):
                        cols = slice(s * SEQ, (s + 1) * SEQ)
                        last = dve.tensor_tensor_scan(hh[:, c, cols], al[q][:, c, cols], xg[:, c, cols], 0.0, ALU.mult, ALU.add)
                last.then_inc(h_ready, 1)

            def add(b):
                dve.wait_ge(y_psum, b + 2)
                dve.tensor_tensor(YB[:, b + 1, :, :], YB[:, b + 1, :, :], yb[:, :].rearrange("p (t d) -> p t d", d=D), ALU.add).then_inc(y_done, 1)

            conv(0, 0, earlier=0)
            conv(1, 1, earlier=1)
            scan(0, 0, first=True)
            with dve.Fori(0, NBLK // 2 - 1) as i:
                for p in range(2):
                    b = i * 2 + p
                    conv(b + 2, p)
                    add(b)
                    scan(b + 1, 1 - p)
            add(NBLK - 2)
            scan(NBLK - 1, 1)
            add(NBLK - 1)

        @block.tensor
        def _(pe):
            pe.wait_ge(w_in, 96)

            def gate(b, q):
                pe.wait_ge(vc_ready, b + 1)
                pe.wait_ge(gates_ready, b + 1)
                for k in range(4):
                    for c in range(2):
                        last = pe.matmul(gb[k][0:HC, :], wg[:, c, k * HC:(k + 1) * HC], vc[q][:, c, :], start=c == 0, stop=c == 1)
                last.then_inc(g_psum, 1)

            def project(b):
                pe.wait_ge(gh_ready, b + 1)
                pe.wait_ge(y_done, b + 1)
                for t in range(TPB):
                    for c in range(2):
                        last = pe.matmul(yb[:, t * D:(t + 1) * D], gh[:, c, t * P:(t + 1) * P], wout[:, c, :], start=c == 0, stop=c == 1)
                last.then_inc(y_psum, 1)

            gate(0, 0)
            with pe.Fori(0, NBLK // 2 - 1) as i:
                for p in range(2):
                    gate(i * 2 + p + 1, 1 - p)
                    project(i * 2 + p)
            gate(NBLK - 1, 1)
            project(NBLK - 2)
            project(NBLK - 1)
    st.close()


def gated_mlp_stage(nc, tag, G, w):
    X, Y, ident = G["X"], G["Y"], G["ident"]
    XB = X[:, :, :].rearrange("p (b t) d -> p b t d", t=TPB)
    YB = Y[:, :, :].rearrange("p (b t) d -> p b t d", t=TPB)
    st = Stage(nc)
    sb, sem = (lambda n, s, d=F32: st.sb(f"{tag}_{n}", s, d)), (lambda n: st.sem(f"{tag}_{n}"))
    spare, credit = sb("spare", [P, 1]), sb("credit", [P, 2])
    stats, mv, half = sb("stats", [P, TPB, 6]), sb("mv", [P, TPB, 2]), sb("half", [P, TPB])
    rs, r2, r3 = [sb(n, [P, TPB]) for n in ("rs", "r2", "r3")]
    xn, xT = sb("xn", [P, TPB, D]), sb("xT", [P, BLK])
    wgr, wsh, g2 = sb("wgr", [D, 4 * P]), sb("wsh", [P, 2, D]), sb("g2", [P, 1])
    gt, mm = sb("gt", [P, 2, BLK]), sb("mm", [P, 2, BLK])
    xb, ob = st.bank(f"{tag}_xb"), st.bank(f"{tag}_ob")
    ub = [st.bank(f"{tag}_u{k}") for k in range(4)]
    w_in, half_set, stat_step, mv_ready, pool_chain, rstd_ready, xn_ready, x_added = [sem(n) for n in ("w_in", "half_set", "stat_step", "mv_ready", "pool_chain", "rstd_ready", "xn_ready", "x_added")]
    xT_psum, xT_ready, gate_psum, v_psum, gate_ready, m_ready, o_psum, x_done = [sem(n) for n in ("xT_psum", "xT_ready", "gate_psum", "v_psum", "gate_ready", "m_ready", "o_psum", "x_done")]

    with nc.Block() as block:
        @block.sync
        def _(sp):
            sp.dma_start(wgr[:, :], w["W_grow"]).then_inc(w_in, 16)
            sp.dma_start(wsh[:, :, :], w["W_shrink"].rearrange("(c p) d -> p c d", p=P)).then_inc(w_in, 16)
            sp.dma_start(g2[:, :], w["gamma2"].rearrange("(p a) -> p a", a=1)).then_inc(w_in, 16)

        @block.gpsimd
        def _(pool):
            pool.memset(half[:, :], -0.5).then_inc(half_set, 1)
            pool.wait_ge(half_set, 1)

            def root(b):
                pool.wait_ge(mv_ready, b + 1)
                ch = Chain(pool, pool_chain, b * 2)
                ch(pool.tensor_tensor(r2[:, :], mv[:, :, 0], mv[:, :, 0], ALU.mult))
                ch(pool.tensor_tensor(r3[:, :], r2[:, :], mv[:, :, 1], ALU.add))
                pool.tensor_tensor(rs[:, :], r3[:, :], half[:, :], ALU.pow).then_inc(rstd_ready, 1)
                pool.tensor_tensor(XB[:, b + 1, :, :], XB[:, b + 1, :, :], YB[:, b + 1, :, :], ALU.add).then_inc(x_added, 1)

            root(0)
            with pool.Fori(1, NBLK) as b:
                root(b)

        @block.scalar
        def _(act):
            with act.Fori(0, NBLK) as b:
                act.wait_ge(gate_psum, b + 1)
                act.wait_ge(m_ready, b + 1)
                for c in range(2):
                    last = act.activation(gt[:, c, :], ub[c][:, :], ACT.Gelu)
                last.then_inc(gate_ready, 1)

        @block.vector
        def _(dve):
            def stat(b):
                for t in range(TPB):
                    last = dve.bn_stats(stats[:, t, :], YB[:, b + 1, t, :])
                last.then_inc(stat_step, 1)
                dve.wait_ge(stat_step, b + 1)
                dve.memset(spare[:, :], 0.0)
                for t in range(TPB):
                    last = dve.bn_aggr(mv[:, t, :], stats[:, t, :])
                last.then_inc(mv_ready, 1)

            def norm(b):
                dve.wait_ge(rstd_ready, b + 1)
                for t in range(TPB):
                    last = dve.tensor_scalar(xn[:, t, :], YB[:, b + 1, t, :], rs[:, t:t + 1], None, ALU.mult)
                last.then_inc(xn_ready, 1)

            def gate(b):
                dve.wait_ge(gate_ready, b + 1)
                dve.wait_ge(v_psum, b + 1)
                for c in range(2):
                    last = dve.tensor_tensor(mm[:, c, :], gt[:, c, :], ub[2 + c][:, :], ALU.mult)
                last.then_inc(m_ready, 1)

            def add(b):
                dve.wait_ge(o_psum, b + 1)
                dve.wait_ge(x_added, b + 1)
                dve.tensor_tensor(XB[:, b + 1, :, :], XB[:, b + 1, :, :], ob[:, :].rearrange("p (t d) -> p t d", d=D), ALU.add).then_inc(x_done, 1)

            def take(b):
                dve.wait_ge(xT_psum, b + 1)
                dve.tensor_scalar(xT[:, :], xb[:, :], g2[:, :], None, ALU.mult).then_inc(xT_ready, 1)

            for k, s in enumerate((m_ready, x_done)):
                dve.memset(credit[:, k:k + 1], 0.0).then_inc(s, 1)
            stat(0)
            norm(0)
            stat(1)
            dve.wait_ge(w_in, 48)
            take(0)
            norm(1)
            stat(2)
            take(1)

            def step(b, ahead=3):
                gate(b)
                if ahead > 1:
                    norm(b + 2)
                if ahead > 2:
                    stat(b + 3)
                add(b)
                if ahead > 1:
                    take(b + 2)

            with dve.Fori(0, NBLK - 3) as b:
                step(b)
            for k in range(3):
                step(NBLK - 3 + k, 2 - k)

        @block.tensor
        def _(pe):
            def turn(b):
                pe.wait_ge(xn_ready, b + 1)
                for t in range(TPB):
                    last = pe.transpose(xb[:, t * P:(t + 1) * P], xn[:, t, :], ident[:, :])
                last.then_inc(xT_psum, 1)

            def gates(b, first=False):
                pe.wait_ge(xT_ready, b + 1)
                if not first:
                    pe.wait_ge(gate_ready, b)
                for k in range(2):
                    last = pe.matmul(ub[k][:, :], wgr[:, k * P:(k + 1) * P], xT[:, :], start=True, stop=True)
                last.then_inc(gate_psum, 1)

            def values(b):
                for k in range(2, 4):
                    last = pe.matmul(ub[k][:, :], wgr[:, k * P:(k + 1) * P], xT[:, :], start=True, stop=True)
                last.then_inc(v_psum, 1)

            def shrink(b):
                pe.wait_ge(m_ready, b + 2)
                pe.wait_ge(x_done, b + 1)
                for t in range(TPB):
                    for c in range(2):
                        last = pe.matmul(ob[:, t * D:(t + 1) * D], mm[:, c, t * P:(t + 1) * P], wsh[:, c, :], start=c == 0, stop=c == 1)
                last.then_inc(o_psum, 1)

            pe.wait_ge(w_in, 48)
            turn(0)
            gates(0, first=True)
            values(0)
            turn(1)
            with pe.Fori(0, NBLK - 2) as b:
                gates(b + 1)
                shrink(b)
                values(b + 1)
                turn(b + 2)
            gates(NBLK - 1)
            shrink(NBLK - 2)
            values(NBLK - 1)
            shrink(NBLK - 1)
    st.close()


def recurrence_layer(nc, G, a):
    w = {k: a["L1_attn_b_" + k] for k in ("gamma1", "W_in", "conv_w", "conv_b", "W_gates", "b_gates", "forget_base", "W_out", "gamma2", "W_grow", "W_shrink")}
    with nc.sbuf_tensor("GT", [HC, 2, NSEQ * SEQ], F32) as GT, nc.sbuf_tensor("VT", [HC, 2, NSEQ, CONV - 1 + SEQ], F32) as VT:
        H = G | {"GT": GT, "VT": VT}
        recurrence_in_stage(nc, "RI", H, w)
        recurrence_stage(nc, "RR", H, w)
    gated_mlp_stage(nc, "RM", G, w)


def network(nc, a, out):
    with ExitStack() as ctx:
        G = make_globals(nc, ctx)
        init_globals(nc, G, a["L0_attn_a_X"].rearrange("b s d -> (b s) d"))
        attention_stage(nc, "A1", "diff", G, attn_args("diff", a))
        with ExitStack() as weights:
            weight_memory(nc, weights, G, "L0", 1024)
            load_gelu_experts(nc, "W0", G, a)
            expert_stage(nc, "F1", "gelu", G, gelu_args(a))
            attention_stage(nc, "A2", "causal", G, attn_args("causal", a))
            expert_stage(nc, "F2", "gelu", G, gelu_args(a))
        weight_memory(nc, ctx, G, "L1", 768)
        single_head_stage(nc, "A3", G, {k: a["L1_attn_a_" + k] for k in ("Wq", "bq", "Wk", "bk", "Wv", "bv")}, swiglu_expert_parts(a))
        attention_stage(nc, "A4", "full", G, attn_args("full", a))
        expert_stage(nc, "F3", "swiglu", G, swiglu_args(a))
        recurrence_layer(nc, G, a)
        attention_stage(nc, "A5", "full", G, attn_args("full", a))
        expert_stage(nc, "F4", "swiglu", G, swiglu_args(a))
        store(nc, G, out.rearrange("b s d -> (b s) d"))


_TURNED = ("L0_attn_b_Wq", "L0_attn_b_Wk", "L0_attn_b_Wv", "L0_attn_b_Wo", "L1_attn_a_Wq", "L1_attn_a_Wk", "L1_attn_a_Wv",
           "L1_attn_b_W_in", "L1_attn_b_W_gates", "L1_attn_b_W_out", "L1_attn_b_W_grow", "L1_attn_b_W_shrink")


def kernel(**inputs):
    import numpy as _np
    import concourse.bacc as _bacc
    from concourse import mybir as _mybir
    from concourse.bass_utils import run_bass_kernel_spmd as _run

    nc = _bacc.Bacc("TRN2", target_bir_lowering=False, num_devices=1)
    arrays, args = {}, {}
    for name, a in inputs.items():
        a = _np.asarray(a)
        a = _np.ascontiguousarray(a.T if name in _TURNED else a)
        arrays[f"in_{name}"] = a
        args[name] = nc.dram_tensor(f"in_{name}", a.shape, _mybir.dt.from_np(a.dtype), kind="ExternalInput").ap()
    out = nc.dram_tensor("out", (NSEQ, SEQ, D), F32, kind="ExternalOutput").ap()
    network(nc, args, out)
    r = _run(nc, [arrays], core_ids=[0])
    return r.results[0]["out"]
```
